# Optimizing a Trainium2 kernel written in Bass

```python
import numpy as np
import jax
import jax.numpy as jnp

def _softmax(x, axis=-1):
    return jax.nn.softmax(x, axis=axis)

def _gelu(x):
    return jax.nn.gelu(x, approximate=True)

def _silu(x):
    return jax.nn.silu(x)

def _sigmoid(x):
    return jax.nn.sigmoid(x)

def _layernorm(x, axis=-1, eps=1e-05):
    m = jnp.mean(x, axis=axis, keepdims=True)
    v = jnp.var(x, axis=axis, keepdims=True)
    return (x - m) / jnp.sqrt(v + eps)

def _scatter_add(tgt, idx, src, axis=0):
    return tgt.at[idx].add(src)

def _segment_sum(src, seg, n):
    return jax.ops.segment_sum(src, seg, n)
kernel_name = 'mk_gnn_preln_d2_gnn_r64_c96231'

def setup_inputs(seed: int=0):
    np.random.seed(seed)
    _w = jnp.asarray

    def _rec_inputs():
        import jax
        import jax.numpy as jnp
        _gk = jax.random.key(seed)
        x = -0.0003713 + 1 * jax.random.normal(jax.random.fold_in(_gk, 1), (3125, 64), jnp.float32)
        _s = jax.random.randint(jax.random.fold_in(_gk, 2), (25000,), 0, 3125, jnp.int32)
        _d = jax.random.randint(jax.random.fold_in(_gk, 3), (25000,), 0, 3125, jnp.int32)
        _loop = jnp.arange(3125, dtype=jnp.int32)
        src = jnp.concatenate([_s, _d, _loop])
        dst = jnp.concatenate([_d, _s, _loop])
        _o = jnp.argsort(dst, stable=True)
        src = src[_o]
        dst = dst[_o]
        edge_attr_8 = 0.000196303 + 1.00016 * jax.random.normal(jax.random.fold_in(_gk, 11), (53125, 8), jnp.float32)
        return (x, src, dst, edge_attr_8)
    x, src, dst, edge_attr_8 = _rec_inputs()

    def _L0_gnn_setup():
        import jax, jax.numpy as jnp
        import numpy as np
        E = 3125
        M = 50000
        IN_DIM = 64
        EMBED = 64
        H = 8
        D = EMBED // H

        def _segment_softmax(logits, index, num_segments):
            seg_max = jax.ops.segment_max(logits, index, num_segments=num_segments)
            seg_max = jnp.where(jnp.isfinite(seg_max), seg_max, 0.0)
            ex = jnp.exp(logits - seg_max[index])
            seg_sum = jax.ops.segment_sum(ex, index, num_segments=num_segments)
            return ex / (seg_sum[index] + 1e-16)
        key = jax.random.key(seed)
        ks = jax.random.split(key, 12)
        s = 1.0 / np.sqrt(IN_DIM)
        inp = {'edge_features': jax.random.normal(ks[0], (E, IN_DIM), dtype=jnp.float32), 'e2e': jax.random.randint(ks[1], (2, M), 0, E, dtype=jnp.int32), 'attn_bias': jax.random.normal(ks[2], (M, H), dtype=jnp.float32), 'Wq': jax.random.uniform(ks[3], (IN_DIM, EMBED), jnp.float32, -s, s), 'bq': jax.random.uniform(ks[4], (EMBED,), jnp.float32, -s, s), 'Wk': jax.random.uniform(ks[5], (IN_DIM, EMBED), jnp.float32, -s, s), 'bk': jax.random.uniform(ks[6], (EMBED,), jnp.float32, -s, s), 'Wv': jax.random.uniform(ks[7], (IN_DIM, EMBED), jnp.float32, -s, s), 'bv': jax.random.uniform(ks[8], (EMBED,), jnp.float32, -s, s), 'Wo': jax.random.uniform(ks[9], (EMBED, EMBED), jnp.float32, -s, s), 'bo': jax.random.uniform(ks[10], (EMBED,), jnp.float32, -s, s)}
        return inp
    _L0_gnn_all = _L0_gnn_setup()
    _L0_gnn_in = {k: v for k, v in _L0_gnn_all.items() if k in ('Wq', 'bq', 'Wk', 'bk', 'Wv', 'bv', 'Wo', 'bo')}
    del _L0_gnn_all

    def _L1_gnn_setup():
        import jax, jax.numpy as jnp
        import numpy as np
        N_NODES = 25000
        N_EDGES = 6250
        D_IN = 64
        D_MODEL = 128
        D_OUT = 64
        N_HEADS = 4
        N_LAYERS = 2

        def _layer_norm(x, scale, bias, eps=1e-06):
            mu = jnp.mean(x, axis=-1, keepdims=True)
            var = jnp.var(x, axis=-1, keepdims=True)
            return (x - mu) * jax.lax.rsqrt(var + eps) * scale + bias

        def _gt_layer(embeds, edge_index, qT, kT, vT, ln_scale, ln_bias):
            rows, cols = (edge_index[0], edge_index[1])
            nvar = embeds.shape[0]
            hd = D_MODEL // N_HEADS
            row_e = embeds[rows]
            col_e = embeds[cols]
            q = (row_e @ qT).reshape(-1, N_HEADS, hd)
            k = (col_e @ kT).reshape(-1, N_HEADS, hd)
            v = (col_e @ vT).reshape(-1, N_HEADS, hd)
            att = jnp.clip(jnp.einsum('ehd,ehd->eh', q, k), -10.0, 10.0)
            exp_att = jnp.exp(att)
            att_norm = jax.ops.segment_sum(exp_att, rows, num_segments=nvar)[rows]
            att = exp_att / (att_norm + 1e-08)
            res = (att[..., None] * v).reshape(-1, D_MODEL)
            agg = jax.ops.segment_sum(res, rows, num_segments=nvar)
            out = agg + embeds
            return _layer_norm(out, ln_scale, ln_bias)
        key = jax.random.key(seed)
        ks = jax.random.split(key, 12)
        glorot = jax.nn.initializers.glorot_uniform()
        inp = {'graph_node': jax.random.normal(ks[0], (N_NODES, D_IN), dtype=jnp.float32), 'edge_index': jax.random.randint(ks[1], (2, N_EDGES), 0, N_NODES, dtype=jnp.int64) if jax.config.jax_enable_x64 else jax.random.randint(ks[1], (2, N_EDGES), 0, N_NODES, dtype=jnp.int32), 'W_P_w': glorot(ks[2], (D_IN, D_MODEL), jnp.float32), 'W_P_b': jnp.zeros((D_MODEL,), jnp.float32), 'W_pos': jax.random.uniform(ks[3], (1, D_MODEL), jnp.float32, -0.02, 0.02), 'qT': glorot(ks[4], (N_LAYERS, D_MODEL, D_MODEL), jnp.float32), 'kT': glorot(ks[5], (N_LAYERS, D_MODEL, D_MODEL), jnp.float32), 'vT': glorot(ks[6], (N_LAYERS, D_MODEL, D_MODEL), jnp.float32), 'ln_scale': jnp.ones((N_LAYERS, D_MODEL), jnp.float32), 'ln_bias': jnp.zeros((N_LAYERS, D_MODEL), jnp.float32), 'inv_w': glorot(ks[7], (D_MODEL, D_OUT), jnp.float32), 'inv_b': jnp.zeros((D_OUT,), jnp.float32)}
        return inp
    _L1_gnn_all = _L1_gnn_setup()
    _L1_gnn_in = {k: v for k, v in _L1_gnn_all.items() if k in ('W_P_w', 'W_P_b', 'W_pos', 'qT', 'kT', 'vT', 'ln_scale', 'ln_bias', 'inv_w', 'inv_b')}
    del _L1_gnn_all
    return {'x': x, 'src': src, 'dst': dst, 'edge_attr_8': edge_attr_8, 'L0_gnn_Wq': _L0_gnn_in['Wq'], 'L0_gnn_bq': _L0_gnn_in['bq'], 'L0_gnn_Wk': _L0_gnn_in['Wk'], 'L0_gnn_bk': _L0_gnn_in['bk'], 'L0_gnn_Wv': _L0_gnn_in['Wv'], 'L0_gnn_bv': _L0_gnn_in['bv'], 'L0_gnn_Wo': _L0_gnn_in['Wo'], 'L0_gnn_bo': _L0_gnn_in['bo'], 'L1_gnn_W_P_w': _L1_gnn_in['W_P_w'], 'L1_gnn_W_P_b': _L1_gnn_in['W_P_b'], 'L1_gnn_W_pos': _L1_gnn_in['W_pos'], 'L1_gnn_qT': _L1_gnn_in['qT'], 'L1_gnn_kT': _L1_gnn_in['kT'], 'L1_gnn_vT': _L1_gnn_in['vT'], 'L1_gnn_ln_scale': _L1_gnn_in['ln_scale'], 'L1_gnn_ln_bias': _L1_gnn_in['ln_bias'], 'L1_gnn_inv_w': _L1_gnn_in['inv_w'], 'L1_gnn_inv_b': _L1_gnn_in['inv_b']}

def reference(x, src, dst, edge_attr_8, L0_gnn_Wq, L0_gnn_bq, L0_gnn_Wk, L0_gnn_bk, L0_gnn_Wv, L0_gnn_bv, L0_gnn_Wo, L0_gnn_bo, L1_gnn_W_P_w, L1_gnn_W_P_b, L1_gnn_W_pos, L1_gnn_qT, L1_gnn_kT, L1_gnn_vT, L1_gnn_ln_scale, L1_gnn_ln_bias, L1_gnn_inv_w, L1_gnn_inv_b):
    import jax
    import jax.numpy as jnp

    def _L0_gnn_ref(edge_features, e2e, attn_bias, Wq, bq, Wk, bk, Wv, bv, Wo, bo):
        import jax, jax.numpy as jnp
        import numpy as np
        E = 3125
        M = 50000
        IN_DIM = 64
        EMBED = 64
        H = 8
        D = EMBED // H

        def _segment_softmax(logits, index, num_segments):
            seg_max = jax.ops.segment_max(logits, index, num_segments=num_segments)
            seg_max = jnp.where(jnp.isfinite(seg_max), seg_max, 0.0)
            ex = jnp.exp(logits - seg_max[index])
            seg_sum = jax.ops.segment_sum(ex, index, num_segments=num_segments)
            return ex / (seg_sum[index] + 1e-16)
        src_e, dst_e = (e2e[0], e2e[1])
        scale = D ** (-0.5)
        q = (edge_features @ Wq + bq).reshape(E, H, D)
        k = (edge_features @ Wk + bk).reshape(E, H, D)
        v = (edge_features @ Wv + bv).reshape(E, H, D)
        q_dst = q[dst_e]
        k_src = k[src_e]
        logits = jnp.sum(q_dst * k_src, axis=-1) * scale
        logits = logits + attn_bias
        attn = _segment_softmax(logits, dst_e, E)
        msg = v[src_e] * attn[..., None]
        out = jax.ops.segment_sum(msg, dst_e, num_segments=E)
        out = out.reshape(E, EMBED)
        return out @ Wo + bo

    def _L1_gnn_ref(graph_node, edge_index, W_P_w, W_P_b, W_pos, qT, kT, vT, ln_scale, ln_bias, inv_w, inv_b):
        import jax, jax.numpy as jnp
        import numpy as np
        N_NODES = 25000
        N_EDGES = 6250
        D_IN = 64
        D_MODEL = 128
        D_OUT = 64
        N_HEADS = 4
        N_LAYERS = 2

        def _layer_norm(x, scale, bias, eps=1e-06):
            mu = jnp.mean(x, axis=-1, keepdims=True)
            var = jnp.var(x, axis=-1, keepdims=True)
            return (x - mu) * jax.lax.rsqrt(var + eps) * scale + bias

        def _gt_layer(embeds, edge_index, qT, kT, vT, ln_scale, ln_bias):
            rows, cols = (edge_index[0], edge_index[1])
            nvar = embeds.shape[0]
            hd = D_MODEL // N_HEADS
            row_e = embeds[rows]
            col_e = embeds[cols]
            q = (row_e @ qT).reshape(-1, N_HEADS, hd)
            k = (col_e @ kT).reshape(-1, N_HEADS, hd)
            v = (col_e @ vT).reshape(-1, N_HEADS, hd)
            att = jnp.clip(jnp.einsum('ehd,ehd->eh', q, k), -10.0, 10.0)
            exp_att = jnp.exp(att)
            att_norm = jax.ops.segment_sum(exp_att, rows, num_segments=nvar)[rows]
            att = exp_att / (att_norm + 1e-08)
            res = (att[..., None] * v).reshape(-1, D_MODEL)
            agg = jax.ops.segment_sum(res, rows, num_segments=nvar)
            out = agg + embeds
            return _layer_norm(out, ln_scale, ln_bias)
        embeds = graph_node @ W_P_w + W_P_b + W_pos
        for l in range(N_LAYERS):
            embeds = _gt_layer(embeds, edge_index, qT[l], kT[l], vT[l], ln_scale[l], ln_bias[l])
        return embeds @ inv_w + inv_b
    edge_index = jnp.stack([src, dst])
    h = jnp.maximum(_layernorm(x, axis=-1), 0.0)
    x = x + _L0_gnn_ref(h, edge_index, edge_attr_8, L0_gnn_Wq, L0_gnn_bq, L0_gnn_Wk, L0_gnn_bk, L0_gnn_Wv, L0_gnn_bv, L0_gnn_Wo, L0_gnn_bo)
    h = jnp.maximum(_layernorm(x, axis=-1), 0.0)
    x = x + _L1_gnn_ref(h, edge_index, L1_gnn_W_P_w, L1_gnn_W_P_b, L1_gnn_W_pos, L1_gnn_qT, L1_gnn_kT, L1_gnn_vT, L1_gnn_ln_scale, L1_gnn_ln_bias, L1_gnn_inv_w, L1_gnn_inv_b)
    return x

_drawn_inputs = setup_inputs


def setup_inputs(seed=0):
    import zlib

    import numpy as np

    out = dict(_drawn_inputs(seed))
    spreads = {'L1_gnn_W_P_b': (0.0, 0.1),
     'L1_gnn_ln_scale': (1.0, 0.2),
     'L1_gnn_ln_bias': (0.0, 0.1),
     'L1_gnn_inv_b': (0.0, 0.1)}
    factors = {'L0_gnn_Wq': 6.327,
     'L0_gnn_bq': 8.0,
     'L0_gnn_Wk': 5.882,
     'L0_gnn_bk': 8.0,
     'L1_gnn_W_pos': 3.035}
    for name, (base, spread) in spreads.items():
        noise = np.random.default_rng([zlib.crc32(name.encode()), seed]).standard_normal(out[name].shape)
        drawn = base * np.exp(spread * noise) if base else spread * noise
        out[name] = jnp.asarray(drawn.astype(out[name].dtype))
    for name, factor in factors.items():
        out[name] = (out[name] * factor).astype(out[name].dtype)
    return out
```

```python
from contextlib import ExitStack

import concourse.bass as bass
from concourse import mybir

P = 128
N = 3125
E = 53125
D0, H0 = 64, 8
DM, H1 = 128, 4
LAYERS = 2
EP, ET = 125, 425
EG = 5
NEG = ET // EG
NB = -(-N // P)
NPAD = NB * P
NWIN = NPAD + P
TG = 4
SLOTS = 4
T = 448
NG = T // TG
TI = T // (TG * SLOTS)
HI = 32
WP = [2 + H0, 2]
NONE = -3.0e38
FLOOR = -1.0e30
BIG = 1.0e38
CHUNKS = [(c, min(512, NWIN - c)) for c in range(0, NWIN, 512)]
assert EP * ET == E and T * P >= N + E and T % (TG * SLOTS) == 0 and NEG % 2 == 1


def build(nc, x, src, dst, edge_attr, wq, bq, wk, bk, wv, bv, wo, bo, wp, wpb, wpos, qT, kT, vT,
          ln_scale, ln_bias, inv_w, inv_b, out):
    f32, i32, f16 = mybir.dt.float32, mybir.dt.int32, mybir.dt.float16
    ALU = mybir.AluOpType
    ACT = mybir.ActivationFunctionType
    AX = mybir.AxisListType
    ds = bass.ds

    ctx = ExitStack()
    with ctx:
        def sb(name, shape, dt=f32):
            return ctx.enter_context(nc.sbuf_tensor(name, shape, dt))

        def dram(name, shape, dt=f32):
            return nc.dram_tensor(name, shape, dt, kind="Internal").ap()

        def sem(name):
            return ctx.enter_context(nc.semaphore(name))

        sorted_d = [dram(f"sorted{k}_d", [P * T, WP[k]]) for k in range(2)]
        npos_d = [dram(f"npos{k}_d", [HI * P]) for k in range(2)]
        base_d = [dram(f"base{k}_d", [T]) for k in range(2)]
        basei_d = [dram(f"basei{k}_d", [T], i32) for k in range(2)]
        kv0_d = dram("kv0_d", [NPAD, 2 * D0])
        q0_d = dram("q0_d", [NWIN, D0])
        kv1_d = [dram(f"kv1_{l}_d", [NPAD, 2 * DM]) for l in range(LAYERS)]
        q1_d = [dram(f"q1_{l}_d", [NWIN, DM]) for l in range(LAYERS)]
        edge_d = [dram(f"edge{n}_d", [T * H0]) for n in range(3)]
        carry_d = [dram(f"carry{n}_d", [T * H0]) for n in range(2)]

        ident = sb("ident", [P, P])
        ident16 = sb("ident16", [P, P], f16)
        diff = sb("diff", [P, P])
        below = sb("below", [P, P])
        above = sb("above", [P, P])
        iota = sb("iota", [P, P])
        iota16 = sb("iota16", [P, P], f16)
        ones = sb("ones", [P, P])
        ones16 = sb("ones16", [P, P], f16)
        thr = sb("thr", [T // 4, 4])
        arena = sb("arena", [P, T * D0])

        def part(start, *shape):
            size = 1
            for n in shape:
                size *= n
            ap = arena[:, start:start + size]
            if len(shape) == 2:
                ap = ap.rearrange("p (a b) -> p a b", a=shape[0])
            return ap

        sort_at = [ET * H0 + T * WP[0] + 2 * N + 2 * T * WP[1] + 9 * ET + 2 * T]

        def sort_part(rows, *shape, dt=f32):
            size = 1
            for n in shape:
                size *= n
            words = size if dt in (f32, i32) else -(-size // 2)
            ap = arena[0:rows, sort_at[0]:sort_at[0] + words]
            sort_at[0] += words + words % 2
            if dt is not f32:
                ap = ap.bitcast(dt)[:, 0:size]
            if len(shape) == 2:
                ap = ap.rearrange("p (a b) -> p a b", a=shape[0])
            if len(shape) == 3:
                ap = ap.rearrange("p (a b c) -> p a b c", a=shape[0], b=shape[1])
            return ap

        attr = arena[0:EP, 0:ET * H0].rearrange("p (t h) -> p t h", h=H0)
        empty = part(ET * H0, T, WP[0])
        npos_bc = part(ET * H0 + T * WP[0], N)
        o = ET * H0 + T * WP[0] + 2 * N + T * WP[1]
        ends_i = part(o, 2, ET).bitcast(i32)[0:EP]
        ends = part(o + 2 * ET, 2, ET)[0:EP]
        digit_i = part(o + 4 * ET, ET).bitcast(i32)[0:EP]
        key1 = part(o + 5 * ET, ET)[0:EP]
        keyc = part(o + 6 * ET, ET)[0:EP]
        khi = part(o + 7 * ET, ET).bitcast(f16)[0:EP, 0:ET]
        klo = part(o + 8 * ET, ET).bitcast(f16)[0:EP, 0:ET]
        base_bc = [part(o + 9 * ET + k * T, T) for k in range(2)]
        npos_le = part(ET * H0 + T * WP[0] + N, N)
        empty2 = part(ET * H0 + T * WP[0] + 2 * N, T, WP[1])
        A16 = sort_part(EP, 2, EG, HI, dt=f16)
        B16 = sort_part(EP, 2, EG, P, dt=f16)
        AT = sort_part(HI, 2, EG, EP)
        diag = sort_part(EP, EG, EP, dt=f16)
        zeros16 = sort_part(EP, P, dt=f16)
        nodes = sort_part(HI, P)
        Hs = sort_part(HI, 2, P)
        scr = sort_part(P, 2, 2, P)
        rank = sort_part(EP, 2, EG)
        first = sort_part(EP, 2, EG)
        place = sort_part(EP, 2, EG, dt=i32)
        phi = sort_part(EP, 2, EG, dt=i32)
        plo = sort_part(EP, 2, EG, dt=i32)
        row = sort_part(EP, 2, EG, dt=i32)
        pay = sort_part(EP, 2, EG, WP[0])
        nullm = sort_part(HI, P)
        cnt = sort_part(HI, P)
        incl = sort_part(HI, P)
        npos = sort_part(HI, P)
        seed = sort_part(HI, P)
        offs = sort_part(HI, 1)
        basec = sort_part(T // 4, 4)
        basei = sort_part(T // 4, 4, dt=i32)
        base_i = [sb(f"base_i{k}", [1, T], i32) for k in range(2)]
        S = [sb("S0", [P, T, WP[0]]), part(o + 9 * ET + 2 * T, T, WP[1])]
        seg = [sb(f"seg{k}", [P, T]) for k in range(2)]
        idx = [sb(f"idx{k}", [P, T], i32) for k in range(2)]

        banks = [ctx.enter_context(nc.psum_tensor(f"bank{n}", [P, 512], f32)) for n in range(8)]

        s_const = sem("s_const")
        s_mask = sem("s_mask")
        s_ends = sem("s_ends")
        s_attr = sem("s_attr")
        s_v = sem("s_v")
        s_key = sem("s_key")
        s_oh = sem("s_oh")
        s_ohu = sem("s_ohu")
        s_scan = sem("s_scan")
        s_offs = sem("s_offs")
        s_npos = sem("s_npos")
        s_nposd = sem("s_nposd")
        s_nposb = sem("s_nposb")
        s_seed = sem("s_seed")
        s_base = sem("s_base")
        s_based = sem("s_based")
        s_basel = sem("s_basel")
        s_at = sem("s_at")
        s_ats = sem("s_ats")
        s_diag = sem("s_diag")
        s_bc = sem("s_bc")
        s_rank = sem("s_rank")
        s_look = sem("s_look")
        s_first = sem("s_first")
        s_h = sem("s_h")
        s_hs = sem("s_hs")
        s_pl = sem("s_pl")
        s_dig = sem("s_dig")
        s_row = sem("s_row")
        s_pay = sem("s_pay")
        s_sc = [sem(f"s_sc{n}") for n in range(2)]
        s_pat = sem("s_pat")
        s_fill = sem("s_fill")
        s_S = sem("s_S")
        s_seg = sem("s_seg")
        s_turn = sem("s_turn")

        vcount = [0]

        def vstep(ins):
            vcount[0] += 1
            ins.then_inc(s_v, 1)
            nc.vector.wait_ge(s_v, vcount[0])

        def since(eng, semaphore, value):
            if not isinstance(value, int) or value > 0:
                eng.wait_ge(semaphore, value)

        def in_pairs(eng, body):
            for b in range(2):
                body(b, 0, b, False)
            with eng.Fori(1, NEG // 2) as i:
                for b in range(2):
                    body(i * 2 + b, i, b, False)
            body(NEG - 1, NEG // 2, 0, True)

        iota_g = iota16[:, :].unsqueeze(1).to_broadcast([P, EG, P])

        H = banks[0][0:HI, 0:P]
        OFFS = banks[1][0:HI, 0:1]
        ATP = banks[6][:, :].bitcast(f16)[0:HI, 0:EG * P].rearrange("p (j e) -> p j e", j=EG)

        def sort_sync(sp, k):
            if k == 0:
                sp.wait_ge(s_pat, 1)
                for n in range(2):
                    sp.dma_start(sorted_d[n].rearrange("(p t) w -> p t w", p=P),
                                 (empty, empty2)[n]).then_inc(s_fill, 16)
            sp.wait_ge(s_npos, k + 1)
            sp.dma_start(npos_d[k].rearrange("(h l) -> h l", h=HI), npos[:, :]).then_inc(s_nposd, 16)
            sp.wait_ge(s_nposd, 16 * (k + 1))
            if k:
                sp.wait_ge(s_base, k)
            sp.dma_start(npos_bc[0:T // 4, :],
                         npos_d[k][0:N].partition_broadcast(T // 4)).then_inc(s_nposb, 16)
            sp.wait_ge(s_base, k + 1)
            sp.dma_start(base_d[k].rearrange("(p g) -> p g", g=4), basec[:, :]).then_inc(s_based, 16)
            sp.dma_start(basei_d[k].rearrange("(p g) -> p g", g=4), basei[:, :]).then_inc(s_based, 16)
            sp.wait_ge(s_based, 32 * (k + 1))
            sp.dma_start(base_bc[k][:, :], base_d[k].partition_broadcast(P)).then_inc(s_basel, 16)
            sp.dma_start(base_i[k][:, :], basei_d[k].rearrange("(a n) -> a n", a=1)).then_inc(s_basel, 16)
            sp.wait_ge(s_sc[0], 16 * EG * (NEG // 2 + 1) * (k + 1))
            sp.wait_ge(s_sc[1], 16 * EG * (NEG // 2) * (k + 1))
            sp.dma_start(S[k][:, :, :],
                         sorted_d[k].rearrange("(p t) w -> p t w", p=P)).then_inc(s_S, 16)

        def onehots(g, b):
            cols = ds(g * EG, EG)
            nc.vector.tensor_tensor(A16[:, b, :, :], iota_g[0:EP, :, 0:HI],
                                    khi[:, cols].unsqueeze(2).to_broadcast([EP, EG, HI]), ALU.is_equal)
            nc.vector.tensor_tensor(B16[:, b, :, :], iota_g[0:EP, :, :],
                                    klo[:, cols].unsqueeze(2).to_broadcast([EP, EG, P]),
                                    ALU.is_equal).then_inc(s_oh, 1)

        def sort_vector(dve, k):
            key = 1 - k
            vstep(nc.vector.tensor_scalar(digit_i[:, :], ends_i[:, key, :], 7, None,
                                          ALU.logical_shift_right))
            vstep(nc.vector.tensor_copy(khi[:, :], digit_i[:, :]))
            vstep(nc.vector.tensor_scalar(digit_i[:, :], ends_i[:, key, :], P - 1, None, ALU.bitwise_and))
            vstep(nc.vector.tensor_copy(klo[:, :], digit_i[:, :]))
            if k:
                dve.wait_ge(s_pay, k * NEG)
            vstep(nc.vector.tensor_scalar(key1[:, :], ends[:, key, :], 1.0, None, ALU.add))
            nc.vector.tensor_scalar(keyc[:, :], ends[:, key, :], -2048.0, None, ALU.add).then_inc(s_key, 1)
            if k:
                dve.wait_ge(s_h, k * (ET + 1))

            def pass1(g, i, b, last):
                since(dve, s_ohu, g + (k * NEG - 1))
                onehots(g, b)

            in_pairs(dve, pass1)
            dve.wait_ge(s_ohu, (k + 1) * NEG)
            vstep(nc.vector.tensor_tensor(cnt[:, :], H, nullm[:, :], ALU.add))
            nc.vector.tensor_tensor_scan(incl[:, :], ones[0:HI, :], cnt[:, :], 0.0, ALU.mult,
                                         ALU.add).then_inc(s_scan, 1)
            dve.wait_ge(s_scan, k + 1)
            dve.wait_ge(s_offs, k + 1)
            vstep(nc.vector.tensor_copy(offs[:, :], OFFS))
            if k:
                dve.wait_ge(s_nposd, 16 * k)
            nc.vector.scalar_tensor_tensor(npos[:, :], incl[:, :], offs[:, 0:1], cnt[:, :], ALU.add,
                                           ALU.subtract).then_inc(s_npos, 1)
            dve.wait_ge(s_npos, k + 1)
            nc.vector.tensor_scalar(seed[:, :], npos[:, :], 1.0, None, ALU.add).then_inc(s_seed, 1)
            dve.wait_ge(s_nposb, 16 * (k + 1))
            if k:
                dve.wait_ge(s_based, 32 * k)
            for g in range(4):
                vstep(nc.vector.tensor_scalar(npos_le[0:T // 4, :], npos_bc[0:T // 4, :], thr[:, g:g + 1],
                                              0.0, ALU.is_le, ALU.add, accum_out=basec[:, g:g + 1]))
            vstep(nc.vector.tensor_scalar(basec[:, :], basec[:, :], -1.0, None, ALU.add))
            nc.vector.tensor_copy(basei[:, :], basec[:, :]).then_inc(s_base, 1)

            def tiles(g, i, b, last):
                if not last:
                    dve.wait_ge(s_h, g * EG + (k * (ET + 1) + 1))
                    onehots(g + 1, 1 - b)
                for j in range(EG):
                    c = g * EG + j
                    since(dve, s_first, c + (k * ET - 1))
                    dve.wait_ge(s_bc, c + (k * ET + 1))
                    nc.vector.scalar_tensor_tensor(
                        scr[0:EP, (b + j) % 2, 0, 0:EP], banks[2 + (b + j) % 2][0:EP, 0:EP], keyc[:, ds(c, 1)], below[0:EP, 0:EP],
                        ALU.is_equal, ALU.mult, accum_out=rank[:, b, j:j + 1]).then_inc(s_rank, 1)
                    dve.wait_ge(s_look, c + (k * ET + 1))
                    nc.vector.scalar_tensor_tensor(
                        scr[0:EP, (b + j) % 2, 1, :], banks[4 + (b + j) % 2][0:EP, 0:P], 1.0, B16[:, b, j, :],
                        ALU.mult, ALU.mult, accum_out=first[:, b, j:j + 1]).then_inc(s_first, 1)
                n = g + (k * NEG + 1)
                dve.wait_ge(s_first, g * EG + (k * ET + EG))
                nc.vector.tensor_tensor(place[:, b, :], rank[:, b, :], first[:, b, :],
                                        ALU.add).then_inc(s_pl, 1)
                dve.wait_ge(s_pl, n)
                nc.vector.tensor_scalar(phi[:, b, :], place[:, b, :], 7, None, ALU.logical_shift_right)
                nc.vector.tensor_scalar(plo[:, b, :], place[:, b, :], P - 1, None,
                                        ALU.bitwise_and).then_inc(s_dig, 1)
                dve.wait_ge(s_dig, n)
                since(dve, s_sc[b], i * (16 * EG) + k * 16 * EG * (NEG // 2 + 1 - b))
                nc.vector.scalar_tensor_tensor(row[:, b, :], plo[:, b, :], float(T), phi[:, b, :],
                                               ALU.mult, ALU.add).then_inc(s_row, 1)

            onehots(0, 0)
            in_pairs(dve, tiles)
            dve.wait_ge(s_S, 16 * (k + 1))
            dve.wait_ge(s_basel, 32 * (k + 1))
            nc.vector.scalar_tensor_tensor(seg[k][:, 0:T], S[k][:, :, 0:1].rearrange("p t w -> p (t w)"),
                                           -1.0, base_bc[k][:, :], ALU.add, ALU.subtract)
            nc.vector.tensor_copy(idx[k][:, :], S[k][:, :, 1:2].rearrange("p t w -> p (t w)")
                                  ).then_inc(s_seg, 1)

        def sort_tensor(pe, k):
            if k == 0:
                pe.wait_ge(s_mask, 1)
            else:
                pe.wait_ge(s_hs, k * (ET + 1))
            nc.tensor.matmul(H, zeros16[:, 0:HI], zeros16[:, :], start=True, stop=True,
                             skip_group_check=True)

            def hist(g, i, b, last):
                pe.wait_ge(s_oh, g + (2 * k * NEG + 1))
                for j in range(EG):
                    done = nc.tensor.matmul(H, A16[:, b, j, :], B16[:, b, j, :], start=False, stop=True,
                                            skip_group_check=True)
                done.then_inc(s_ohu, 1)

            in_pairs(pe, hist)
            pe.wait_ge(s_scan, k + 1)
            nc.tensor.matmul(OFFS, above[0:HI, 0:HI], incl[:, P - 1:P], start=True,
                             stop=True).then_inc(s_offs, 1)
            pe.wait_ge(s_seed, k + 1)
            nc.tensor.matmul(H, ident[0:HI, 0:HI], seed[:, :], start=True, stop=True,
                             skip_group_check=True).then_inc(s_h, 1)

            def transposes(g, b):
                pe.wait_ge(s_oh, g + ((2 * k + 1) * NEG + 1))
                since(pe, s_ats, g + k * NEG)
                for j in range(EG):
                    done = nc.tensor.transpose(ATP[:, j, 0:EP], A16[:, b, j, :], ident16[0:EP, 0:EP])
                done.then_inc(s_at, 1)

            def tiles(g, i, b, last):
                if not last:
                    transposes(g + 1, 1 - b)
                pe.wait_ge(s_ats, g + (k * NEG + 1))
                for j in range(EG):
                    n = g * EG + (k * ET + j)
                    pe.wait_ge(s_diag, n + 1)
                    since(pe, s_rank, n - 1)
                    nc.tensor.matmul(banks[2 + (b + j) % 2][0:EP, 0:EP], ones16[0:EP, 0:EP], diag[:, j, :],
                                     start=True, stop=True).then_inc(s_bc, 1)
                    pe.wait_ge(s_hs, n + (k + 1))
                    nc.tensor.matmul(H, A16[:, b, j, :], B16[:, b, j, :], start=False, stop=True,
                                     skip_group_check=True).then_inc(s_h, 1)
                    since(pe, s_first, n - 1)
                    nc.tensor.matmul(banks[4 + (b + j) % 2][0:EP, 0:P], AT[:, b, j, :],
                                     Hs[:, (b + j) % 2, :], start=True, stop=True).then_inc(s_look, 1)

            transposes(0, 0)
            in_pairs(pe, tiles)

        def sort_scalar(act, k):
            words = WP[k]
            if k == 0:
                act.wait_ge(s_ends, 32)
                act.wait_ge(s_attr, 16)
            act.wait_ge(s_key, k + 1)

            def diagonal(g, j):
                nc.scalar.activation(diag[:, j, :], ident16[0:EP, 0:EP], ACT.Copy,
                                     scale=keyc[:, ds(g * EG + j, 1)]).then_inc(s_diag, 1)

            def transposed(g, b):
                act.wait_ge(s_at, g + (k * NEG + 1))
                nc.scalar.copy(AT[:, b, :, :], ATP[:, :, 0:EP]).then_inc(s_ats, 1)

            def table(n, slot):
                act.wait_ge(s_h, n)
                nc.scalar.copy(Hs[:, slot, :], H).then_inc(s_hs, 1)

            def tiles(g, i, b, last):
                since(act, s_sc[b], i * (16 * EG) + k * 16 * EG * (NEG // 2 + 1 - b))
                cols = ds(g * EG, EG)
                if k == 0:
                    nc.scalar.copy(pay[:, b, :, 2:words], attr[:, cols, :])
                nc.scalar.copy(pay[:, b, :, 0:1], key1[:, cols].unsqueeze(2))
                nc.scalar.copy(pay[:, b, :, 1:2], ends[:, k, cols].unsqueeze(2)).then_inc(s_pay, 1)
                if not last:
                    transposed(g + 1, 1 - b)
                for j in range(EG):
                    n = g * EG + (k * ET + j)
                    if not last:
                        act.wait_ge(s_bc, n + 1)
                        diagonal(g + 1, j)
                    table(n + (k + 2), (b + j + 1) % 2)

            for j in range(EG):
                diagonal(0, j)
            transposed(0, 0)
            table(k * (ET + 1) + 1, 0)
            in_pairs(act, tiles)

        def sort_gpsimd(gp, k):
            if k == 0:
                gp.wait_ge(s_fill, 32)

            def tiles(g, i, b, last):
                gp.wait_ge(s_row, g + (k * NEG + 1))
                gp.wait_ge(s_pay, g + (k * NEG + 1))
                gp.sem_inc(s_turn, 1)
                for j in range(EG):
                    gp.indirect_dma_start(
                        out=sorted_d[k],
                        out_offset=bass.IndirectOffsetOnAxis(ap=row[:, b, j:j + 1], axis=0),
                        in_=pay[:, b, j, 0:WP[k]], in_offset=None).then_inc(s_sc[b], 16)

            in_pairs(gp, tiles)

        s_g = sem("s_g")
        gcount = [0]

        def gstep(ins):
            gcount[0] += 1
            ins.then_inc(s_g, 1)
            nc.gpsimd.wait_ge(s_g, gcount[0])

        def constants_gpsimd(gp):
            kw = dict(allow_small_or_imprecise_dtypes=True)
            nc.gpsimd.iota(diff[:, :], [[1, P]], base=0, channel_multiplier=-1, **kw)
            nc.gpsimd.iota(iota[:, :], [[1, P]], base=0, channel_multiplier=0, **kw)
            nc.gpsimd.iota(iota16[:, :], [[1, P]], base=0, channel_multiplier=0, **kw)
            nc.gpsimd.iota(nodes[:, :], [[1, P]], base=0, channel_multiplier=P, **kw)
            nc.gpsimd.iota(thr[:, :], [[P, 4]], base=0, channel_multiplier=4 * P, **kw).then_inc(s_const, 1)
            nc.gpsimd.memset(empty2[:, :, :], 0.0)
            gstep(nc.gpsimd.memset(empty[:, :, :], NONE))
            nc.gpsimd.memset(empty[:, :, 0:2], 0.0).then_inc(s_pat, 1)

        def constants_vector(dve):
            nc.vector.memset(ones[:, :], 1.0)
            nc.vector.memset(ones16[:, :], 1.0)
            nc.vector.memset(zeros16[:, :], 0.0)
            dve.wait_ge(s_const, 1)
            nc.vector.tensor_scalar(ident[:, :], diff[:, :], 0.0, None, ALU.is_equal)
            nc.vector.tensor_scalar(ident16[:, :], diff[:, :], 0.0, None, ALU.is_equal)
            nc.vector.tensor_scalar(below[:, :], diff[:, :], 0.0, None, ALU.is_lt)
            nc.vector.tensor_scalar(nullm[:, :], nodes[:, :], float(N), None, ALU.is_lt)
            nc.vector.tensor_scalar(above[:, :], diff[:, :], 0.0, None, ALU.is_gt).then_inc(s_mask, 1)
            dve.wait_ge(s_mask, 1)
            dve.wait_ge(s_ends, 32)
            vstep(nc.vector.tensor_copy(ends[:, :, :], ends_i[:, :, :]))

        def loads_sync(sp):
            sp.dma_start(ends_i[:, 0, :], src.rearrange("(p t) -> p t", p=EP)).then_inc(s_ends, 16)
            sp.dma_start(ends_i[:, 1, :], dst.rearrange("(p t) -> p t", p=EP)).then_inc(s_ends, 16)
            sp.dma_start(attr, edge_attr.rearrange("(p t) h -> p t h", p=EP)).then_inc(s_attr, 16)

        stage0 = part(0, NB + 1, 3 * D0)
        values = part(0, T, D0)
        stage1 = part(0, NB + 1, 3 * DM)
        acc1 = part((NB + 1) * 3 * DM, 2, NWIN)
        o = (NB + 1) * 3 * DM + 2 * NWIN
        emb = part(o, NWIN)
        cent = part(o + NWIN, NWIN)
        work1 = part(o + 2 * NWIN, NWIN)
        hT = cent[0:D0 + 1, :]
        den0 = work1[0:D0, :]
        hs = part(o - NWIN, NB, D0)
        sq = part(o - 2 * NWIN, NB, D0)

        xs = sb("xs", [P, NB, D0])
        mean = sb("mean", [P, NB])
        var = sb("var", [P, NB])
        W0 = sb("W0", [D0 + 1, 3 * D0])
        Wo = sb("Wo", [D0 + 1, D0])
        Wp = sb("Wp", [D0, DM])
        shift = sb("shift", [P, 2])
        W1 = sb("W1", [P, LAYERS, 3, DM])
        lns = sb("lns", [P, LAYERS])
        lnb = sb("lnb", [P, LAYERS])
        invw = sb("invw", [P, D0])
        invb = sb("invb", [P, D0])
        avg = sb("avg", [P, P])
        eps = sb("eps", [P, 1])
        idxs = sb("idxs", [P, SLOTS, TG], i32)
        kv = sb("kv", [P, SLOTS, TG, 2 * DM])
        acc0 = kv[:, :, :, :].rearrange("p a b c -> p (a b c)")[:, 0:NWIN]
        scratch = sb("scratch", [P, SLOTS * TG * DM + 2 * TG * P])
        qw = scratch[:, 0:SLOTS * TG * DM].rearrange("p (s j c) -> p s j c", s=SLOTS, j=TG)
        RT = scratch[:, SLOTS * TG * DM:].rearrange("p (s c) -> p s c", s=2)
        chain = scratch[0:H0, 0:5 * T].rearrange("p (n t) -> p n t", n=5)
        R = sb("R", [P, SLOTS, TG, P])
        prod = sb("prod", [P, 2, TG, DM])
        red = sb("red", [P, 2, TG * H0])
        wts = sb("wts", [P, 2, TG * H1])
        vw = sb("vw", [P, 2, TG, DM])
        wx = sb("wx", [P, 2, TG, DM])
        LT = kv[:, :, :, :].rearrange("p a b c -> p (a b c)")[:, 0:T * H0]
        EB = T * H0 // P
        EH = EB // 4
        fwd = prod[:, :, :, :].rearrange("p a b c -> p (a b c)")[:, 0:EH * P]
        bwd = vw[:, :, :, :].rearrange("p a b c -> p (a b c)")[:, 0:EH * P]
        gate = R[:, :, :, :].rearrange("p a b c -> p (a b c)")[:, 0:EH * P]
        gate2 = R[:, :, :, :].rearrange("p a b c -> p (a b c)")[:, EH * P:2 * EH * P]
        ends_f = sb("ends_f", [P, 3, EB])
        carries = sb("carries", [P, 2, EB])

        s_x = sem("s_x")
        s_w = sem("s_w")
        s_zero = sem("s_zero")
        s_var = sem("s_var")
        s_std = sem("s_std")
        s_hn = sem("s_hn")
        s_tp = sem("s_tp")
        s_ts = sem("s_ts")
        s_pj = sem("s_pj")
        s_pjs = sem("s_pjs")
        s_tab = sem("s_tab")
        s_ix = sem("s_ix")
        s_kv = [sem(f"s_kv{n}") for n in range(SLOTS)]
        s_qw = [sem(f"s_qw{n}") for n in range(SLOTS)]
        s_R = sem("s_R")
        s_rt = sem("s_rt")
        s_rts = sem("s_rts")
        s_qe = sem("s_qe")
        s_prod = sem("s_prod")
        s_red = sem("s_red")
        s_lg = sem("s_lg")
        s_vc = sem("s_vc")
        s_wt = sem("s_wt")
        s_vw = sem("s_vw")
        s_wb = sem("s_wb")
        s_sum = sem("s_sum")
        s_acc = sem("s_acc")
        s_ls = sem("s_ls")
        s_lt = sem("s_lt")
        s_lts = sem("s_lts")
        s_ed = sem("s_ed")
        s_edd = sem("s_edd")
        s_edl = sem("s_edl")
        s_ca = sem("s_ca")
        s_cad = sem("s_cad")
        s_cal = sem("s_cal")
        s_mx = sem("s_mx")
        s_mt = sem("s_mt")
        s_sh = sem("s_sh")
        s_ex = sem("s_ex")
        s_den = sem("s_den")
        s_agg = sem("s_agg")
        s_o = sem("s_o")
        s_emb = sem("s_emb")
        s_c1 = sem("s_c1")
        s_m1 = sem("s_m1")
        s_xb = sem("s_xb")
        s_c1x = sem("s_c1x")
        s_mm = sem("s_mm")
        s_sq = sem("s_sq")
        s_root = sem("s_root")
        s_nm = sem("s_nm")
        s_fin = sem("s_fin")
        s_out = sem("s_out")

        def fours(eng, stages):
            def step(i, s):
                for lag, fn in stages:
                    ii, ss = i + (s - lag) // SLOTS, (s - lag) % SLOTS
                    if isinstance(i, int) and not 0 <= ii * SLOTS + ss < NG:
                        continue
                    fn(ii, ss, ii * SLOTS + ss)
            lead = min(0, min(lag for lag, _ in stages))
            for n in range(lead, 0):
                step(n // SLOTS, n % SLOTS)
            for s in range(SLOTS):
                step(0, s)
            with eng.Fori(1, TI - 1) as i:
                for s in range(SLOTS):
                    step(i, s)
            for n in range((TI - 1) * SLOTS, NG + max(lag for lag, _ in stages)):
                step(n // SLOTS, n % SLOTS)

        def load_weights(sp):
            def w(dst_ap, src_ap):
                sp.dma_start(dst_ap, src_ap).then_inc(s_w, 16)
                wcount[0] += 16
            rowv = lambda a: a.rearrange("(o n) -> o n", o=1)
            col = lambda a: a.rearrange("(n o) -> n o", o=1)
            for n, (m, v) in enumerate(((wq, bq), (wk, bk), (wv, bv))):
                w(W0[0:D0, n * D0:(n + 1) * D0], m)
                w(W0[D0:D0 + 1, n * D0:(n + 1) * D0], rowv(v))
            w(Wo[0:D0, :], wo)
            w(Wo[D0:D0 + 1, :], rowv(bo))
            w(Wp[:, :], wp)
            w(shift[:, 0:1], col(wpb))
            w(shift[:, 1:2], wpos.rearrange("o n -> n o"))
            for l in range(LAYERS):
                for n, m in enumerate((qT, kT, vT)):
                    w(W1[:, l, n, :], m[l])
                w(lns[:, l:l + 1], col(ln_scale[l]))
                w(lnb[:, l:l + 1], col(ln_bias[l]))
            w(invw[:, :], inv_w)
            w(invb[:, :], inv_b.partition_broadcast(P))
        wcount = [0]

        def zeros_gpsimd(gp):
            nc.gpsimd.memset(xs[:, NB - 1:NB, :], 0.0).then_inc(s_zero, 1)
            nc.gpsimd.memset(avg[:, :], 1.0 / DM)
            nc.gpsimd.memset(eps[:, :], 1e-6).then_inc(s_zero, 1)

        def load_x(sp):
            sp.wait_ge(s_zero, 1)
            full = (NB - 1) * P
            sp.dma_start(xs[:, 0:NB - 1, :], x[0:full].rearrange("(b p) c -> p b c", p=P)).then_inc(s_x, 16)
            sp.dma_start(xs[0:N - full, NB - 1, :], x[full:N]).then_inc(s_x, 16)

        def hT_borders():
            nc.vector.memset(hT[0:D0, NPAD:NWIN], 0.0)
            vstep(nc.vector.memset(hT[D0:D0 + 1, :], 1.0))

        def norm_vector(dve, n):
            if n == 0:
                hT_borders()
            vstep(nc.vector.tensor_reduce(mean[:, :], xs[:, :, :], AX.X, ALU.add))
            vstep(nc.vector.tensor_scalar(mean[:, :], mean[:, :], 1.0 / D0, None, ALU.mult))
            vstep(nc.vector.tensor_tensor(hs[:, :, :], xs[:, :, :],
                                          mean[:, :].unsqueeze(2).to_broadcast([P, NB, D0]), ALU.subtract))
            vstep(nc.vector.tensor_tensor(sq[:, :, :], hs[:, :, :], hs[:, :, :], ALU.mult))
            vstep(nc.vector.tensor_reduce(var[:, :], sq[:, :, :], AX.X, ALU.add))
            nc.vector.tensor_scalar(var[:, :], var[:, :], 1.0 / D0, 1e-5, ALU.mult, ALU.add).then_inc(s_var, 1)
            dve.wait_ge(s_std, n + 1)
            vstep(nc.vector.reciprocal(var[:, :], var[:, :]))
            vstep(nc.vector.tensor_tensor(hs[:, :, :], hs[:, :, :],
                                          var[:, :].unsqueeze(2).to_broadcast([P, NB, D0]), ALU.mult))
            nc.vector.tensor_scalar(hs[:, :, :], hs[:, :, :], 0.0, None, ALU.max).then_inc(s_hn, 1)

        TR = -(-NB // 4)

        def norm_scalar(act, n):
            act.wait_ge(s_var, n + 1)
            nc.scalar.activation(var[:, :], var[:, :], ACT.Sqrt).then_inc(s_std, 1)
            for g in range(TR):
                blocks = min(4, NB - g * 4)
                act.wait_ge(s_tp, n * TR + g + 1)
                nc.scalar.copy(hT[0:D0, g * 512:g * 512 + blocks * P],
                               banks[g][0:D0, 0:blocks * P]).then_inc(s_ts, 1)

        def norm_tensor(pe, n):
            pe.wait_ge(s_hn, n + 1)
            for g in range(TR):
                for b in range(g * 4, min(g * 4 + 4, NB)):
                    done = nc.tensor.transpose(banks[g][0:D0, (b % 4) * P:(b % 4 + 1) * P], hs[:, b, :],
                                               ident[:, :])
                done.then_inc(s_tp, 1)
            pe.wait_ge(s_ts, (n + 1) * TR)

        NT = NB + 1

        def project_tensor(pe, n, lhs, rhs, cols):
            for b in range(NT):
                m = n * NT + b
                since(pe, s_pjs, m - 3)
                nc.tensor.matmul(banks[b % 4][:, 0:cols], lhs[:, b * P:(b + 1) * P], rhs, start=True,
                                 stop=True).then_inc(s_pj, 1)

        def project_scalar(act, n, stage, cols):
            for b in range(NT):
                act.wait_ge(s_pj, n * NT + b + 1)
                nc.scalar.copy(stage[:, b, :], banks[b % 4][:, 0:cols]).then_inc(s_pjs, 1)

        def tables_sync(sp, n, stage, width, q_d, kv_d):
            sp.wait_ge(s_pjs, (n + 1) * NT)
            sp.dma_start(q_d.rearrange("(b p) c -> p b c", p=P), stage[:, :, 0:width]).then_inc(s_tab, 16)
            sp.dma_start(kv_d.rearrange("(b p) c -> p b c", p=P),
                         stage[:, 0:NB, width:3 * width]).then_inc(s_tab, 16)

        def windows_sync(sp, n, k, q_d, width):
            sp.wait_ge(s_tab, 32 * (n + 1))
            if n < 2:
                sp.wait_ge(s_basel, 32 * (k + 1))

            def load(i, s, g):
                since(sp, s_qe, g + (n * NG - SLOTS + 1))
                for j in range(TG):
                    base = sp.value_load(base_i[k][0:1, ds(g * TG + j, 1)], min_val=0, max_val=N - 1)
                    sp.dma_start(qw[:, s, j, 0:width], q_d[ds(base, P), :]).then_inc(s_qw[s], 16)

            fours(sp, [(0, load)])

        def gather_gpsimd(gp, n, kv_d, width):
            gp.wait_ge(s_tab, 32 * (n + 1))

            def gather(i, s, g):
                gp.wait_ge(s_ix, g + (n * NG + 1))
                since(gp, s_prod, g + (n * NG - SLOTS + 1))
                since(gp, s_vw if n else s_vc, g + (n * NG - SLOTS + 1))
                gp.sem_inc(s_turn, 1)
                for j in range(TG):
                    gp.indirect_dma_start(
                        out=kv[:, s, j, 0:2 * width], out_offset=None, in_=kv_d,
                        in_offset=bass.IndirectOffsetOnAxis(ap=idxs[:, s, j:j + 1], axis=0)
                    ).then_inc(s_kv[s], 16)

            fours(gp, [(0, gather)])

        def rows(n, i):
            return i * (16 * TG) + (n * TI + 1) * 16 * TG

        def stage_indices(act, n, k):
            def fn(i, s, g):
                since(act, s_kv[s], rows(n, i) - 16 * TG)
                nc.scalar.copy(idxs[:, s, :], idx[k][:, ds(g * TG, TG)]).then_inc(s_ix, 1)
            return fn

        def copy_transposed(act, n):
            def fn(i, s, g):
                act.wait_ge(s_rt, g + (n * NG + 1))
                since(act, s_qe, g + (n * NG - 1))
                nc.scalar.copy(RT[:, s % 2, :], banks[s % 2][:, :]).then_inc(s_rts, 1)
            return fn

        def keep_values(act):
            def fn(i, s, g):
                act.wait_ge(s_kv[s], rows(0, i))
                nc.scalar.copy(values[:, ds(g * TG, TG), :], kv[:, s, :, 0:2 * D0][:, :, D0:2 * D0]
                               ).then_inc(s_vc, 1)
            return fn

        def one_hot(dve, n, k, ring):
            def fn(i, s, g):
                ring(i, s, g)
                nc.vector.tensor_tensor(R[:, s, :, :], iota[:, :].unsqueeze(1).to_broadcast([P, TG, P]),
                                        seg[k][:, ds(g * TG, TG)].unsqueeze(2).to_broadcast([P, TG, P]),
                                        ALU.is_equal).then_inc(s_R, 1)
            return fn

        def transposes(pe, n, nR):
            def fn(i, s, g):
                pe.wait_ge(s_R, g + (nR * NG + 1))
                since(pe, s_rts, g + (n * NG - 1))
                for j in range(TG):
                    done = nc.tensor.transpose(banks[s % 2][:, j * P:(j + 1) * P], R[:, s, j, :], ident[:, :])
                done.then_inc(s_rt, 1)
            return fn

        def expand(pe, n, width):
            def fn(i, s, g):
                pe.wait_ge(s_rts, g + (n * NG + 1))
                pe.wait_ge(s_qw[s], rows(n, i))
                since(pe, s_prod, g + (n * NG - 1))
                for j in range(TG):
                    done = nc.tensor.matmul(banks[2 + s % 2][:, j * width:(j + 1) * width],
                                            RT[:, s % 2, j * P:(j + 1) * P], qw[:, s, j, 0:width],
                                            start=True, stop=True)
                done.then_inc(s_qe, 1)
            return fn

        def logits(dve, n, width, heads):
            def fn(i, s, g):
                dve.wait_ge(s_kv[s], rows(n, i))
                dve.wait_ge(s_qe, g + (n * NG + 1))
                since(dve, s_red, g + (n * NG - 1))
                nc.vector.tensor_tensor(prod[:, s % 2, :, 0:width], kv[:, s, :, 0:width],
                                        banks[2 + s % 2][:, 0:TG * width].rearrange("p (j c) -> p j c", j=TG),
                                        ALU.mult).then_inc(s_prod, 1)
                dve.wait_ge(s_prod, g + (n * NG + 1))
                since(dve, s_lg, g + (n * NG - 1))
                nc.vector.tensor_reduce(red[:, s % 2, 0:TG * heads].rearrange("p (j h) -> p j h", j=TG),
                                        prod[:, s % 2, :, 0:width].rearrange("p j (h d) -> p j h d", h=heads),
                                        AX.X, ALU.add).then_inc(s_red, 1)
                dve.wait_ge(s_red, g + (n * NG + 1))
            return fn

        def a_vector(dve):
            dot = logits(dve, 0, D0, H0)

            def bias(i, s, g):
                dot(i, s, g)
                at = S[0][:, ds(g * TG, TG), 2:2 + H0]
                nc.vector.scalar_tensor_tensor(
                    at, red[:, s % 2, :].rearrange("p (j h) -> p j h", j=TG), (D0 // H0) ** -0.5, at,
                    ALU.mult, ALU.add).then_inc(s_lg, 1)

            def ring(i, s, g):
                since(dve, s_rt, g - SLOTS + 1)

            fours(dve, [(0, one_hot(dve, 0, 0, ring)), (1, bias)])

        def max_tensor(pe):
            pe.wait_ge(s_lg, NG)
            for g in range(EB // 4):
                pe.wait_ge(s_ls, g + 1)
                since(pe, s_lts, g - 3)
                for b in range(4):
                    done = nc.tensor.transpose(banks[4 + g % 4][:, b * P:(b + 1) * P],
                                               RT[:, g % 2, b * P:(b + 1) * P], ident[:, :])
                done.then_inc(s_lt, 1)
            pe.wait_ge(s_mx, 4)
            for g in range(EB // 4):
                since(pe, s_sh, g - 3)
                for b in range(4):
                    c = (g * 4 + b) * P
                    done = nc.tensor.transpose(banks[4 + g % 4][:, b * P:(b + 1) * P], LT[:, c:c + P],
                                               ident[:, :])
                done.then_inc(s_mt, 1)

        def max_scalar(act):
            act.wait_ge(s_lg, NG)
            act.wait_ge(s_qe, NG)
            for g in range(EB // 4):
                t = g * 4 * (P // H0)
                since(act, s_lt, g - 1)
                nc.scalar.copy(RT[:, g % 2, :].rearrange("p (t h) -> p t h", h=H0),
                               S[0][:, t:t + 4 * (P // H0), 2:2 + H0]).then_inc(s_ls, 1)
                act.wait_ge(s_lt, g + 1)
                nc.scalar.copy(LT[:, g * 512:(g + 1) * 512], banks[4 + g % 4][:, :]).then_inc(s_lts, 1)
            act.wait_ge(s_sh, EB // 4)
            at = S[0][:, :, 2:2 + H0]
            nc.scalar.activation(at, at, ACT.Exp).then_inc(s_ex, 1)

        def scans(c):
            x = LT[:, c * EH * P:(c + 1) * EH * P]
            pos = lambda ap: ap.rearrange("p (b e) -> p b e", e=P)
            vstep(nc.vector.tensor_scalar(gate, x, FLOOR, 2 * BIG, ALU.is_gt, ALU.mult))
            vstep(nc.vector.tensor_scalar(gate, gate, -BIG, None, ALU.add))
            vstep(nc.vector.tensor_copy(gate2, gate))
            nc.vector.memset(pos(gate)[:, :, 0:1], -BIG)
            vstep(nc.vector.memset(pos(gate2)[:, :, P - 1:P], -BIG))
            nc.vector.tensor_tensor_scan(fwd, gate, x, -BIG, ALU.min, ALU.max)
            vstep(nc.vector.tensor_tensor_scan(bwd[:, ::-1], gate2[:, ::-1], x[:, ::-1], -BIG,
                                               ALU.min, ALU.max))
            return x, pos

        def max_vector(dve):
            dve.wait_ge(s_lts, EB // 4)
            for c in range(4):
                x, pos = scans(c)
                blocks = slice(c * EH, (c + 1) * EH)
                nc.vector.tensor_copy(ends_f[:, 0, blocks], pos(fwd)[:, :, P - 1])
                nc.vector.tensor_copy(ends_f[:, 1, blocks], pos(bwd)[:, :, 0])
                vstep(nc.vector.tensor_reduce(ends_f[:, 2, blocks], pos(x), AX.X, ALU.min))
            vstep(nc.vector.tensor_scalar(ends_f[:, 2, :], ends_f[:, 2, :], FLOOR, 2 * BIG, ALU.is_gt,
                                          ALU.mult))
            nc.vector.tensor_scalar(ends_f[:, 2, :], ends_f[:, 2, :], -BIG, None, ALU.add).then_inc(s_ed, 1)
            dve.wait_ge(s_edl, 48)
            nc.vector.memset(chain[:, 3, 0:1], -BIG)
            nc.vector.memset(chain[:, 4, T - 1:T], -BIG)
            vstep(nc.vector.tensor_tensor_scan(chain[:, 3, 1:T], chain[:, 2, 0:T - 1], chain[:, 0, 0:T - 1],
                                               -BIG, ALU.min, ALU.max))
            nc.vector.tensor_tensor_scan(chain[:, 4, T - 2::-1], chain[:, 2, T - 1:0:-1],
                                         chain[:, 1, T - 1:0:-1], -BIG, ALU.min, ALU.max).then_inc(s_ca, 1)
            dve.wait_ge(s_cal, 32)
            for c in range(4):
                x = LT[:, c * EH * P:(c + 1) * EH * P].rearrange("p (b e) -> p b e", e=P)
                blocks = slice(c * EH, (c + 1) * EH)
                for n, e in enumerate((0, P - 1)):
                    g1 = red[:, n, 0:EH]
                    vstep(nc.vector.tensor_scalar(g1, x[:, :, e], FLOOR, 2 * BIG, ALU.is_gt, ALU.mult))
                    vstep(nc.vector.scalar_tensor_tensor(g1, g1, -BIG, carries[:, n, blocks], ALU.add,
                                                         ALU.min))
                    vstep(nc.vector.tensor_tensor(x[:, :, e], x[:, :, e], g1, ALU.max))
                xq, pos = scans(c)
                nc.vector.scalar_tensor_tensor(xq, fwd, FLOOR, bwd, ALU.max, ALU.max).then_inc(s_mx, 1)
                dve.wait_ge(s_mx, c + 1)
            for g in range(EB // 4):
                t = g * 4 * (P // H0)
                at = S[0][:, t:t + 4 * (P // H0), 2:2 + H0]
                dve.wait_ge(s_mt, g + 1)
                nc.vector.tensor_tensor(at, at, banks[4 + g % 4][:, :].rearrange("p (t h) -> p t h", h=H0),
                                        ALU.subtract).then_inc(s_sh, 1)

        def max_sync(sp):
            sp.wait_ge(s_ed, 1)
            for n in range(3):
                sp.dma_start(edge_d[n].rearrange("(b p) -> p b", p=P), ends_f[:, n, :],
                             allow_slow_non_contiguous=True).then_inc(s_edd, 16)
            sp.wait_ge(s_edd, 48)
            for n in range(3):
                sp.dma_start(chain[:, n, :], edge_d[n].rearrange("(t h) -> h t", h=H0),
                             allow_slow_non_contiguous=True).then_inc(s_edl, 16)
            sp.wait_ge(s_ca, 1)
            for n in range(2):
                sp.dma_start(carry_d[n].rearrange("(t h) -> h t", h=H0), chain[:, 3 + n, :],
                             allow_slow_non_contiguous=True).then_inc(s_cad, 16)
            sp.wait_ge(s_cad, 32)
            for n in range(2):
                sp.dma_start(carries[:, n, :], carry_d[n].rearrange("(b p) -> p b", p=P),
                             allow_slow_non_contiguous=True).then_inc(s_cal, 16)

        def add_sums(dve, m, k, acc, bank):
            def fn(i, s, g):
                dve.wait_ge(s_sum, g + (m * NG + 1))
                for j in range(TG):
                    base = dve.value_load(base_i[k][0:1, ds(g * TG + j, 1)], min_val=0, max_val=N - 1)
                    to, add = acc(base), bank(s, j)
                    since(dve, s_acc, g * TG + (m * T + j))
                    nc.vector.tensor_tensor(to, to, add, ALU.add).then_inc(s_acc, 1)
            return fn

        def b_vector(dve):
            dve.wait_ge(s_ex, 1)
            vstep(nc.vector.memset(acc0[:, :], 0.0))

            def ring(i, s, g):
                since(dve, s_sum, g - SLOTS + 1)

            def weigh(i, s, g):
                since(dve, s_sum, g - 1)
                w = S[0][:, ds(g * TG, TG), 2:2 + H0].unsqueeze(3)
                nc.vector.tensor_tensor(
                    vw[:, s % 2, :, 0:D0].rearrange("p j (h d) -> p j h d", h=H0),
                    values[:, ds(g * TG, TG), :].rearrange("p j (h d) -> p j h d", h=H0),
                    w.to_broadcast([P, TG, H0, D0 // H0]), ALU.mult).then_inc(s_vw, 1)

            sums = add_sums(dve, 0, 0, lambda base: acc0[:, ds(base, P)],
                            lambda s, j: banks[4 + s % 2][:, j * P:(j + 1) * P])
            fours(dve, [(0, one_hot(dve, 0, 0, ring)), (0, weigh), (1, sums)])

        def b_scalar(act):
            def beside(i, s, g):
                since(act, s_sum, g - 1)
                w = S[0][:, ds(g * TG, TG), 2:2 + H0].unsqueeze(3)
                nc.scalar.copy(vw[:, s % 2, :, D0:2 * D0].rearrange("p j (h d) -> p j h d", h=H0),
                               w.to_broadcast([P, TG, H0, D0 // H0])).then_inc(s_wb, 1)

            act.wait_ge(s_ex, 1)
            fours(act, [(0, beside)])

        def b_tensor(pe):
            def fn(i, s, g):
                pe.wait_ge(s_R, g + (NG + 1))
                pe.wait_ge(s_vw, g + 1)
                pe.wait_ge(s_wb, g + 1)
                since(pe, s_acc, (g - 1) * TG)
                for j in range(TG):
                    done = nc.tensor.matmul(banks[4 + s % 2][:, j * P:(j + 1) * P], vw[:, s % 2, j, :],
                                            R[:, s, j, :], start=True, stop=True)
                done.then_inc(s_sum, 1)

            fours(pe, [(0, fn)])

        def out0_sync(sp):
            sp.wait_ge(s_acc, T)
            sp.dma_start(den0[:, :], acc0[D0:2 * D0, :]).then_inc(s_den, 16)

        def out0_vector(dve):
            hT_borders()
            dve.wait_ge(s_den, 16)
            vstep(nc.vector.tensor_scalar(den0[:, :], den0[:, :], 1e-16, None, ALU.add))
            vstep(nc.vector.reciprocal(den0[:, :], den0[:, :]))
            nc.vector.tensor_tensor(hT[0:D0, 0:NPAD], acc0[0:D0, 0:NPAD], den0[:, 0:NPAD],
                                    ALU.mult).then_inc(s_agg, 1)
            for g in range(4):
                lo, hi = g * 7, min(g * 7 + 7, NB)
                dve.wait_ge(s_o, g + 1)
                vstep(nc.vector.tensor_tensor(
                    xs[:, lo:hi, :], xs[:, lo:hi, :],
                    banks[g][:, 0:(hi - lo) * D0].rearrange("p (b c) -> p b c", c=D0), ALU.add))

        def out_tensor(pe, lhs, rhs):
            for g in range(4):
                for b in range(g * 7, min(g * 7 + 7, NB)):
                    done = nc.tensor.matmul(banks[g][:, (b % 7) * D0:(b % 7 + 1) * D0],
                                            lhs[:, b * P:(b + 1) * P], rhs, start=True, stop=True)
                done.then_inc(s_o, 1)

        def embed_tensor(pe):
            for c, (lo, w) in enumerate(CHUNKS):
                nc.tensor.matmul(banks[c][:, 0:w], Wp[:, :], hT[0:D0, lo:lo + w], start=True,
                                 stop=True).then_inc(s_c1, 1)

        def embed_scalar(act):
            for c, (lo, w) in enumerate(CHUNKS):
                act.wait_ge(s_c1, c + 1)
                nc.scalar.activation(emb[:, lo:lo + w], banks[c][:, 0:w], ACT.Identity,
                                     bias=shift[:, 0:1]).then_inc(s_emb, 1)

        def c_vector(dve, l):
            n = l + 1
            dot = logits(dve, n, DM, H1)

            def clip(i, s, g):
                dot(i, s, g)
                since(dve, s_wt, g + (l * NG - 1))
                nc.vector.tensor_scalar(red[:, s % 2, 0:TG * H1], red[:, s % 2, 0:TG * H1], -10.0, 10.0,
                                        ALU.max, ALU.min).then_inc(s_lg, 1)

            def ring(i, s, g):
                since(dve, s_sum, g + (n * NG - SLOTS + 1))

            def weigh(i, s, g):
                dve.wait_ge(s_vc, g + (n * NG + 1))
                since(dve, s_sum, g + (n * NG - 1))
                nc.vector.scalar_tensor_tensor(
                    wts[:, s % 2, :].rearrange("p (j h) -> p j h", j=TG),
                    seg[1][:, ds(g * TG, TG)].unsqueeze(2).to_broadcast([P, TG, H1]), 0.0,
                    red[:, s % 2, 0:TG * H1].rearrange("p (j h) -> p j h", j=TG),
                    ALU.is_ge, ALU.mult).then_inc(s_wt, 1)
                dve.wait_ge(s_wt, g + (l * NG + 1))
                nc.vector.tensor_tensor(
                    vw[:, s % 2, :, :].rearrange("p j (h d) -> p j h d", h=H1),
                    kv[:, s, :, DM:2 * DM].rearrange("p j (h d) -> p j h d", h=H1),
                    wts[:, s % 2, :].rearrange("p (j h) -> p j h", j=TG).unsqueeze(3)
                    .to_broadcast([P, TG, H1, DM // H1]),
                    ALU.mult).then_inc(s_vw, 1)

            sums = add_sums(dve, n, 1, lambda base: acc1[:, :, ds(base, P)],
                            lambda s, j: banks[4 + 2 * (s % 2) + j // 2][:, (j % 2) * 2 * P:(j % 2 + 1) * 2 * P]
                            .rearrange("p (a m) -> p a m", a=2))
            nc.vector.memset(acc1[:, :, :], 0.0).then_inc(s_m1, 1)
            dve.wait_ge(s_m1, l + 1)
            fours(dve, [(0, one_hot(dve, n, 1, ring)), (1, clip), (2, weigh), (3, sums)])

        def c_scalar(act, l):
            n = l + 1

            def exp(i, s, g):
                act.wait_ge(s_lg, g + (n * NG + 1))
                nc.scalar.activation(red[:, s % 2, 0:TG * H1], red[:, s % 2, 0:TG * H1],
                                     ACT.Exp).then_inc(s_vc, 1)

            def beside(i, s, g):
                act.wait_ge(s_wt, g + (l * NG + 1))
                since(act, s_sum, g + (n * NG - 1))
                nc.scalar.copy(wx[:, s % 2, :, :].rearrange("p j (h d) -> p (j h) d", h=H1),
                               wts[:, s % 2, :].unsqueeze(2).to_broadcast([P, TG * H1, DM // H1])
                               ).then_inc(s_wb, 1)

            fours(act, [(-3, stage_indices(act, n, 1)), (0, copy_transposed(act, n)), (1, exp),
                        (2, beside)])

        def c_tensor(pe, l):
            n = l + 1

            def sums(i, s, g):
                pe.wait_ge(s_vw, g + (n * NG + 1))
                pe.wait_ge(s_wb, g + (n * NG + 1))
                since(pe, s_acc, g * TG + (n * T - TG))
                for j in range(TG):
                    to = banks[4 + 2 * (s % 2) + j // 2]
                    at = (j % 2) * 2 * P
                    nc.tensor.matmul(to[:, at:at + P], vw[:, s % 2, j, :], R[:, s, j, :], start=True,
                                     stop=True)
                    done = nc.tensor.matmul(
                        to[:, at + P:at + 2 * P], wx[:, s % 2, j, :], R[:, s, j, :], start=True, stop=True)
                done.then_inc(s_sum, 1)

            fours(pe, [(0, transposes(pe, n, n + 1)), (1, expand(pe, n, DM)), (2, sums)])

        def post_vector(dve, l):
            num, den = acc1[:, 0, :], acc1[:, 1, :]
            dve.wait_ge(s_acc, T * (l + 2))
            vstep(nc.vector.tensor_scalar(den, den, 1e-8, None, ALU.add))
            vstep(nc.vector.reciprocal(den, den))
            vstep(nc.vector.tensor_tensor(num, num, den, ALU.mult))
            nc.vector.tensor_tensor(num, num, emb[:, :], ALU.add).then_inc(s_c1x, 1)
            C = len(CHUNKS)
            for c, (lo, w) in enumerate(CHUNKS):
                dve.wait_ge(s_mm, 2 * C * l + c + 1)
                vstep(nc.vector.tensor_tensor(cent[:, lo:lo + w], num[:, lo:lo + w], banks[c][:, 0:w],
                                              ALU.subtract))
                nc.vector.tensor_tensor(work1[:, lo:lo + w], cent[:, lo:lo + w], cent[:, lo:lo + w],
                                        ALU.mult).then_inc(s_sq, 1)
            dve.wait_ge(s_root, (l + 1) * C)
            vstep(nc.vector.reciprocal(work1[:, :], work1[:, :]))
            nc.vector.tensor_tensor(cent[:, :], cent[:, :], work1[:, :], ALU.mult).then_inc(s_nm, 1)

        def post_tensor(pe, l):
            C = len(CHUNKS)
            pe.wait_ge(s_c1x, l + 1)
            for c, (lo, w) in enumerate(CHUNKS):
                nc.tensor.matmul(banks[c][:, 0:w], avg[:, :], acc1[:, 0, lo:lo + w], start=True,
                                 stop=True).then_inc(s_mm, 1)
            for c, (lo, w) in enumerate(CHUNKS):
                pe.wait_ge(s_sq, l * C + c + 1)
                nc.tensor.matmul(banks[c][:, 0:w], avg[:, :], work1[:, lo:lo + w], start=True,
                                 stop=True).then_inc(s_mm, 1)

        def post_scalar(act, l):
            C = len(CHUNKS)
            for c, (lo, w) in enumerate(CHUNKS):
                act.wait_ge(s_mm, 2 * C * l + C + c + 1)
                nc.scalar.activation(work1[:, lo:lo + w], banks[c][:, 0:w], ACT.Sqrt,
                                     bias=eps[:, 0:1]).then_inc(s_root, 1)
            act.wait_ge(s_nm, l + 1)
            nc.scalar.activation(emb[:, :], cent[:, :], ACT.Identity, bias=lnb[:, l:l + 1],
                                 scale=lns[:, l:l + 1]).then_inc(s_emb, 1)

        block = ctx.enter_context(nc.Block())
        EMB = len(CHUNKS)

        @block.sync
        def _(sp):
            loads_sync(sp)
            load_x(sp)
            load_weights(sp)
            for k in range(2):
                sort_sync(sp, k)
            tables_sync(sp, 0, stage0, D0, q0_d, kv0_d)
            windows_sync(sp, 0, 0, q0_d, D0)
            max_sync(sp)
            out0_sync(sp)
            for l in range(LAYERS):
                tables_sync(sp, l + 1, stage1, DM, q1_d[l], kv1_d[l])
                windows_sync(sp, l + 1, 1, q1_d[l], DM)
            full = (NB - 1) * P
            sp.wait_ge(s_fin, 4)
            sp.dma_start(out[0:full].rearrange("(b p) c -> p b c", p=P), xs[:, 0:NB - 1, :]).then_inc(s_out, 16)
            sp.dma_start(out[full:N], xs[0:N - full, NB - 1, :]).then_inc(s_out, 16)
            sp.wait_ge(s_out, 32)

        @block.gpsimd
        def _(gp):
            constants_gpsimd(gp)
            zeros_gpsimd(gp)
            for k in range(2):
                sort_gpsimd(gp, k)
            gather_gpsimd(gp, 0, kv0_d, D0)
            for l in range(LAYERS):
                gather_gpsimd(gp, l + 1, kv1_d[l], DM)

        @block.vector
        def _(dve):
            constants_vector(dve)
            for k in range(2):
                sort_vector(dve, k)
            dve.wait_ge(s_seg, 2)
            dve.wait_ge(s_x, 32)
            norm_vector(dve, 0)
            dve.wait_ge(s_seg, 2)
            a_vector(dve)
            max_vector(dve)
            b_vector(dve)
            out0_vector(dve)
            norm_vector(dve, 1)
            dve.wait_ge(s_w, wcount[0])
            vstep(nc.vector.tensor_tensor(shift[:, 0:1], shift[:, 0:1], shift[:, 1:2], ALU.add))
            nc.vector.tensor_tensor(xs[:, :, :], xs[:, :, :], invb[:, :].unsqueeze(1).to_broadcast([P, NB, D0]),
                                    ALU.add).then_inc(s_xb, 1)
            for l in range(LAYERS):
                dve.wait_ge(s_emb, EMB + l)
                c_vector(dve, l)
                post_vector(dve, l)
            dve.wait_ge(s_xb, 1)
            for g in range(4):
                lo, hi = g * 7, min(g * 7 + 7, NB)
                dve.wait_ge(s_o, g + 5)
                nc.vector.tensor_tensor(xs[:, lo:hi, :], xs[:, lo:hi, :],
                                        banks[g][:, 0:(hi - lo) * D0].rearrange("p (b c) -> p b c", c=D0),
                                        ALU.add).then_inc(s_fin, 1)

        @block.scalar
        def _(act):
            for k in range(2):
                sort_scalar(act, k)
            norm_scalar(act, 0)
            act.wait_ge(s_fill, 32)
            project_scalar(act, 0, stage0, 3 * D0)
            act.wait_ge(s_seg, 2)
            act.wait_ge(s_tab, 32)
            fours(act, [(-3, stage_indices(act, 0, 0)), (0, copy_transposed(act, 0)), (1, keep_values(act))])
            max_scalar(act)
            b_scalar(act)
            norm_scalar(act, 1)
            act.wait_ge(s_xb, 1)
            embed_scalar(act)
            for l in range(LAYERS):
                project_scalar(act, l + 1, stage1, 3 * DM)
                c_scalar(act, l)
                post_scalar(act, l)

        @block.tensor
        def _(pe):
            for k in range(2):
                sort_tensor(pe, k)
            norm_tensor(pe, 0)
            pe.wait_ge(s_w, wcount[0])
            pe.wait_ge(s_zero, 2)
            project_tensor(pe, 0, hT, W0[:, :], 3 * D0)
            pe.wait_ge(s_pjs, NT)
            fours(pe, [(0, transposes(pe, 0, 0)), (1, expand(pe, 0, D0))])
            max_tensor(pe)
            b_tensor(pe)
            pe.wait_ge(s_agg, 1)
            out_tensor(pe, hT, Wo[:, :])
            norm_tensor(pe, 1)
            embed_tensor(pe)
            for l in range(LAYERS):
                pe.wait_ge(s_emb, EMB + l)
                project_tensor(pe, l + 1, emb, W1[:, l, :, :].rearrange("p a n -> p (a n)"), 3 * DM)
                pe.wait_ge(s_pjs, (l + 2) * NT)
                c_tensor(pe, l)
                post_tensor(pe, l)
            pe.wait_ge(s_emb, EMB + LAYERS)
            out_tensor(pe, emb, invw[:, :])


_INS = ['x', 'src', 'dst', 'edge_attr_8', 'L0_gnn_Wq', 'L0_gnn_bq', 'L0_gnn_Wk', 'L0_gnn_bk', 'L0_gnn_Wv',
        'L0_gnn_bv', 'L0_gnn_Wo', 'L0_gnn_bo', 'L1_gnn_W_P_w', 'L1_gnn_W_P_b', 'L1_gnn_W_pos',
        'L1_gnn_qT', 'L1_gnn_kT', 'L1_gnn_vT', 'L1_gnn_ln_scale', 'L1_gnn_ln_bias', 'L1_gnn_inv_w',
        'L1_gnn_inv_b']


def kernel(**inputs):
    import numpy as _np
    import concourse.bacc as _bacc
    from concourse import mybir as _mybir
    from concourse.bass_utils import run_bass_kernel_spmd as _run

    nc = _bacc.Bacc("TRN2", target_bir_lowering=False, num_devices=1)
    arrays, args = {}, []
    for name in _INS:
        a = _np.ascontiguousarray(inputs[name])
        arrays[f"in_{name}_dram"] = a
        args.append(nc.dram_tensor(f"in_{name}_dram", a.shape, _mybir.dt.from_np(a.dtype), kind="ExternalInput").ap())
    args.append(nc.dram_tensor("out_0_dram", (N, D0), _mybir.dt.from_np(_np.dtype("float32")),
                               kind="ExternalOutput").ap())
    build(nc, *args)
    r = _run(nc, [arrays], core_ids=[0])
    return r.results[0]["out_0_dram"]
```

```python
from contextlib import ExitStack

import concourse.bass as bass
from concourse import mybir

P = 128
N = 3125
E = 53125
D0, H0 = 64, 8
DM, H1 = 128, 4
LAYERS = 2
EP, ET = 125, 425
EG = 5
NEG = ET // EG
NB = -(-N // P)
NPAD = NB * P
NWIN = NPAD + P
TG = 4
SLOTS = 4
T = 448
NG = T // TG
TI = T // (TG * SLOTS)
HI = 32
WP = [2 + H0, 2]
NONE = -3.0e38
FLOOR = -1.0e30
BIG = 1.0e38
CHUNKS = [(c, min(512, NWIN - c)) for c in range(0, NWIN, 512)]
assert EP * ET == E and T * P >= N + E and T % (TG * SLOTS) == 0 and NEG % 2 == 1


def build(nc, x, src, dst, edge_attr, wq, bq, wk, bk, wv, bv, wo, bo, wp, wpb, wpos, qT, kT, vT,
          ln_scale, ln_bias, inv_w, inv_b, out):
    f32, i32, f16 = mybir.dt.float32, mybir.dt.int32, mybir.dt.float16
    ALU = mybir.AluOpType
    ACT = mybir.ActivationFunctionType
    AX = mybir.AxisListType
    ds = bass.ds

    ctx = ExitStack()
    with ctx:
        def sb(name, shape, dt=f32):
            return ctx.enter_context(nc.sbuf_tensor(name, shape, dt))

        def dram(name, shape, dt=f32):
            return nc.dram_tensor(name, shape, dt, kind="Internal").ap()

        def sem(name):
            return ctx.enter_context(nc.semaphore(name))

        sorted_d = [dram(f"sorted{k}_d", [P * T, WP[k]]) for k in range(2)]
        npos_d = [dram(f"npos{k}_d", [HI * P]) for k in range(2)]
        base_d = [dram(f"base{k}_d", [T]) for k in range(2)]
        basei_d = [dram(f"basei{k}_d", [T], i32) for k in range(2)]
        kv0_d = dram("kv0_d", [NPAD, 2 * D0])
        q0_d = dram("q0_d", [NWIN, D0])
        kv1_d = [dram(f"kv1_{l}_d", [NPAD, 2 * DM]) for l in range(LAYERS)]
        q1_d = [dram(f"q1_{l}_d", [NWIN, DM]) for l in range(LAYERS)]
        edge_d = [dram(f"edge{n}_d", [T * H0]) for n in range(3)]
        carry_d = [dram(f"carry{n}_d", [T * H0]) for n in range(2)]

        ident = sb("ident", [P, P])
        ident16 = sb("ident16", [P, P], f16)
        diff = sb("diff", [P, P])
        below = sb("below", [P, P])
        above = sb("above", [P, P])
        iota = sb("iota", [P, P])
        iota16 = sb("iota16", [P, P], f16)
        ones = sb("ones", [P, P])
        ones16 = sb("ones16", [P, P], f16)
        thr = sb("thr", [T // 4, 4])
        arena = sb("arena", [P, T * D0])

        def part(start, *shape):
            size = 1
            for n in shape:
                size *= n
            ap = arena[:, start:start + size]
            if len(shape) == 2:
                ap = ap.rearrange("p (a b) -> p a b", a=shape[0])
            return ap

        sort_at = [ET * H0 + T * WP[0] + 2 * N + 2 * T * WP[1] + 11 * ET + 2 * T]

        def sort_part(rows, *shape, dt=f32):
            size = 1
            for n in shape:
                size *= n
            words = size if dt in (f32, i32) else -(-size // 2)
            ap = arena[0:rows, sort_at[0]:sort_at[0] + words]
            sort_at[0] += words + words % 2
            if dt is not f32:
                ap = ap.bitcast(dt)[:, 0:size]
            if len(shape) == 2:
                ap = ap.rearrange("p (a b) -> p a b", a=shape[0])
            if len(shape) == 3:
                ap = ap.rearrange("p (a b c) -> p a b c", a=shape[0], b=shape[1])
            return ap

        attr = arena[0:EP, 0:ET * H0].rearrange("p (t h) -> p t h", h=H0)
        empty = part(ET * H0, T, WP[0])
        npos_bc = part(ET * H0 + T * WP[0], N)
        o = ET * H0 + T * WP[0] + 2 * N + T * WP[1]
        ends_i = part(o, 2, ET).bitcast(i32)[0:EP]
        ends = part(o + 2 * ET, 2, ET)[0:EP]
        digit_i = part(o + 4 * ET, ET).bitcast(i32)[0:EP]
        key1 = [part(o + (5 + k) * ET, ET)[0:EP] for k in range(2)]
        keyc = [part(o + (7 + k) * ET, ET)[0:EP] for k in range(2)]
        khi = [part(o + (9 + k) * ET, ET).bitcast(f16)[0:EP, 0:ET] for k in range(2)]
        klo = [part(o + (9 + k) * ET, ET).bitcast(f16)[0:EP, ET:2 * ET] for k in range(2)]
        base_bc = [part(o + 11 * ET + k * T, T) for k in range(2)]
        npos_le = part(ET * H0 + T * WP[0] + N, N)
        empty2 = part(ET * H0 + T * WP[0] + 2 * N, T, WP[1])
        A16 = [sort_part(EP, 2, EG, HI, dt=f16) for _ in range(2)]
        B16 = [sort_part(EP, 2, EG, P, dt=f16) for _ in range(2)]
        AT = [sort_part(HI, 2, EG, EP) for _ in range(2)]
        diag = [sort_part(EP, EG, EP, dt=f16) for _ in range(2)]
        zeros16 = sort_part(EP, P, dt=f16)
        nodes = sort_part(HI, P)
        Hs = [sort_part(HI, 2, P) for _ in range(2)]
        scr = [sort_part(P, 2, 2, P) for _ in range(2)]
        rank = [sort_part(EP, 2, EG) for _ in range(2)]
        first = [sort_part(EP, 2, EG) for _ in range(2)]
        place = [sort_part(EP, 2, EG, dt=i32) for _ in range(2)]
        phi = [sort_part(EP, 2, EG, dt=i32) for _ in range(2)]
        plo = [sort_part(EP, 2, EG, dt=i32) for _ in range(2)]
        row = [sort_part(EP, 2, EG, dt=i32) for _ in range(2)]
        pay = [sort_part(EP, 2, EG, WP[k]) for k in range(2)]
        nullm = sort_part(HI, P)
        cnt = [sort_part(HI, P) for _ in range(2)]
        incl = [scr[k][0:HI, 0, 0, :] for k in range(2)]
        npos = [sb(f"npos{k}", [HI, P])[:, :] for k in range(2)]
        seed = [sb(f"seed{k}", [HI, P])[:, :] for k in range(2)]
        offs = [sb(f"offs{k}", [HI, 1])[:, :] for k in range(2)]
        basec = [sb(f"basec{k}", [T // 4, 4])[:, :] for k in range(2)]
        basei = [sb(f"basei{k}", [T // 4, 4], i32)[:, :] for k in range(2)]
        base_i = [sb(f"base_i{k}", [1, T], i32) for k in range(2)]
        S = [sb("S0", [P, T, WP[0]]), part(o + 11 * ET + 2 * T, T, WP[1])]
        seg = [sb(f"seg{k}", [P, T]) for k in range(2)]
        idx = [sb(f"idx{k}", [P, T], i32) for k in range(2)]

        banks = [ctx.enter_context(nc.psum_tensor(f"bank{n}", [P, 512], f32)) for n in range(8)]

        def sems(name):
            return [sem(f"{name}{k}") for k in range(2)]

        s_const = sem("s_const")
        s_mask = sem("s_mask")
        s_ends = sem("s_ends")
        s_attr = sem("s_attr")
        s_v = sem("s_v")
        s_key = sem("s_key")
        s_oh = sems("s_oh")
        s_ohu = sems("s_ohu")
        s_scan = sems("s_scan")
        s_offs = sems("s_offs")
        s_npos = sems("s_npos")
        s_nposd = sems("s_nposd")
        s_nposb = sems("s_nposb")
        s_seed = sems("s_seed")
        s_base = sems("s_base")
        s_based = sems("s_based")
        s_basel = sems("s_basel")
        s_at = sems("s_at")
        s_ats = sems("s_ats")
        s_diag = sems("s_diag")
        s_bc = sems("s_bc")
        s_rank = sems("s_rank")
        s_look = sems("s_look")
        s_first = sems("s_first")
        s_h = sems("s_h")
        s_hs = sems("s_hs")
        s_pl = sems("s_pl")
        s_dig = sems("s_dig")
        s_row = sems("s_row")
        s_pay = sems("s_pay")
        s_sc = [[sem(f"s_sc{k}{n}") for n in range(2)] for k in range(2)]
        s_pat = sem("s_pat")
        s_fill = sem("s_fill")
        s_S = sems("s_S")
        s_seg = sem("s_seg")
        s_turn = sem("s_turn")

        vcount = [0]

        def vstep(ins):
            vcount[0] += 1
            ins.then_inc(s_v, 1)
            nc.vector.wait_ge(s_v, vcount[0])

        def since(eng, semaphore, value):
            if not isinstance(value, int) or value > 0:
                eng.wait_ge(semaphore, value)

        def in_pairs(eng, body):
            for b in range(2):
                body(b, 0, b, False)
            with eng.Fori(1, NEG // 2) as i:
                for b in range(2):
                    body(i * 2 + b, i, b, False)
            body(NEG - 1, NEG // 2, 0, True)

        iota_g = iota16[:, :].unsqueeze(1).to_broadcast([P, EG, P])

        H = [banks[k][0:HI, 0:P] for k in range(2)]
        KEYS = [banks[2 + k][0:EP, 0:EP] for k in range(2)]
        LOOK = [banks[4 + k][0:EP, 0:P] for k in range(2)]
        OFFS = [banks[6 + k][0:HI, 0:1] for k in range(2)]
        ATP = [banks[6 + k][:, :].bitcast(f16)[0:HI, 0:EG * P].rearrange("p (j e) -> p j e", j=EG)
               for k in range(2)]
        BOTH = range(2)

        def sort_sync(sp):
            sp.wait_ge(s_pat, 1)
            for k in BOTH:
                sp.dma_start(sorted_d[k].rearrange("(p t) w -> p t w", p=P),
                             (empty, empty2)[k]).then_inc(s_fill, 16)
            for k in BOTH:
                sp.wait_ge(s_npos[k], 1)
                sp.dma_start(npos_d[k].rearrange("(h l) -> h l", h=HI), npos[k]).then_inc(s_nposd[k], 16)
            for k in BOTH:
                sp.wait_ge(s_nposd[k], 16)
                if k:
                    sp.wait_ge(s_base[0], 1)
                sp.dma_start(npos_bc[0:T // 4, :],
                             npos_d[k][0:N].partition_broadcast(T // 4)).then_inc(s_nposb[k], 16)
            for k in BOTH:
                sp.wait_ge(s_base[k], 1)
                sp.dma_start(base_d[k].rearrange("(p g) -> p g", g=4), basec[k]).then_inc(s_based[k], 16)
                sp.dma_start(basei_d[k].rearrange("(p g) -> p g", g=4), basei[k]).then_inc(s_based[k], 16)
            for k in BOTH:
                sp.wait_ge(s_based[k], 32)
                sp.dma_start(base_bc[k][:, :], base_d[k].partition_broadcast(P)).then_inc(s_basel[k], 16)
                sp.dma_start(base_i[k][:, :],
                             basei_d[k].rearrange("(a n) -> a n", a=1)).then_inc(s_basel[k], 16)
            for k in BOTH:
                for b in range(2):
                    sp.wait_ge(s_sc[k][b], 16 * EG * (NEG // 2 + 1 - b))
                sp.dma_start(S[k][:, :, :],
                             sorted_d[k].rearrange("(p t) w -> p t w", p=P)).then_inc(s_S[k], 16)

        def onehots(k, g, b):
            cols = ds(g * EG, EG)
            nc.vector.tensor_tensor(A16[k][:, b, :, :], iota_g[0:EP, :, 0:HI],
                                    khi[k][:, cols].unsqueeze(2).to_broadcast([EP, EG, HI]), ALU.is_equal)
            nc.vector.tensor_tensor(B16[k][:, b, :, :], iota_g[0:EP, :, :],
                                    klo[k][:, cols].unsqueeze(2).to_broadcast([EP, EG, P]),
                                    ALU.is_equal).then_inc(s_oh[k], 1)

        def sort_vector(dve):
            for k in BOTH:
                key = 1 - k
                vstep(nc.vector.tensor_scalar(digit_i, ends_i[:, key, :], 7, None, ALU.logical_shift_right))
                vstep(nc.vector.tensor_copy(khi[k], digit_i))
                vstep(nc.vector.tensor_scalar(digit_i, ends_i[:, key, :], P - 1, None, ALU.bitwise_and))
                vstep(nc.vector.tensor_copy(klo[k], digit_i))
                nc.vector.tensor_scalar(key1[k], ends[:, key, :], 1.0, None, ALU.add)
                nc.vector.tensor_scalar(keyc[k], ends[:, key, :], -2048.0, None, ALU.add).then_inc(s_key, 1)
            dve.wait_ge(s_key, 2)

            def pass1(g, i, b, last):
                for k in BOTH:
                    since(dve, s_ohu[k], g - 1)
                    onehots(k, g, b)

            in_pairs(dve, pass1)
            for k in BOTH:
                dve.wait_ge(s_ohu[k], NEG)
                vstep(nc.vector.tensor_tensor(cnt[k], H[k], nullm[:, :], ALU.add))
                nc.vector.tensor_tensor_scan(incl[k], ones[0:HI, :], cnt[k], 0.0, ALU.mult,
                                             ALU.add).then_inc(s_scan[k], 1)
            for k in BOTH:
                dve.wait_ge(s_scan[k], 1)
                dve.wait_ge(s_offs[k], 1)
                vstep(nc.vector.tensor_copy(offs[k], OFFS[k]))
                nc.vector.scalar_tensor_tensor(npos[k], incl[k], offs[k], cnt[k], ALU.add,
                                               ALU.subtract).then_inc(s_npos[k], 1)
                dve.wait_ge(s_npos[k], 1)
                nc.vector.tensor_scalar(seed[k], npos[k], 1.0, None, ALU.add).then_inc(s_seed[k], 1)
            for k in BOTH:
                onehots(k, 0, 0)

            def bases(k):
                dve.wait_ge(s_nposb[k], 16)
                for g in range(4):
                    vstep(nc.vector.tensor_scalar(npos_le[0:T // 4, :], npos_bc[0:T // 4, :],
                                                  thr[:, g:g + 1], 0.0, ALU.is_le, ALU.add,
                                                  accum_out=basec[k][:, g:g + 1]))
                vstep(nc.vector.tensor_scalar(basec[k], basec[k], -1.0, None, ALU.add))
                nc.vector.tensor_copy(basei[k], basec[k]).then_inc(s_base[k], 1)

            def tiles(g, i, b, last):
                if not last:
                    for k in BOTH:
                        dve.wait_ge(s_h[k], g * EG + 1)
                        onehots(k, g + 1, 1 - b)
                for j in range(EG):
                    c = g * EG + j
                    for k in BOTH:
                        since(dve, s_first[k], c - 1)
                        dve.wait_ge(s_bc[k], c + 1)
                        nc.vector.scalar_tensor_tensor(
                            scr[k][0:EP, (b + j) % 2, 0, 0:EP], KEYS[k], keyc[k][:, ds(c, 1)],
                            below[0:EP, 0:EP], ALU.is_equal, ALU.mult,
                            accum_out=rank[k][:, b, j:j + 1]).then_inc(s_rank[k], 1)
                    for k in BOTH:
                        dve.wait_ge(s_look[k], c + 1)
                        nc.vector.scalar_tensor_tensor(
                            scr[k][0:EP, (b + j) % 2, 1, :], LOOK[k], 1.0, B16[k][:, b, j, :],
                            ALU.mult, ALU.mult, accum_out=first[k][:, b, j:j + 1]).then_inc(s_first[k], 1)
                for k in BOTH:
                    dve.wait_ge(s_first[k], g * EG + EG)
                    nc.vector.tensor_tensor(place[k][:, b, :], rank[k][:, b, :], first[k][:, b, :],
                                            ALU.add).then_inc(s_pl[k], 1)
                for k in BOTH:
                    dve.wait_ge(s_pl[k], g + 1)
                    nc.vector.tensor_scalar(phi[k][:, b, :], place[k][:, b, :], 7, None,
                                            ALU.logical_shift_right)
                    nc.vector.tensor_scalar(plo[k][:, b, :], place[k][:, b, :], P - 1, None,
                                            ALU.bitwise_and).then_inc(s_dig[k], 1)
                for k in BOTH:
                    dve.wait_ge(s_dig[k], g + 1)
                    since(dve, s_sc[k][b], i * (16 * EG))
                    nc.vector.scalar_tensor_tensor(row[k][:, b, :], plo[k][:, b, :], float(T),
                                                   phi[k][:, b, :], ALU.mult, ALU.add).then_inc(s_row[k], 1)

            in_pairs(dve, tiles)
            for k in BOTH:
                bases(k)
            for k in BOTH:
                dve.wait_ge(s_S[k], 16)
                dve.wait_ge(s_basel[k], 32)
                nc.vector.scalar_tensor_tensor(seg[k][:, 0:T], S[k][:, :, 0:1].rearrange("p t w -> p (t w)"),
                                               -1.0, base_bc[k][:, :], ALU.add, ALU.subtract)
                nc.vector.tensor_copy(idx[k][:, :], S[k][:, :, 1:2].rearrange("p t w -> p (t w)")
                                      ).then_inc(s_seg, 1)

        def sort_tensor(pe):
            pe.wait_ge(s_mask, 1)
            for k in BOTH:
                nc.tensor.matmul(H[k], zeros16[:, 0:HI], zeros16[:, :], start=True, stop=True,
                                 skip_group_check=True)

            def count(k, b, j):
                return nc.tensor.matmul(H[k], A16[k][:, b, j, :], B16[k][:, b, j, :], start=False,
                                        stop=True, skip_group_check=True)

            def hist(g, i, b, last):
                for k in BOTH:
                    pe.wait_ge(s_oh[k], g + 1)
                    for j in range(EG):
                        done = count(k, b, j)
                    done.then_inc(s_ohu[k], 1)

            in_pairs(pe, hist)
            for k in BOTH:
                pe.wait_ge(s_scan[k], 1)
                nc.tensor.matmul(OFFS[k], above[0:HI, 0:HI], incl[k][:, P - 1:P], start=True,
                                 stop=True).then_inc(s_offs[k], 1)
            for k in BOTH:
                pe.wait_ge(s_seed[k], 1)
                nc.tensor.matmul(H[k], ident[0:HI, 0:HI], seed[k], start=True, stop=True,
                                 skip_group_check=True).then_inc(s_h[k], 1)

            def transposes(k, g, b):
                pe.wait_ge(s_oh[k], g + (NEG + 1))
                since(pe, s_ats[k], g)
                for j in range(EG):
                    done = nc.tensor.transpose(ATP[k][:, j, 0:EP], A16[k][:, b, j, :], ident16[0:EP, 0:EP])
                done.then_inc(s_at[k], 1)

            def tiles(g, i, b, last):
                if not last:
                    for k in BOTH:
                        transposes(k, g + 1, 1 - b)
                for k in BOTH:
                    pe.wait_ge(s_ats[k], g + 1)
                for j in range(EG):
                    c = g * EG + j
                    for k in BOTH:
                        pe.wait_ge(s_hs[k], c + 1)
                        count(k, b, j).then_inc(s_h[k], 1)
                        pe.wait_ge(s_diag[k], c + 1)
                        since(pe, s_rank[k], c)
                        nc.tensor.matmul(KEYS[k], ones16[0:EP, 0:EP], diag[k][:, j, :],
                                         start=True, stop=True).then_inc(s_bc[k], 1)
                        since(pe, s_first[k], c)
                        nc.tensor.matmul(LOOK[k], AT[k][:, b, j, :], Hs[k][:, (b + j) % 2, :],
                                         start=True, stop=True).then_inc(s_look[k], 1)

            for k in BOTH:
                transposes(k, 0, 0)
            in_pairs(pe, tiles)

        def sort_scalar(act):
            act.wait_ge(s_ends, 32)
            act.wait_ge(s_attr, 16)
            act.wait_ge(s_key, 2)

            def diagonal(k, g, j):
                nc.scalar.activation(diag[k][:, j, :], ident16[0:EP, 0:EP], ACT.Copy,
                                     scale=keyc[k][:, ds(g * EG + j, 1)]).then_inc(s_diag[k], 1)

            def transposed(k, g, b):
                act.wait_ge(s_at[k], g + 1)
                nc.scalar.copy(AT[k][:, b, :, :], ATP[k][:, :, 0:EP]).then_inc(s_ats[k], 1)

            def table(k, n, slot):
                act.wait_ge(s_h[k], n)
                nc.scalar.copy(Hs[k][:, slot, :], H[k]).then_inc(s_hs[k], 1)

            def tiles(g, i, b, last):
                cols = ds(g * EG, EG)
                for k in BOTH:
                    since(act, s_sc[k][b], i * (16 * EG))
                    if k == 0:
                        nc.scalar.copy(pay[k][:, b, :, 2:WP[0]], attr[:, cols, :])
                    nc.scalar.copy(pay[k][:, b, :, 0:1], key1[k][:, cols].unsqueeze(2))
                    nc.scalar.copy(pay[k][:, b, :, 1:2],
                                   ends[:, k, cols].unsqueeze(2)).then_inc(s_pay[k], 1)
                if not last:
                    for k in BOTH:
                        transposed(k, g + 1, 1 - b)
                for j in range(EG):
                    c = g * EG + j
                    for k in BOTH:
                        table(k, c + 2, (b + j + 1) % 2)
                        if not last:
                            act.wait_ge(s_bc[k], c + 1)
                            diagonal(k, g + 1, j)

            for k in BOTH:
                for j in range(EG):
                    diagonal(k, 0, j)
                transposed(k, 0, 0)
                table(k, 1, 0)
            in_pairs(act, tiles)

        def sort_gpsimd(gp):
            gp.wait_ge(s_fill, 32)

            def tiles(g, i, b, last):
                for k in BOTH:
                    gp.wait_ge(s_row[k], g + 1)
                    gp.wait_ge(s_pay[k], g + 1)
                    gp.sem_inc(s_turn, 1)
                    for j in range(EG):
                        gp.indirect_dma_start(
                            out=sorted_d[k],
                            out_offset=bass.IndirectOffsetOnAxis(ap=row[k][:, b, j:j + 1], axis=0),
                            in_=pay[k][:, b, j, 0:WP[k]], in_offset=None).then_inc(s_sc[k][b], 16)

            in_pairs(gp, tiles)

        s_g = sem("s_g")
        gcount = [0]

        def gstep(ins):
            gcount[0] += 1
            ins.then_inc(s_g, 1)
            nc.gpsimd.wait_ge(s_g, gcount[0])

        def constants_gpsimd(gp):
            kw = dict(allow_small_or_imprecise_dtypes=True)
            nc.gpsimd.iota(diff[:, :], [[1, P]], base=0, channel_multiplier=-1, **kw)
            nc.gpsimd.iota(iota[:, :], [[1, P]], base=0, channel_multiplier=0, **kw)
            nc.gpsimd.iota(iota16[:, :], [[1, P]], base=0, channel_multiplier=0, **kw)
            nc.gpsimd.iota(nodes[:, :], [[1, P]], base=0, channel_multiplier=P, **kw)
            nc.gpsimd.iota(thr[:, :], [[P, 4]], base=0, channel_multiplier=4 * P, **kw).then_inc(s_const, 1)
            nc.gpsimd.memset(empty2[:, :, :], 0.0)
            gstep(nc.gpsimd.memset(empty[:, :, :], NONE))
            nc.gpsimd.memset(empty[:, :, 0:2], 0.0).then_inc(s_pat, 1)

        def constants_vector(dve):
            nc.vector.memset(ones[:, :], 1.0)
            nc.vector.memset(ones16[:, :], 1.0)
            nc.vector.memset(zeros16[:, :], 0.0)
            dve.wait_ge(s_const, 1)
            nc.vector.tensor_scalar(ident[:, :], diff[:, :], 0.0, None, ALU.is_equal)
            nc.vector.tensor_scalar(ident16[:, :], diff[:, :], 0.0, None, ALU.is_equal)
            nc.vector.tensor_scalar(below[:, :], diff[:, :], 0.0, None, ALU.is_lt)
            nc.vector.tensor_scalar(nullm[:, :], nodes[:, :], float(N), None, ALU.is_lt)
            nc.vector.tensor_scalar(above[:, :], diff[:, :], 0.0, None, ALU.is_gt).then_inc(s_mask, 1)
            dve.wait_ge(s_mask, 1)
            dve.wait_ge(s_ends, 32)
            vstep(nc.vector.tensor_copy(ends[:, :, :], ends_i[:, :, :]))

        def loads_sync(sp):
            sp.dma_start(ends_i[:, 0, :], src.rearrange("(p t) -> p t", p=EP)).then_inc(s_ends, 16)
            sp.dma_start(ends_i[:, 1, :], dst.rearrange("(p t) -> p t", p=EP)).then_inc(s_ends, 16)
            sp.dma_start(attr, edge_attr.rearrange("(p t) h -> p t h", p=EP)).then_inc(s_attr, 16)

        stage0 = part(0, NB + 1, 3 * D0)
        values = part(0, T, D0)
        stage1 = part(0, NB + 1, 3 * DM)
        acc1 = part((NB + 1) * 3 * DM, 2, NWIN)
        odd1 = part(0, 2, NWIN)
        o = (NB + 1) * 3 * DM + 2 * NWIN
        emb = part(o, NWIN)
        cent = part(o + NWIN, NWIN)
        work1 = part(o + 2 * NWIN, NWIN)
        hT = cent[0:D0 + 1, :]
        den0 = work1[0:D0, :]
        hs = part(o - NWIN, NB, D0)
        sq = part(o - 2 * NWIN, NB, D0)

        xs = sb("xs", [P, NB, D0])
        mean = sb("mean", [P, NB])
        var = sb("var", [P, NB])
        W0 = sb("W0", [D0 + 1, 3 * D0])
        Wo = sb("Wo", [D0 + 1, D0])
        Wp = sb("Wp", [D0, DM])
        shift = sb("shift", [P, 2])
        W1 = sb("W1", [P, LAYERS, 3, DM])
        lns = sb("lns", [P, LAYERS])
        lnb = sb("lnb", [P, LAYERS])
        invw = sb("invw", [P, D0])
        invb = sb("invb", [P, D0])
        avg = sb("avg", [P, P])
        eps = sb("eps", [P, 1])
        idxs = sb("idxs", [P, SLOTS, TG], i32)
        kv = sb("kv", [P, SLOTS, TG, 2 * DM])
        acc0 = kv[:, :, :, :].rearrange("p a b c -> p (a b c)")[:, 0:NWIN]
        scratch = sb("scratch", [P, SLOTS * TG * DM + 2 * TG * P + 2 * TG * DM])
        qw = scratch[:, 0:SLOTS * TG * DM].rearrange("p (s j c) -> p s j c", s=SLOTS, j=TG)
        o = SLOTS * TG * DM
        RT = scratch[:, o:o + 2 * TG * P].rearrange("p (s c) -> p s c", s=2)
        prods = scratch[:, o + 2 * TG * P:]
        prod = prods.rearrange("p (s j c) -> p s j c", s=2, j=TG)
        odd0 = scratch[:, 0:NWIN]
        chain = scratch[0:H0, 0:5 * T].rearrange("p (n t) -> p n t", n=5)
        R = sb("R", [P, SLOTS, TG, P])
        red = sb("red", [P, 2, TG * H0])
        wts = sb("wts", [P, 2, TG * H1])
        vw = sb("vw", [P, 2, TG, DM])
        wx = sb("wx", [P, 2, TG, DM])
        LT = kv[:, :, :, :].rearrange("p a b c -> p (a b c)")[:, 0:T * H0]
        EB = T * H0 // P
        EH = EB // 4
        fwd = prods[:, 0:EH * P]
        bwd = vw[:, :, :, :].rearrange("p a b c -> p (a b c)")[:, 0:EH * P]
        gate = R[:, :, :, :].rearrange("p a b c -> p (a b c)")[:, 0:EH * P]
        gate2 = R[:, :, :, :].rearrange("p a b c -> p (a b c)")[:, EH * P:2 * EH * P]
        ends_f = sb("ends_f", [P, 3, EB])
        carries = sb("carries", [P, 2, EB])

        s_x = sem("s_x")
        s_w = sem("s_w")
        s_zero = sem("s_zero")
        s_var = sem("s_var")
        s_std = sem("s_std")
        s_hn = sem("s_hn")
        s_tp = sem("s_tp")
        s_ts = sem("s_ts")
        s_pj = sem("s_pj")
        s_pjs = sem("s_pjs")
        s_tab = sem("s_tab")
        s_ix = sem("s_ix")
        s_kv = [sem(f"s_kv{n}") for n in range(SLOTS)]
        s_qw = [sem(f"s_qw{n}") for n in range(SLOTS)]
        s_R = sem("s_R")
        s_dist = sem("s_dist")
        s_rt = sem("s_rt")
        s_rts = sem("s_rts")
        s_qe = sem("s_qe")
        s_prod = sem("s_prod")
        s_red = sem("s_red")
        s_lg = sem("s_lg")
        s_vc = sem("s_vc")
        s_wt = sem("s_wt")
        s_vw = sem("s_vw")
        s_wb = sem("s_wb")
        s_sum = sem("s_sum")
        s_acc = sem("s_acc")
        s_ls = sem("s_ls")
        s_lt = sem("s_lt")
        s_lts = sem("s_lts")
        s_ed = sem("s_ed")
        s_edd = sem("s_edd")
        s_edl = sem("s_edl")
        s_ca = sem("s_ca")
        s_cad = sem("s_cad")
        s_cal = sem("s_cal")
        s_mx = sem("s_mx")
        s_mt = sem("s_mt")
        s_sh = sem("s_sh")
        s_ex = sem("s_ex")
        s_both = sem("s_both")
        s_den = sem("s_den")
        s_agg = sem("s_agg")
        s_o = sem("s_o")
        s_emb = sem("s_emb")
        s_c1 = sem("s_c1")
        s_m1 = sem("s_m1")
        s_xb = sem("s_xb")
        s_c1x = sem("s_c1x")
        s_mm = sem("s_mm")
        s_sq = sem("s_sq")
        s_root = sem("s_root")
        s_nm = sem("s_nm")
        s_fin = sem("s_fin")
        s_out = sem("s_out")

        def fours(eng, stages):
            def step(i, s):
                for lag, fn in stages:
                    ii, ss = i + (s - lag) // SLOTS, (s - lag) % SLOTS
                    if isinstance(i, int) and not 0 <= ii * SLOTS + ss < NG:
                        continue
                    fn(ii, ss, ii * SLOTS + ss)
            lead = min(0, min(lag for lag, _ in stages))
            for n in range(lead, 0):
                step(n // SLOTS, n % SLOTS)
            for s in range(SLOTS):
                step(0, s)
            with eng.Fori(1, TI - 1) as i:
                for s in range(SLOTS):
                    step(i, s)
            for n in range((TI - 1) * SLOTS, NG + max(lag for lag, _ in stages)):
                step(n // SLOTS, n % SLOTS)

        def load_weights(sp):
            def w(dst_ap, src_ap):
                sp.dma_start(dst_ap, src_ap).then_inc(s_w, 16)
                wcount[0] += 16
            rowv = lambda a: a.rearrange("(o n) -> o n", o=1)
            col = lambda a: a.rearrange("(n o) -> n o", o=1)
            for n, (m, v) in enumerate(((wq, bq), (wk, bk), (wv, bv))):
                w(W0[0:D0, n * D0:(n + 1) * D0], m)
                w(W0[D0:D0 + 1, n * D0:(n + 1) * D0], rowv(v))
            w(Wo[0:D0, :], wo)
            w(Wo[D0:D0 + 1, :], rowv(bo))
            w(Wp[:, :], wp)
            w(shift[:, 0:1], col(wpb))
            w(shift[:, 1:2], wpos.rearrange("o n -> n o"))
            for l in range(LAYERS):
                for n, m in enumerate((qT, kT, vT)):
                    w(W1[:, l, n, :], m[l])
                w(lns[:, l:l + 1], col(ln_scale[l]))
                w(lnb[:, l:l + 1], col(ln_bias[l]))
            w(invw[:, :], inv_w)
            w(invb[:, :], inv_b.partition_broadcast(P))
        wcount = [0]

        def zeros_gpsimd(gp):
            nc.gpsimd.memset(xs[:, NB - 1:NB, :], 0.0).then_inc(s_zero, 1)
            nc.gpsimd.memset(avg[:, :], 1.0 / DM)
            nc.gpsimd.memset(eps[:, :], 1e-6).then_inc(s_zero, 1)

        def load_x(sp):
            sp.wait_ge(s_zero, 1)
            full = (NB - 1) * P
            sp.dma_start(xs[:, 0:NB - 1, :], x[0:full].rearrange("(b p) c -> p b c", p=P)).then_inc(s_x, 16)
            sp.dma_start(xs[0:N - full, NB - 1, :], x[full:N]).then_inc(s_x, 16)

        def hT_borders():
            nc.vector.memset(hT[0:D0, NPAD:NWIN], 0.0)
            vstep(nc.vector.memset(hT[D0:D0 + 1, :], 1.0))

        def norm_vector(dve, n):
            if n == 0:
                hT_borders()
            vstep(nc.vector.tensor_reduce(mean[:, :], xs[:, :, :], AX.X, ALU.add))
            vstep(nc.vector.tensor_scalar(mean[:, :], mean[:, :], 1.0 / D0, None, ALU.mult))
            vstep(nc.vector.tensor_tensor(hs[:, :, :], xs[:, :, :],
                                          mean[:, :].unsqueeze(2).to_broadcast([P, NB, D0]), ALU.subtract))
            vstep(nc.vector.tensor_tensor(sq[:, :, :], hs[:, :, :], hs[:, :, :], ALU.mult))
            vstep(nc.vector.tensor_reduce(var[:, :], sq[:, :, :], AX.X, ALU.add))
            nc.vector.tensor_scalar(var[:, :], var[:, :], 1.0 / D0, 1e-5, ALU.mult, ALU.add).then_inc(s_var, 1)
            dve.wait_ge(s_std, n + 1)
            vstep(nc.vector.reciprocal(var[:, :], var[:, :]))
            vstep(nc.vector.tensor_tensor(hs[:, :, :], hs[:, :, :],
                                          var[:, :].unsqueeze(2).to_broadcast([P, NB, D0]), ALU.mult))
            nc.vector.tensor_scalar(hs[:, :, :], hs[:, :, :], 0.0, None, ALU.max).then_inc(s_hn, 1)

        TR = -(-NB // 4)

        def norm_scalar(act, n):
            act.wait_ge(s_var, n + 1)
            nc.scalar.activation(var[:, :], var[:, :], ACT.Sqrt).then_inc(s_std, 1)
            for g in range(TR):
                blocks = min(4, NB - g * 4)
                act.wait_ge(s_tp, n * TR + g + 1)
                nc.scalar.copy(hT[0:D0, g * 512:g * 512 + blocks * P],
                               banks[g][0:D0, 0:blocks * P]).then_inc(s_ts, 1)

        def norm_tensor(pe, n):
            pe.wait_ge(s_hn, n + 1)
            for g in range(TR):
                for b in range(g * 4, min(g * 4 + 4, NB)):
                    done = nc.tensor.transpose(banks[g][0:D0, (b % 4) * P:(b % 4 + 1) * P], hs[:, b, :],
                                               ident[:, :])
                done.then_inc(s_tp, 1)
            pe.wait_ge(s_ts, (n + 1) * TR)

        NT = NB + 1

        def project_tensor(pe, n, lhs, rhs, cols):
            for b in range(NT):
                m = n * NT + b
                since(pe, s_pjs, m - 3)
                nc.tensor.matmul(banks[b % 4][:, 0:cols], lhs[:, b * P:(b + 1) * P], rhs, start=True,
                                 stop=True).then_inc(s_pj, 1)

        def project_scalar(act, n, stage, cols):
            for b in range(NT):
                act.wait_ge(s_pj, n * NT + b + 1)
                nc.scalar.copy(stage[:, b, :], banks[b % 4][:, 0:cols]).then_inc(s_pjs, 1)

        def tables_sync(sp, n, stage, width, q_d, kv_d):
            sp.wait_ge(s_pjs, (n + 1) * NT)
            sp.dma_start(q_d.rearrange("(b p) c -> p b c", p=P), stage[:, :, 0:width]).then_inc(s_tab, 16)
            sp.dma_start(kv_d.rearrange("(b p) c -> p b c", p=P),
                         stage[:, 0:NB, width:3 * width]).then_inc(s_tab, 16)

        def windows_sync(sp, n, k, q_d, width):
            sp.wait_ge(s_tab, 32 * (n + 1))
            sp.wait_ge(s_basel[k], 32)

            def load(i, s, g):
                since(sp, s_qe, g + (n * NG - SLOTS + 1))
                _, bases = nc.values_load_multi_w_load_instructions(
                    base_i[k][0:1, ds(g * TG, TG)], min_val=0, max_val=N - 1, engines=[mybir.EngineType.SP])
                for j in range(TG):
                    sp.dma_start(qw[:, s, j, 0:width], q_d[ds(bases[j], P), :]).then_inc(s_qw[s], 16)

            fours(sp, [(0, load)])

        def gather_gpsimd(gp, n, kv_d, width):
            gp.wait_ge(s_tab, 32 * (n + 1))

            def gather(i, s, g):
                gp.wait_ge(s_ix, g + (n * NG + 1))
                since(gp, s_prod, g + (n * NG - SLOTS + 1))
                since(gp, s_vw if n else s_vc, g + (n * NG - SLOTS + 1))
                gp.sem_inc(s_turn, 1)
                for j in range(TG):
                    gp.indirect_dma_start(
                        out=kv[:, s, j, 0:2 * width], out_offset=None, in_=kv_d,
                        in_offset=bass.IndirectOffsetOnAxis(ap=idxs[:, s, j:j + 1], axis=0)
                    ).then_inc(s_kv[s], 16)

            fours(gp, [(0, gather)])

        def rows(n, i):
            return i * (16 * TG) + (n * TI + 1) * 16 * TG

        def stage_indices(act, n, k):
            def fn(i, s, g):
                since(act, s_kv[s], rows(n, i) - 16 * TG)
                nc.scalar.copy(idxs[:, s, :], idx[k][:, ds(g * TG, TG)]).then_inc(s_ix, 1)
            return fn

        def copy_transposed(act, n):
            def fn(i, s, g):
                act.wait_ge(s_rt, g + (n * NG + 1))
                since(act, s_qe, g + (n * NG - 1))
                nc.scalar.copy(RT[:, s % 2, :], banks[s % 2][:, :]).then_inc(s_rts, 1)
            return fn

        def keep_values(act):
            def fn(i, s, g):
                act.wait_ge(s_kv[s], rows(0, i))
                nc.scalar.copy(values[:, ds(g * TG, TG), :], kv[:, s, :, 0:2 * D0][:, :, D0:2 * D0]
                               ).then_inc(s_vc, 1)
            return fn

        def one_hot(dve, n, k, ring):
            def fn(i, s, g):
                ring(i, s, g)
                nc.vector.tensor_tensor(R[:, s, :, :], iota[:, :].unsqueeze(1).to_broadcast([P, TG, P]),
                                        seg[k][:, ds(g * TG, TG)].unsqueeze(2).to_broadcast([P, TG, P]),
                                        ALU.is_equal).then_inc(s_R, 1)
            return fn

        def one_hot_scalar(act, nR, k, ring):
            def distance(i, s, g):
                ring(i, s, g)
                for j in range(TG):
                    done = nc.scalar.activation(R[:, s, j, :], iota[:, :], ACT.Abs, scale=-1.0,
                                                bias=seg[k][:, ds(g * TG + j, 1)])
                done.then_inc(s_dist, 1)

            def at_zero(i, s, g):
                act.wait_ge(s_dist, g + ((nR - 1) * NG + 1))
                nc.scalar.activation(R[:, s, :, :], R[:, s, :, :], ACT.Relu, scale=-1.0,
                                     bias=ones[:, 0:1]).then_inc(s_R, 1)
            return distance, at_zero

        def transposes(pe, n, nR):
            def fn(i, s, g):
                pe.wait_ge(s_R, g + (nR * NG + 1))
                since(pe, s_rts, g + (n * NG - 1))
                for j in range(TG):
                    done = nc.tensor.transpose(banks[s % 2][:, j * P:(j + 1) * P], R[:, s, j, :], ident[:, :])
                done.then_inc(s_rt, 1)
            return fn

        def expand(pe, n, width):
            def fn(i, s, g):
                pe.wait_ge(s_rts, g + (n * NG + 1))
                pe.wait_ge(s_qw[s], rows(n, i))
                since(pe, s_prod, g + (n * NG - 1))
                for j in range(TG):
                    done = nc.tensor.matmul(banks[2 + s % 2][:, j * width:(j + 1) * width],
                                            RT[:, s % 2, j * P:(j + 1) * P], qw[:, s, j, 0:width],
                                            start=True, stop=True)
                done.then_inc(s_qe, 1)
            return fn

        def logits(dve, n, width, heads):
            def times(i, s, g):
                dve.wait_ge(s_kv[s], rows(n, i))
                dve.wait_ge(s_qe, g + (n * NG + 1))
                since(dve, s_red, g + (n * NG - 1))
                nc.vector.tensor_tensor(prod[:, s % 2, :, 0:width], kv[:, s, :, 0:width],
                                        banks[2 + s % 2][:, 0:TG * width].rearrange("p (j c) -> p j c", j=TG),
                                        ALU.mult).then_inc(s_prod, 1)

            def total(i, s, g):
                dve.wait_ge(s_prod, g + (n * NG + 1))
                since(dve, s_lg, g + (n * NG - 1))
                nc.vector.tensor_reduce(red[:, s % 2, 0:TG * heads].rearrange("p (j h) -> p j h", j=TG),
                                        prod[:, s % 2, :, 0:width].rearrange("p j (h d) -> p j h d", h=heads),
                                        AX.X, ALU.add).then_inc(s_red, 1)
            return times, total

        def a_vector(dve):
            times, total = logits(dve, 0, D0, H0)

            def bias(i, s, g):
                dve.wait_ge(s_red, g + 1)
                at = S[0][:, ds(g * TG, TG), 2:2 + H0]
                nc.vector.scalar_tensor_tensor(
                    at, red[:, s % 2, :].rearrange("p (j h) -> p j h", j=TG), (D0 // H0) ** -0.5, at,
                    ALU.mult, ALU.add).then_inc(s_lg, 1)

            def ring(i, s, g):
                since(dve, s_rt, g - SLOTS + 1)

            fours(dve, [(0, one_hot(dve, 0, 0, ring)), (1, times), (1, total), (1, bias)])

        def max_tensor(pe):
            pe.wait_ge(s_lg, NG)
            for g in range(EB // 4):
                pe.wait_ge(s_ls, g + 1)
                since(pe, s_lts, g - 3)
                for b in range(4):
                    done = nc.tensor.transpose(banks[4 + g % 4][:, b * P:(b + 1) * P],
                                               RT[:, g % 2, b * P:(b + 1) * P], ident[:, :])
                done.then_inc(s_lt, 1)
            pe.wait_ge(s_mx, 4)
            for g in range(EB // 4):
                since(pe, s_sh, g - 3)
                for b in range(4):
                    c = (g * 4 + b) * P
                    done = nc.tensor.transpose(banks[4 + g % 4][:, b * P:(b + 1) * P], LT[:, c:c + P],
                                               ident[:, :])
                done.then_inc(s_mt, 1)

        def max_scalar(act):
            act.wait_ge(s_lg, NG)
            act.wait_ge(s_qe, NG)
            for g in range(EB // 4):
                t = g * 4 * (P // H0)
                since(act, s_lt, g - 1)
                nc.scalar.copy(RT[:, g % 2, :].rearrange("p (t h) -> p t h", h=H0),
                               S[0][:, t:t + 4 * (P // H0), 2:2 + H0]).then_inc(s_ls, 1)
                act.wait_ge(s_lt, g + 1)
                nc.scalar.copy(LT[:, g * 512:(g + 1) * 512], banks[4 + g % 4][:, :]).then_inc(s_lts, 1)
            act.wait_ge(s_sh, EB // 4)
            at = S[0][:, :, 2:2 + H0]
            nc.scalar.activation(at, at, ACT.Exp).then_inc(s_ex, 1)

        def scans(c):
            x = LT[:, c * EH * P:(c + 1) * EH * P]
            pos = lambda ap: ap.rearrange("p (b e) -> p b e", e=P)
            vstep(nc.vector.tensor_scalar(gate, x, FLOOR, 2 * BIG, ALU.is_gt, ALU.mult))
            vstep(nc.vector.tensor_scalar(gate, gate, -BIG, None, ALU.add))
            vstep(nc.vector.tensor_copy(gate2, gate))
            nc.vector.memset(pos(gate)[:, :, 0:1], -BIG)
            vstep(nc.vector.memset(pos(gate2)[:, :, P - 1:P], -BIG))
            nc.vector.tensor_tensor_scan(fwd, gate, x, -BIG, ALU.min, ALU.max)
            vstep(nc.vector.tensor_tensor_scan(bwd[:, ::-1], gate2[:, ::-1], x[:, ::-1], -BIG,
                                               ALU.min, ALU.max))
            return x, pos

        def max_vector(dve):
            dve.wait_ge(s_lts, EB // 4)
            for c in range(4):
                x, pos = scans(c)
                blocks = slice(c * EH, (c + 1) * EH)
                nc.vector.tensor_copy(ends_f[:, 0, blocks], pos(fwd)[:, :, P - 1])
                nc.vector.tensor_copy(ends_f[:, 1, blocks], pos(bwd)[:, :, 0])
                vstep(nc.vector.tensor_reduce(ends_f[:, 2, blocks], pos(x), AX.X, ALU.min))
            vstep(nc.vector.tensor_scalar(ends_f[:, 2, :], ends_f[:, 2, :], FLOOR, 2 * BIG, ALU.is_gt,
                                          ALU.mult))
            nc.vector.tensor_scalar(ends_f[:, 2, :], ends_f[:, 2, :], -BIG, None, ALU.add).then_inc(s_ed, 1)
            dve.wait_ge(s_edl, 48)
            nc.vector.memset(chain[:, 3, 0:1], -BIG)
            nc.vector.memset(chain[:, 4, T - 1:T], -BIG)
            vstep(nc.vector.tensor_tensor_scan(chain[:, 3, 1:T], chain[:, 2, 0:T - 1], chain[:, 0, 0:T - 1],
                                               -BIG, ALU.min, ALU.max))
            nc.vector.tensor_tensor_scan(chain[:, 4, T - 2::-1], chain[:, 2, T - 1:0:-1],
                                         chain[:, 1, T - 1:0:-1], -BIG, ALU.min, ALU.max).then_inc(s_ca, 1)
            dve.wait_ge(s_cal, 32)
            for c in range(4):
                x = LT[:, c * EH * P:(c + 1) * EH * P].rearrange("p (b e) -> p b e", e=P)
                blocks = slice(c * EH, (c + 1) * EH)
                for n, e in enumerate((0, P - 1)):
                    g1 = red[:, n, 0:EH]
                    vstep(nc.vector.tensor_scalar(g1, x[:, :, e], FLOOR, 2 * BIG, ALU.is_gt, ALU.mult))
                    vstep(nc.vector.scalar_tensor_tensor(g1, g1, -BIG, carries[:, n, blocks], ALU.add,
                                                         ALU.min))
                    vstep(nc.vector.tensor_tensor(x[:, :, e], x[:, :, e], g1, ALU.max))
                xq, pos = scans(c)
                nc.vector.scalar_tensor_tensor(xq, fwd, FLOOR, bwd, ALU.max, ALU.max).then_inc(s_mx, 1)
                dve.wait_ge(s_mx, c + 1)
            for g in range(EB // 4):
                t = g * 4 * (P // H0)
                at = S[0][:, t:t + 4 * (P // H0), 2:2 + H0]
                dve.wait_ge(s_mt, g + 1)
                nc.vector.tensor_tensor(at, at, banks[4 + g % 4][:, :].rearrange("p (t h) -> p t h", h=H0),
                                        ALU.subtract).then_inc(s_sh, 1)

        def max_sync(sp):
            sp.wait_ge(s_ed, 1)
            for n in range(3):
                sp.dma_start(edge_d[n].rearrange("(b p) -> p b", p=P), ends_f[:, n, :],
                             allow_slow_non_contiguous=True).then_inc(s_edd, 16)
            sp.wait_ge(s_edd, 48)
            for n in range(3):
                sp.dma_start(chain[:, n, :], edge_d[n].rearrange("(t h) -> h t", h=H0),
                             allow_slow_non_contiguous=True).then_inc(s_edl, 16)
            sp.wait_ge(s_ca, 1)
            for n in range(2):
                sp.dma_start(carry_d[n].rearrange("(t h) -> h t", h=H0), chain[:, 3 + n, :],
                             allow_slow_non_contiguous=True).then_inc(s_cad, 16)
            sp.wait_ge(s_cad, 32)
            for n in range(2):
                sp.dma_start(carries[:, n, :], carry_d[n].rearrange("(b p) -> p b", p=P),
                             allow_slow_non_contiguous=True).then_inc(s_cal, 16)

        def add_sums(dve, m, k, acc, bank, apart):
            bases = [None] * TG

            def load(*tiles):
                def fn(i, s, g):
                    _, bases[tiles[0]:tiles[-1] + 1] = nc.values_load_multi_w_load_instructions(
                        base_i[k][0:1, ds(g * TG + tiles[0], len(tiles))], min_val=0, max_val=N - 1,
                        engines=[mybir.EngineType.DVE])
                return fn

            def fn(i, s, g):
                dve.wait_ge(s_sum, g + (m * NG + 1))
                for j in range(TG):
                    to, add = acc(bases[j], j), bank(s, j)
                    since(dve, s_acc, g * TG + (m * T + j + 1 - apart))
                    nc.vector.tensor_tensor(to, to, add, ALU.add).then_inc(s_acc, 1)
            return load, fn

        def b_vector(dve):
            dve.wait_ge(s_ex, 1)
            nc.vector.memset(odd0, 0.0)
            vstep(nc.vector.memset(acc0[:, :], 0.0))

            def weigh(i, s, g):
                since(dve, s_sum, g - 1)
                w = S[0][:, ds(g * TG, TG), 2:2 + H0].unsqueeze(3)
                nc.vector.tensor_tensor(
                    vw[:, s % 2, :, 0:D0].rearrange("p j (h d) -> p j h d", h=H0),
                    values[:, ds(g * TG, TG), :].rearrange("p j (h d) -> p j h d", h=H0),
                    w.to_broadcast([P, TG, H0, D0 // H0]), ALU.mult).then_inc(s_vw, 1)

            load, sums = add_sums(dve, 0, 0, lambda base, j: (acc0, odd0)[j % 2][:, ds(base, P)],
                                  lambda s, j: banks[4 + s % 2][:, j * P:(j + 1) * P], 2)
            fours(dve, [(0, weigh), (1, load(0, 1, 2, 3)), (1, sums)])
            dve.wait_ge(s_acc, T)
            nc.vector.tensor_tensor(acc0[:, :], acc0[:, :], odd0, ALU.add).then_inc(s_both, 1)

        def b_scalar(act):
            def beside(i, s, g):
                since(act, s_sum, g - 1)
                w = S[0][:, ds(g * TG, TG), 2:2 + H0].unsqueeze(3)
                nc.scalar.copy(vw[:, s % 2, :, D0:2 * D0].rearrange("p j (h d) -> p j h d", h=H0),
                               w.to_broadcast([P, TG, H0, D0 // H0])).then_inc(s_wb, 1)

            def ring(i, s, g):
                since(act, s_sum, g - SLOTS + 1)

            act.wait_ge(s_ex, 1)
            distance, at_zero = one_hot_scalar(act, 1, 0, ring)
            fours(act, [(-2, distance), (-1, at_zero), (0, beside)])

        def b_tensor(pe):
            def fn(i, s, g):
                pe.wait_ge(s_R, g + (NG + 1))
                pe.wait_ge(s_vw, g + 1)
                pe.wait_ge(s_wb, g + 1)
                since(pe, s_acc, (g - 1) * TG)
                for j in range(TG):
                    done = nc.tensor.matmul(banks[4 + s % 2][:, j * P:(j + 1) * P], vw[:, s % 2, j, :],
                                            R[:, s, j, :], start=True, stop=True)
                done.then_inc(s_sum, 1)

            fours(pe, [(0, fn)])

        def out0_sync(sp):
            sp.wait_ge(s_both, 1)
            sp.dma_start(den0[:, :], acc0[D0:2 * D0, :]).then_inc(s_den, 16)

        def out0_vector(dve):
            hT_borders()
            dve.wait_ge(s_den, 16)
            vstep(nc.vector.tensor_scalar(den0[:, :], den0[:, :], 1e-16, None, ALU.add))
            vstep(nc.vector.reciprocal(den0[:, :], den0[:, :]))
            nc.vector.tensor_tensor(hT[0:D0, 0:NPAD], acc0[0:D0, 0:NPAD], den0[:, 0:NPAD],
                                    ALU.mult).then_inc(s_agg, 1)
            for g in range(4):
                lo, hi = g * 7, min(g * 7 + 7, NB)
                dve.wait_ge(s_o, g + 1)
                vstep(nc.vector.tensor_tensor(
                    xs[:, lo:hi, :], xs[:, lo:hi, :],
                    banks[g][:, 0:(hi - lo) * D0].rearrange("p (b c) -> p b c", c=D0), ALU.add))

        def out_tensor(pe, lhs, rhs):
            for g in range(4):
                for b in range(g * 7, min(g * 7 + 7, NB)):
                    done = nc.tensor.matmul(banks[g][:, (b % 7) * D0:(b % 7 + 1) * D0],
                                            lhs[:, b * P:(b + 1) * P], rhs, start=True, stop=True)
                done.then_inc(s_o, 1)

        def embed_tensor(pe):
            for c, (lo, w) in enumerate(CHUNKS):
                nc.tensor.matmul(banks[c][:, 0:w], Wp[:, :], hT[0:D0, lo:lo + w], start=True,
                                 stop=True).then_inc(s_c1, 1)

        def embed_scalar(act):
            for c, (lo, w) in enumerate(CHUNKS):
                act.wait_ge(s_c1, c + 1)
                nc.scalar.activation(emb[:, lo:lo + w], banks[c][:, 0:w], ACT.Identity,
                                     bias=shift[:, 0:1]).then_inc(s_emb, 1)

        def c_vector(dve, l):
            n = l + 1
            times, total = logits(dve, n, DM, H1)

            def clip(i, s, g):
                dve.wait_ge(s_red, g + (n * NG + 1))
                since(dve, s_wt, g + (l * NG - 1))
                nc.vector.tensor_scalar(red[:, s % 2, 0:TG * H1], red[:, s % 2, 0:TG * H1], -10.0, 10.0,
                                        ALU.max, ALU.min).then_inc(s_lg, 1)

            def weigh(i, s, g):
                dve.wait_ge(s_vc, g + (n * NG + 1))
                since(dve, s_sum, g + (n * NG - 1))
                nc.vector.scalar_tensor_tensor(
                    wts[:, s % 2, :].rearrange("p (j h) -> p j h", j=TG),
                    seg[1][:, ds(g * TG, TG)].unsqueeze(2).to_broadcast([P, TG, H1]), 0.0,
                    red[:, s % 2, 0:TG * H1].rearrange("p (j h) -> p j h", j=TG),
                    ALU.is_ge, ALU.mult).then_inc(s_wt, 1)
                dve.wait_ge(s_wt, g + (l * NG + 1))
                nc.vector.tensor_tensor(
                    vw[:, s % 2, :, :].rearrange("p j (h d) -> p j h d", h=H1),
                    kv[:, s, :, DM:2 * DM].rearrange("p j (h d) -> p j h d", h=H1),
                    wts[:, s % 2, :].rearrange("p (j h) -> p j h", j=TG).unsqueeze(3)
                    .to_broadcast([P, TG, H1, DM // H1]),
                    ALU.mult).then_inc(s_vw, 1)

            load, sums = add_sums(dve, n, 1, lambda base, j: (acc1, odd1)[j % 2][:, :, ds(base, P)],
                            lambda s, j: banks[4 + 2 * (s % 2) + j // 2][:, (j % 2) * 2 * P:(j % 2 + 1) * 2 * P]
                            .rearrange("p (a m) -> p a m", a=2), 2)
            dve.wait_ge(s_tab, 32 * (n + 1))
            nc.vector.memset(odd1[:, :, :], 0.0)
            nc.vector.memset(acc1[:, :, :], 0.0).then_inc(s_m1, 1)
            dve.wait_ge(s_m1, l + 1)
            fours(dve, [(2, weigh), (1, times), (3, load(0, 1, 2, 3)), (1, total), (1, clip), (3, sums)])

        def c_scalar(act, l):
            n = l + 1

            def exp(i, s, g):
                act.wait_ge(s_lg, g + (n * NG + 1))
                nc.scalar.activation(red[:, s % 2, 0:TG * H1], red[:, s % 2, 0:TG * H1],
                                     ACT.Exp).then_inc(s_vc, 1)

            def beside(i, s, g):
                act.wait_ge(s_wt, g + (l * NG + 1))
                since(act, s_sum, g + (n * NG - 1))
                nc.scalar.copy(wx[:, s % 2, :, :].rearrange("p j (h d) -> p (j h) d", h=H1),
                               wts[:, s % 2, :].unsqueeze(2).to_broadcast([P, TG * H1, DM // H1])
                               ).then_inc(s_wb, 1)

            def ring(i, s, g):
                since(act, s_sum, g + (n * NG - SLOTS + 1))

            distance, at_zero = one_hot_scalar(act, n + 1, 1, ring)
            fours(act, [(2, beside), (0, copy_transposed(act, n)), (-1, distance), (-3, stage_indices(act, n, 1)), (1, exp), (-1, at_zero)])

        def c_tensor(pe, l):
            n = l + 1

            def sums(i, s, g):
                pe.wait_ge(s_vw, g + (n * NG + 1))
                pe.wait_ge(s_wb, g + (n * NG + 1))
                since(pe, s_acc, g * TG + (n * T - TG))
                for j in range(TG):
                    to = banks[4 + 2 * (s % 2) + j // 2]
                    at = (j % 2) * 2 * P
                    nc.tensor.matmul(to[:, at:at + P], vw[:, s % 2, j, :], R[:, s, j, :], start=True,
                                     stop=True)
                    done = nc.tensor.matmul(
                        to[:, at + P:at + 2 * P], wx[:, s % 2, j, :], R[:, s, j, :], start=True, stop=True)
                done.then_inc(s_sum, 1)

            fours(pe, [(1, expand(pe, n, DM)), (0, transposes(pe, n, n + 1)), (2, sums)])

        def post_vector(dve, l):
            num, den = acc1[:, 0, :], acc1[:, 1, :]
            dve.wait_ge(s_acc, T * (l + 2))
            vstep(nc.vector.tensor_tensor(acc1[:, :, :], acc1[:, :, :], odd1[:, :, :], ALU.add))
            vstep(nc.vector.tensor_scalar(den, den, 1e-8, None, ALU.add))
            vstep(nc.vector.reciprocal(den, den))
            vstep(nc.vector.tensor_tensor(num, num, den, ALU.mult))
            nc.vector.tensor_tensor(num, num, emb[:, :], ALU.add).then_inc(s_c1x, 1)
            C = len(CHUNKS)
            for c, (lo, w) in enumerate(CHUNKS):
                dve.wait_ge(s_mm, 2 * C * l + c + 1)
                vstep(nc.vector.tensor_tensor(cent[:, lo:lo + w], num[:, lo:lo + w], banks[c][:, 0:w],
                                              ALU.subtract))
                nc.vector.tensor_tensor(work1[:, lo:lo + w], cent[:, lo:lo + w], cent[:, lo:lo + w],
                                        ALU.mult).then_inc(s_sq, 1)
            dve.wait_ge(s_root, (l + 1) * C)
            vstep(nc.vector.reciprocal(work1[:, :], work1[:, :]))
            nc.vector.tensor_tensor(cent[:, :], cent[:, :], work1[:, :], ALU.mult).then_inc(s_nm, 1)

        def post_tensor(pe, l):
            C = len(CHUNKS)
            pe.wait_ge(s_c1x, l + 1)
            for c, (lo, w) in enumerate(CHUNKS):
                nc.tensor.matmul(banks[c][:, 0:w], avg[:, :], acc1[:, 0, lo:lo + w], start=True,
                                 stop=True).then_inc(s_mm, 1)
            for c, (lo, w) in enumerate(CHUNKS):
                pe.wait_ge(s_sq, l * C + c + 1)
                nc.tensor.matmul(banks[c][:, 0:w], avg[:, :], work1[:, lo:lo + w], start=True,
                                 stop=True).then_inc(s_mm, 1)

        def post_scalar(act, l):
            C = len(CHUNKS)
            for c, (lo, w) in enumerate(CHUNKS):
                act.wait_ge(s_mm, 2 * C * l + C + c + 1)
                nc.scalar.activation(work1[:, lo:lo + w], banks[c][:, 0:w], ACT.Sqrt,
                                     bias=eps[:, 0:1]).then_inc(s_root, 1)
            act.wait_ge(s_nm, l + 1)
            nc.scalar.activation(emb[:, :], cent[:, :], ACT.Identity, bias=lnb[:, l:l + 1],
                                 scale=lns[:, l:l + 1]).then_inc(s_emb, 1)

        block = ctx.enter_context(nc.Block())
        EMB = len(CHUNKS)

        @block.sync
        def _(sp):
            loads_sync(sp)
            load_x(sp)
            load_weights(sp)
            sort_sync(sp)
            tables_sync(sp, 0, stage0, D0, q0_d, kv0_d)
            windows_sync(sp, 0, 0, q0_d, D0)
            max_sync(sp)
            out0_sync(sp)
            for l in range(LAYERS):
                tables_sync(sp, l + 1, stage1, DM, q1_d[l], kv1_d[l])
                windows_sync(sp, l + 1, 1, q1_d[l], DM)
            full = (NB - 1) * P
            sp.wait_ge(s_fin, 4)
            sp.dma_start(out[0:full].rearrange("(b p) c -> p b c", p=P), xs[:, 0:NB - 1, :]).then_inc(s_out, 16)
            sp.dma_start(out[full:N], xs[0:N - full, NB - 1, :]).then_inc(s_out, 16)
            sp.wait_ge(s_out, 32)

        @block.gpsimd
        def _(gp):
            constants_gpsimd(gp)
            zeros_gpsimd(gp)
            sort_gpsimd(gp)
            gather_gpsimd(gp, 0, kv0_d, D0)
            for l in range(LAYERS):
                gather_gpsimd(gp, l + 1, kv1_d[l], DM)

        @block.vector
        def _(dve):
            constants_vector(dve)
            sort_vector(dve)
            dve.wait_ge(s_seg, 2)
            dve.wait_ge(s_x, 32)
            norm_vector(dve, 0)
            a_vector(dve)
            max_vector(dve)
            b_vector(dve)
            out0_vector(dve)
            norm_vector(dve, 1)
            dve.wait_ge(s_w, wcount[0])
            vstep(nc.vector.tensor_tensor(shift[:, 0:1], shift[:, 0:1], shift[:, 1:2], ALU.add))
            nc.vector.tensor_tensor(xs[:, :, :], xs[:, :, :], invb[:, :].unsqueeze(1).to_broadcast([P, NB, D0]),
                                    ALU.add).then_inc(s_xb, 1)
            for l in range(LAYERS):
                dve.wait_ge(s_emb, EMB + l)
                c_vector(dve, l)
                post_vector(dve, l)
            dve.wait_ge(s_xb, 1)
            for g in range(4):
                lo, hi = g * 7, min(g * 7 + 7, NB)
                dve.wait_ge(s_o, g + 5)
                nc.vector.tensor_tensor(xs[:, lo:hi, :], xs[:, lo:hi, :],
                                        banks[g][:, 0:(hi - lo) * D0].rearrange("p (b c) -> p b c", c=D0),
                                        ALU.add).then_inc(s_fin, 1)

        @block.scalar
        def _(act):
            sort_scalar(act)
            norm_scalar(act, 0)
            act.wait_ge(s_fill, 32)
            project_scalar(act, 0, stage0, 3 * D0)
            act.wait_ge(s_seg, 2)
            act.wait_ge(s_tab, 32)
            fours(act, [(-3, stage_indices(act, 0, 0)), (0, copy_transposed(act, 0)), (1, keep_values(act))])
            max_scalar(act)
            b_scalar(act)
            norm_scalar(act, 1)
            act.wait_ge(s_xb, 1)
            embed_scalar(act)
            for l in range(LAYERS):
                project_scalar(act, l + 1, stage1, 3 * DM)
                c_scalar(act, l)
                post_scalar(act, l)

        @block.tensor
        def _(pe):
            sort_tensor(pe)
            norm_tensor(pe, 0)
            pe.wait_ge(s_w, wcount[0])
            pe.wait_ge(s_zero, 2)
            project_tensor(pe, 0, hT, W0[:, :], 3 * D0)
            pe.wait_ge(s_pjs, NT)
            fours(pe, [(0, transposes(pe, 0, 0)), (0, expand(pe, 0, D0))])
            max_tensor(pe)
            b_tensor(pe)
            pe.wait_ge(s_agg, 1)
            out_tensor(pe, hT, Wo[:, :])
            norm_tensor(pe, 1)
            embed_tensor(pe)
            for l in range(LAYERS):
                pe.wait_ge(s_emb, EMB + l)
                project_tensor(pe, l + 1, emb, W1[:, l, :, :].rearrange("p a n -> p (a n)"), 3 * DM)
                pe.wait_ge(s_pjs, (l + 2) * NT)
                c_tensor(pe, l)
                post_tensor(pe, l)
            pe.wait_ge(s_emb, EMB + LAYERS)
            out_tensor(pe, emb, invw[:, :])


_INS = ['x', 'src', 'dst', 'edge_attr_8', 'L0_gnn_Wq', 'L0_gnn_bq', 'L0_gnn_Wk', 'L0_gnn_bk', 'L0_gnn_Wv',
        'L0_gnn_bv', 'L0_gnn_Wo', 'L0_gnn_bo', 'L1_gnn_W_P_w', 'L1_gnn_W_P_b', 'L1_gnn_W_pos',
        'L1_gnn_qT', 'L1_gnn_kT', 'L1_gnn_vT', 'L1_gnn_ln_scale', 'L1_gnn_ln_bias', 'L1_gnn_inv_w',
        'L1_gnn_inv_b']


def kernel(**inputs):
    import numpy as _np
    import concourse.bacc as _bacc
    from concourse import mybir as _mybir
    from concourse.bass_utils import run_bass_kernel_spmd as _run

    nc = _bacc.Bacc("TRN2", target_bir_lowering=False, num_devices=1)
    arrays, args = {}, []
    for name in _INS:
        a = _np.ascontiguousarray(inputs[name])
        arrays[f"in_{name}_dram"] = a
        args.append(nc.dram_tensor(f"in_{name}_dram", a.shape, _mybir.dt.from_np(a.dtype), kind="ExternalInput").ap())
    args.append(nc.dram_tensor("out_0_dram", (N, D0), _mybir.dt.from_np(_np.dtype("float32")),
                               kind="ExternalOutput").ap())
    build(nc, *args)
    r = _run(nc, [arrays], core_ids=[0])
    return r.results[0]["out_0_dram"]
```

```python
from contextlib import ExitStack

import concourse.bass as bass
from concourse import mybir

P = 128
N = 3125
E = 53125
D0, H0 = 64, 8
DM, H1 = 128, 4
LAYERS = 2
EP, ET = 125, 425
EG = 5
NEG = ET // EG
NB = -(-N // P)
NPAD = NB * P
NWIN = NPAD + P
TG = 4
SLOTS = 4
T = 448
NG = T // TG
TI = T // (TG * SLOTS)
HI = 32
WP = [2 + H0, 2]
NONE = -3.0e38
FLOOR = -1.0e30
BIG = 1.0e38
CB = 4
CHUNKS = [(c, min(CB * P, NWIN - c)) for c in range(0, NWIN, CB * P)]
C = len(CHUNKS)
assert NB % CB == 1 and N % P
assert EP * ET == E and T * P >= N + E and T % (TG * SLOTS) == 0 and NEG % 2 == 1


def build(nc, x, src, dst, edge_attr, wq, bq, wk, bk, wv, bv, wo, bo, wp, wpb, wpos, qT, kT, vT,
          ln_scale, ln_bias, inv_w, inv_b, out):
    f32, i32, f16 = mybir.dt.float32, mybir.dt.int32, mybir.dt.float16
    ALU = mybir.AluOpType
    ACT = mybir.ActivationFunctionType
    AX = mybir.AxisListType
    ds = bass.ds

    ctx = ExitStack()
    with ctx:
        def sb(name, shape, dt=f32):
            return ctx.enter_context(nc.sbuf_tensor(name, shape, dt))

        def dram(name, shape, dt=f32):
            return nc.dram_tensor(name, shape, dt, kind="Internal").ap()

        def sem(name):
            return ctx.enter_context(nc.semaphore(name))

        sorted_d = [dram(f"sorted{k}_d", [P * T, WP[k]]) for k in range(2)]
        npos_d = [dram(f"npos{k}_d", [HI * P]) for k in range(2)]
        base_d = [dram(f"base{k}_d", [T]) for k in range(2)]
        basei_d = [dram(f"basei{k}_d", [T], i32) for k in range(2)]
        kv0_d = dram("kv0_d", [NPAD, 2 * D0])
        q0_d = dram("q0_d", [NWIN, D0])
        kv1_d = [dram(f"kv1_{l}_d", [NPAD, 2 * DM]) for l in range(LAYERS)]
        q1_d = [dram(f"q1_{l}_d", [NWIN, DM]) for l in range(LAYERS)]
        edge_d = [dram(f"edge{n}_d", [T * H0]) for n in range(3)]
        carry_d = [dram(f"carry{n}_d", [T * H0]) for n in range(2)]

        ident = sb("ident", [P, P])
        ident16 = sb("ident16", [P, P], f16)
        diff = sb("diff", [P, P])
        below = sb("below", [P, P])
        above = sb("above", [P, P])
        iota = sb("iota", [P, P])
        iota16 = sb("iota16", [P, P], f16)
        ones = sb("ones", [P, P])
        ones16 = sb("ones16", [P, P], f16)
        thr = sb("thr", [T // 4, 4])
        seg = [sb(f"seg{k}", [P, T]) for k in range(2)]
        idx = [sb(f"idx{k}", [P, T], i32) for k in range(2)]
        wx = sb("wx", [P, 2, TG, DM])
        row1 = sb("row1", [EP, 2, EG], i32)
        pay1 = sb("pay1", [EP, 2, EG, WP[1]])
        arena = sb("arena", [P, T * D0])

        def part(start, *shape):
            size = 1
            for n in shape:
                size *= n
            ap = arena[:, start:start + size]
            if len(shape) == 2:
                ap = ap.rearrange("p (a b) -> p a b", a=shape[0])
            return ap

        sort_at = [ET * H0 + T * WP[0] + 2 * N + 2 * T * WP[1] + 11 * ET + 2 * T]

        def sort_part(rows, *shape, dt=f32):
            size = 1
            for n in shape:
                size *= n
            words = size if dt in (f32, i32) else -(-size // 2)
            ap = arena[0:rows, sort_at[0]:sort_at[0] + words]
            sort_at[0] += words + words % 2
            if dt is not f32:
                ap = ap.bitcast(dt)[:, 0:size]
            if len(shape) == 2:
                ap = ap.rearrange("p (a b) -> p a b", a=shape[0])
            if len(shape) == 3:
                ap = ap.rearrange("p (a b c) -> p a b c", a=shape[0], b=shape[1])
            return ap

        attr = arena[0:EP, 0:ET * H0].rearrange("p (t h) -> p t h", h=H0)
        empty = part(ET * H0, T, WP[0])
        npos_bc = part(ET * H0 + T * WP[0], N)
        o = ET * H0 + T * WP[0] + 2 * N + T * WP[1]
        ends_i = part(o, 2, ET).bitcast(i32)[0:EP]
        ends = part(o + 2 * ET, 2, ET)[0:EP]
        digit_i = part(o + 4 * ET, ET).bitcast(i32)[0:EP]
        key1 = [part(o + (5 + k) * ET, ET)[0:EP] for k in range(2)]
        keyc = [part(o + (7 + k) * ET, ET)[0:EP] for k in range(2)]
        khi = [part(o + (9 + k) * ET, ET).bitcast(f16)[0:EP, 0:ET] for k in range(2)]
        klo = [part(o + (9 + k) * ET, ET).bitcast(f16)[0:EP, ET:2 * ET] for k in range(2)]
        base_bc = part(o + 11 * ET, T)
        npos_le = part(ET * H0 + T * WP[0] + N, N)
        empty2 = part(ET * H0 + T * WP[0] + 2 * N, T, WP[1])
        A16 = [sort_part(EP, 2, EG, HI, dt=f16) for _ in range(2)]
        B16 = [sort_part(EP, 2, EG, P, dt=f16) for _ in range(2)]
        AT = [sort_part(HI, 2, EG, EP) for _ in range(2)]
        diag = [sort_part(EP, EG, EP, dt=f16) for _ in range(2)]
        zeros16 = sort_part(EP, P, dt=f16)
        nodes = sort_part(HI, P)
        Hs = [sort_part(HI, 2, P) for _ in range(2)]
        scr = [sort_part(P, 2, 2, P) for _ in range(2)]
        rank = [sort_part(EP, 2, EG) for _ in range(2)]
        first = [sort_part(EP, 2, EG) for _ in range(2)]
        place = [sort_part(EP, 2, EG, dt=i32) for _ in range(2)]
        phi = [sort_part(EP, 2, EG, dt=i32) for _ in range(2)]
        plo = [sort_part(EP, 2, EG, dt=i32) for _ in range(2)]
        rows1 = idx[1][0:EP, 0:ET]
        words1 = wx[:, :, :, :].rearrange("p a b c -> p (a b c)")[0:EP, 0:ET * WP[1]].rearrange(
            "p (t w) -> p t w", w=WP[1])
        row = sort_part(EP, 2, EG, dt=i32)
        pay = sort_part(EP, 2, EG, WP[0])
        nullm = sort_part(HI, P)
        cnt = [sort_part(HI, P) for _ in range(2)]
        incl = [scr[k][0:HI, 0, 0, :] for k in range(2)]
        npos = [sb(f"npos{k}", [HI, P])[:, :] for k in range(2)]
        seed = [sb(f"seed{k}", [HI, P])[:, :] for k in range(2)]
        offs = [sb(f"offs{k}", [HI, 1])[:, :] for k in range(2)]
        basec = [sb(f"basec{k}", [T // 4, 4])[:, :] for k in range(2)]
        basei = [sb(f"basei{k}", [T // 4, 4], i32)[:, :] for k in range(2)]
        base_i = [sb(f"base_i{k}", [1, T], i32) for k in range(2)]
        S = [sb("S0", [P, T, WP[0]]), wx[:, :, :, :].rearrange("p a b c -> p (a b c)")[:, 0:T * WP[1]].rearrange(
            "p (t w) -> p t w", w=WP[1])]

        banks = [ctx.enter_context(nc.psum_tensor(f"bank{n}", [P, 512], f32)) for n in range(8)]

        def sems(name):
            return [sem(f"{name}{k}") for k in range(2)]

        s_const = sem("s_const")
        s_mask = sem("s_mask")
        s_ends = sem("s_ends")
        s_attr = sem("s_attr")
        s_v = sem("s_v")
        s_key = sem("s_key")
        s_oh = sems("s_oh")
        s_ohu = sems("s_ohu")
        s_scan = sems("s_scan")
        s_offs = sems("s_offs")
        s_npos = sems("s_npos")
        s_nposd = sems("s_nposd")
        s_nposb = sems("s_nposb")
        s_seed = sems("s_seed")
        s_base = sems("s_base")
        s_based = sems("s_based")
        s_basel = sems("s_basel")
        s_at = sems("s_at")
        s_ats = sems("s_ats")
        s_diag = sems("s_diag")
        s_bc = sems("s_bc")
        s_rank = sems("s_rank")
        s_look = sems("s_look")
        s_first = sems("s_first")
        s_h = sems("s_h")
        s_hs = sems("s_hs")
        s_pl = sems("s_pl")
        s_dig = sems("s_dig")
        s_row = sems("s_row")
        s_pay = sems("s_pay")
        s_sc = [[sem(f"s_sc{k}{n}") for n in range(2)] for k in range(2)]
        s_pat = sem("s_pat")
        s_fill = sem("s_fill")
        s_S = sems("s_S")
        s_seg = sem("s_seg")
        s_kept = sem("s_kept")
        s_turn = sem("s_turn")

        vcount = [0]

        def vstep(ins):
            vcount[0] += 1
            ins.then_inc(s_v, 1)
            nc.vector.wait_ge(s_v, vcount[0])

        def since(eng, semaphore, value):
            if not isinstance(value, int) or value > 0:
                eng.wait_ge(semaphore, value)

        def in_pairs(eng, body):
            for b in range(2):
                body(b, 0, b, False)
            with eng.Fori(1, NEG // 2) as i:
                for b in range(2):
                    body(i * 2 + b, i, b, False)
            body(NEG - 1, NEG // 2, 0, True)

        iota_g = iota16[:, :].unsqueeze(1).to_broadcast([P, EG, P])

        H = [banks[k][0:HI, 0:P] for k in range(2)]
        KEYS = [[banks[2 + n][0:EP, k * P:k * P + EP] for n in range(2)] for k in range(2)]
        LOOK = [[banks[4 + n][0:EP, k * P:(k + 1) * P] for n in range(2)] for k in range(2)]
        OFFS = [banks[6 + k][0:HI, 0:1] for k in range(2)]
        ATP = [banks[6 + k][:, :].bitcast(f16)[0:HI, 0:EG * P].rearrange("p (j e) -> p j e", j=EG)
               for k in range(2)]
        BOTH = range(2)

        def sort_sync(sp):
            sp.wait_ge(s_pat, 1)
            for k in BOTH:
                sp.dma_start(sorted_d[k].rearrange("(p t) w -> p t w", p=P),
                             (empty, empty2)[k]).then_inc(s_fill, 16)
            for k in BOTH:
                sp.wait_ge(s_npos[k], 1)
                sp.dma_start(npos_d[k].rearrange("(h l) -> h l", h=HI), npos[k]).then_inc(s_nposd[k], 16)
            for k in BOTH:
                sp.wait_ge(s_nposd[k], 16)
                if k:
                    sp.wait_ge(s_base[0], 1)
                sp.dma_start(npos_bc[0:T // 4, :],
                             npos_d[k][0:N].partition_broadcast(T // 4)).then_inc(s_nposb[k], 16)
            for k in BOTH:
                sp.wait_ge(s_base[k], 1)
                sp.dma_start(base_d[k].rearrange("(p g) -> p g", g=4), basec[k]).then_inc(s_based[k], 16)
                sp.dma_start(basei_d[k].rearrange("(p g) -> p g", g=4), basei[k]).then_inc(s_based[k], 16)
            for k in BOTH:
                sp.wait_ge(s_based[k], 32)
                sp.dma_start((base_bc, seg[1])[k][:, :], base_d[k].partition_broadcast(P)).then_inc(s_basel[k], 16)
                sp.dma_start(base_i[k][:, :],
                             basei_d[k].rearrange("(a n) -> a n", a=1)).then_inc(s_basel[k], 16)
            sorted_sync(sp, 0)

        def sorted_sync(sp, k):
            for b in range(2):
                sp.wait_ge(s_sc[k][b], 16 * EG * (NEG // 2 + 1 - b))
            sp.dma_start(S[k][:, :, :],
                         sorted_d[k].rearrange("(p t) w -> p t w", p=P)).then_inc(s_S[k], 16)

        def onehots(k, g, b):
            cols = ds(g * EG, EG)
            nc.vector.tensor_tensor(A16[k][:, b, :, :], iota_g[0:EP, :, 0:HI],
                                    khi[k][:, cols].unsqueeze(2).to_broadcast([EP, EG, HI]), ALU.is_equal)
            nc.vector.tensor_tensor(B16[k][:, b, :, :], iota_g[0:EP, :, :],
                                    klo[k][:, cols].unsqueeze(2).to_broadcast([EP, EG, P]),
                                    ALU.is_equal).then_inc(s_oh[k], 1)

        def sort_vector(dve):
            for k in BOTH:
                key = 1 - k
                vstep(nc.vector.tensor_scalar(digit_i, ends_i[:, key, :], 7, None, ALU.logical_shift_right))
                vstep(nc.vector.tensor_copy(khi[k], digit_i))
                vstep(nc.vector.tensor_scalar(digit_i, ends_i[:, key, :], P - 1, None, ALU.bitwise_and))
                vstep(nc.vector.tensor_copy(klo[k], digit_i))
                nc.vector.tensor_scalar(key1[k], ends[:, key, :], 1.0, None, ALU.add)
                nc.vector.tensor_scalar(keyc[k], ends[:, key, :], -2048.0, None, ALU.add).then_inc(s_key, 1)
            dve.wait_ge(s_key, 2)

            def pass1(g, i, b, last):
                for k in BOTH:
                    since(dve, s_ohu[k], g - 1)
                    onehots(k, g, b)

            in_pairs(dve, pass1)
            for k in BOTH:
                dve.wait_ge(s_ohu[k], NEG)
                vstep(nc.vector.tensor_tensor(cnt[k], H[k], nullm[:, :], ALU.add))
                nc.vector.tensor_tensor_scan(incl[k], ones[0:HI, :], cnt[k], 0.0, ALU.mult,
                                             ALU.add).then_inc(s_scan[k], 1)
            for k in BOTH:
                dve.wait_ge(s_scan[k], 1)
                dve.wait_ge(s_offs[k], 1)
                vstep(nc.vector.tensor_copy(offs[k], OFFS[k]))
                nc.vector.scalar_tensor_tensor(npos[k], incl[k], offs[k], cnt[k], ALU.add,
                                               ALU.subtract).then_inc(s_npos[k], 1)
                dve.wait_ge(s_npos[k], 1)
                nc.vector.tensor_scalar(seed[k], npos[k], 1.0, None, ALU.add).then_inc(s_seed[k], 1)
            for k in BOTH:
                onehots(k, 0, 0)

            def bases(k):
                dve.wait_ge(s_nposb[k], 16)
                for g in range(4):
                    vstep(nc.vector.tensor_scalar(npos_le[0:T // 4, :], npos_bc[0:T // 4, :],
                                                  thr[:, g:g + 1], 0.0, ALU.is_le, ALU.add,
                                                  accum_out=basec[k][:, g:g + 1]))
                vstep(nc.vector.tensor_scalar(basec[k], basec[k], -1.0, None, ALU.add))
                nc.vector.tensor_copy(basei[k], basec[k]).then_inc(s_base[k], 1)

            def tiles(g, i, b, last):
                for j in range(EG):
                    c = g * EG + j
                    n = (b + j) % 2
                    for k in BOTH:
                        if not last and j == (0, 2)[k]:
                            dve.wait_ge(s_h[k], g * EG + 1)
                            onehots(k, g + 1, 1 - b)
                    for k in BOTH:
                        since(dve, s_first[k], c - 1)
                        dve.wait_ge(s_bc[k], c + 1)
                    for k in BOTH:
                        nc.vector.scalar_tensor_tensor(
                            scr[k][0:EP, n, 0, 0:EP], KEYS[k][n], keyc[k][:, ds(c, 1)],
                            below[0:EP, 0:EP], ALU.is_equal, ALU.mult,
                            accum_out=rank[k][:, b, j:j + 1]).then_inc(s_rank[k], 1)
                    for k in BOTH:
                        dve.wait_ge(s_look[k], c + 1)
                    for k in BOTH:
                        nc.vector.scalar_tensor_tensor(
                            scr[k][0:EP, n, 1, :], LOOK[k][n], 1.0, B16[k][:, b, j, :],
                            ALU.mult, ALU.mult, accum_out=first[k][:, b, j:j + 1]).then_inc(s_first[k], 1)
                for k in BOTH:
                    dve.wait_ge(s_first[k], g * EG + EG)
                    nc.vector.tensor_tensor(place[k][:, b, :], rank[k][:, b, :], first[k][:, b, :],
                                            ALU.add).then_inc(s_pl[k], 1)
                for k in BOTH:
                    dve.wait_ge(s_pl[k], g + 1)
                    nc.vector.tensor_scalar(phi[k][:, b, :], place[k][:, b, :], 7, None,
                                            ALU.logical_shift_right)
                    nc.vector.tensor_scalar(plo[k][:, b, :], place[k][:, b, :], P - 1, None,
                                            ALU.bitwise_and).then_inc(s_dig[k], 1)
                for k in BOTH:
                    dve.wait_ge(s_dig[k], g + 1)
                    if k == 0:
                        since(dve, s_sc[0][b], i * (16 * EG))
                    to = rows1[:, ds(g * EG, EG)] if k else row[:, b, :]
                    nc.vector.scalar_tensor_tensor(to, plo[k][:, b, :], float(T),
                                                   phi[k][:, b, :], ALU.mult, ALU.add).then_inc(s_row[k], 1)

            in_pairs(dve, tiles)
            for k in BOTH:
                bases(k)
            windows_vector(dve, 0)

        def windows_vector(dve, k):
            dve.wait_ge(s_S[k], 16)
            dve.wait_ge(s_basel[k], 32)
            nc.vector.scalar_tensor_tensor(seg[k][:, 0:T], S[k][:, :, 0:1].rearrange("p t w -> p (t w)"),
                                           -1.0, (base_bc, seg[1])[k][:, :], ALU.add, ALU.subtract)
            nc.vector.tensor_copy(idx[k][:, :], S[k][:, :, 1:2].rearrange("p t w -> p (t w)")
                                  ).then_inc(s_seg, 1)

        def sort_tensor(pe):
            pe.wait_ge(s_mask, 1)
            for k in BOTH:
                nc.tensor.matmul(H[k], zeros16[:, 0:HI], zeros16[:, :], start=True, stop=True,
                                 skip_group_check=True)

            def count(k, b, j):
                return nc.tensor.matmul(H[k], A16[k][:, b, j, :], B16[k][:, b, j, :], start=False,
                                        stop=True, skip_group_check=True)

            def hist(g, i, b, last):
                for k in BOTH:
                    pe.wait_ge(s_oh[k], g + 1)
                    for j in range(EG):
                        done = count(k, b, j)
                    done.then_inc(s_ohu[k], 1)

            in_pairs(pe, hist)
            for k in BOTH:
                pe.wait_ge(s_scan[k], 1)
                nc.tensor.matmul(OFFS[k], above[0:HI, 0:HI], incl[k][:, P - 1:P], start=True,
                                 stop=True).then_inc(s_offs[k], 1)
            for k in BOTH:
                pe.wait_ge(s_seed[k], 1)
                nc.tensor.matmul(H[k], ident[0:HI, 0:HI], seed[k], start=True, stop=True,
                                 skip_group_check=True).then_inc(s_h[k], 1)

            def transposes(k, g, b):
                pe.wait_ge(s_oh[k], g + (NEG + 1))
                since(pe, s_ats[k], g)
                for j in range(EG):
                    done = nc.tensor.transpose(ATP[k][:, j, 0:EP], A16[k][:, b, j, :], ident16[0:EP, 0:EP])
                done.then_inc(s_at[k], 1)

            def tiles(g, i, b, last):
                for k in BOTH:
                    pe.wait_ge(s_ats[k], g + 1)
                for j in range(EG):
                    c = g * EG + j
                    for k in BOTH:
                        pe.wait_ge(s_hs[k], c + 1)
                        count(k, b, j).then_inc(s_h[k], 1)
                    n = (b + j) % 2
                    for k in BOTH:
                        pe.wait_ge(s_diag[k], c + 1)
                        for kk in BOTH:
                            since(pe, s_rank[kk], c - 1)
                        nc.tensor.matmul(KEYS[k][n], ones16[0:EP, 0:EP], diag[k][:, j, :],
                                         start=True, stop=True).then_inc(s_bc[k], 1)
                    for k in BOTH:
                        for kk in BOTH:
                            since(pe, s_first[kk], c - 1)
                        nc.tensor.matmul(LOOK[k][n], AT[k][:, b, j, :], Hs[k][:, n, :],
                                         start=True, stop=True).then_inc(s_look[k], 1)
                    if not last and j == 3:
                        for k in BOTH:
                            transposes(k, g + 1, 1 - b)

            for k in BOTH:
                transposes(k, 0, 0)
            in_pairs(pe, tiles)

        def sort_scalar(act):
            act.wait_ge(s_ends, 32)
            act.wait_ge(s_attr, 16)
            act.wait_ge(s_key, 2)

            def diagonal(k, g, j):
                nc.scalar.activation(diag[k][:, j, :], ident16[0:EP, 0:EP], ACT.Copy,
                                     scale=keyc[k][:, ds(g * EG + j, 1)]).then_inc(s_diag[k], 1)

            def transposed(k, g, b):
                act.wait_ge(s_at[k], g + 1)
                nc.scalar.copy(AT[k][:, b, :, :], ATP[k][:, :, 0:EP]).then_inc(s_ats[k], 1)

            def table(k, n, slot):
                act.wait_ge(s_h[k], n)
                nc.scalar.copy(Hs[k][:, slot, :], H[k]).then_inc(s_hs[k], 1)

            def tiles(g, i, b, last):
                cols = ds(g * EG, EG)
                since(act, s_sc[0][b], i * (16 * EG))
                nc.scalar.copy(pay[:, b, :, 2:WP[0]], attr[:, cols, :])
                for k in BOTH:
                    to = words1[:, cols, :] if k else pay[:, b, :, :]
                    nc.scalar.copy(to[:, :, 0:1], key1[k][:, cols].unsqueeze(2))
                    nc.scalar.copy(to[:, :, 1:2], ends[:, k, cols].unsqueeze(2)).then_inc(s_pay[k], 1)
                for j in range(EG):
                    c = g * EG + j
                    for k in BOTH:
                        table(k, c + 2, (b + j + 1) % 2)
                        if not last:
                            act.wait_ge(s_bc[k], c + 1)
                            diagonal(k, g + 1, j)
                    if not last and j == 3:
                        for k in BOTH:
                            transposed(k, g + 1, 1 - b)

            for k in BOTH:
                for j in range(EG):
                    diagonal(k, 0, j)
                transposed(k, 0, 0)
                table(k, 1, 0)
            in_pairs(act, tiles)

        def scatter(gp, k, b, rows, words):
            for j in range(EG):
                gp.indirect_dma_start(
                    out=sorted_d[k], out_offset=bass.IndirectOffsetOnAxis(ap=rows[:, b, j:j + 1], axis=0),
                    in_=words[:, b, j, 0:WP[k]], in_offset=None).then_inc(s_sc[k][b], 16)

        def sort_gpsimd(gp):
            gp.wait_ge(s_fill, 32)

            def tiles(g, i, b, last):
                gp.wait_ge(s_row[0], g + 1)
                gp.wait_ge(s_pay[0], g + 1)
                gp.sem_inc(s_turn, 1)
                scatter(gp, 0, b, row, pay)

            in_pairs(gp, tiles)

        def second_gpsimd(gp):
            gp.wait_ge(s_row[1], NEG)
            gp.wait_ge(s_pay[1], NEG)

            def tiles(g, i, b, last):
                since(gp, s_sc[1][b], i * (16 * EG))
                nc.gpsimd.tensor_copy(row1[:, b, :], rows1[:, ds(g * EG, EG)])
                nc.gpsimd.tensor_copy(pay1[:, b, :, :], words1[:, ds(g * EG, EG), :]).then_inc(s_kept, 1)
                gp.wait_ge(s_kept, g + 1)
                gp.sem_inc(s_turn, 1)
                scatter(gp, 1, b, row1, pay1)

            in_pairs(gp, tiles)

        s_g = sem("s_g")
        gcount = [0]

        def gstep(ins):
            gcount[0] += 1
            ins.then_inc(s_g, 1)
            nc.gpsimd.wait_ge(s_g, gcount[0])

        def constants_gpsimd(gp):
            kw = dict(allow_small_or_imprecise_dtypes=True)
            nc.gpsimd.iota(diff[:, :], [[1, P]], base=0, channel_multiplier=-1, **kw)
            nc.gpsimd.iota(iota[:, :], [[1, P]], base=0, channel_multiplier=0, **kw)
            nc.gpsimd.iota(iota16[:, :], [[1, P]], base=0, channel_multiplier=0, **kw)
            nc.gpsimd.iota(nodes[:, :], [[1, P]], base=0, channel_multiplier=P, **kw)
            nc.gpsimd.iota(thr[:, :], [[P, 4]], base=0, channel_multiplier=4 * P, **kw).then_inc(s_const, 1)
            nc.gpsimd.memset(empty2[:, :, :], 0.0)
            gstep(nc.gpsimd.memset(empty[:, :, :], NONE))
            nc.gpsimd.memset(empty[:, :, 0:2], 0.0).then_inc(s_pat, 1)

        def constants_vector(dve):
            nc.vector.memset(ones[:, :], 1.0)
            nc.vector.memset(ones16[:, :], 1.0)
            nc.vector.memset(zeros16[:, :], 0.0)
            dve.wait_ge(s_const, 1)
            nc.vector.tensor_scalar(ident[:, :], diff[:, :], 0.0, None, ALU.is_equal)
            nc.vector.tensor_scalar(ident16[:, :], diff[:, :], 0.0, None, ALU.is_equal)
            nc.vector.tensor_scalar(below[:, :], diff[:, :], 0.0, None, ALU.is_lt)
            nc.vector.tensor_scalar(nullm[:, :], nodes[:, :], float(N), None, ALU.is_lt)
            nc.vector.tensor_scalar(above[:, :], diff[:, :], 0.0, None, ALU.is_gt).then_inc(s_mask, 1)
            dve.wait_ge(s_mask, 1)
            dve.wait_ge(s_ends, 32)
            vstep(nc.vector.tensor_copy(ends[:, :, :], ends_i[:, :, :]))

        def loads_sync(sp):
            sp.dma_start(ends_i[:, 0, :], src.rearrange("(p t) -> p t", p=EP)).then_inc(s_ends, 16)
            sp.dma_start(ends_i[:, 1, :], dst.rearrange("(p t) -> p t", p=EP)).then_inc(s_ends, 16)
            sp.dma_start(attr, edge_attr.rearrange("(p t) h -> p t h", p=EP)).then_inc(s_attr, 16)

        stage0 = [part(r * CB * 3 * D0, CB, 3 * D0) for r in range(3)]
        values = part(0, T, D0)
        acc1 = part((NB + 1) * 3 * DM, 2, NWIN)
        odd1 = part(0, 2, NWIN)
        o = (NB + 1) * 3 * DM + 2 * NWIN
        emb = part(o, NWIN)
        cent = part(o + NWIN, NWIN)
        work1 = part(o + 2 * NWIN, NWIN)
        hT = cent[0:D0 + 1, :]
        den0 = work1[0:D0, :]
        hs = part(2 * NWIN, NB, D0)
        sq = part(2 * NWIN + NB * D0, NB, D0)

        xs = sb("xs", [P, NB, D0])
        mean = sb("mean", [P, NB])
        var = sb("var", [P, NB])
        W0 = sb("W0", [D0 + 1, 3 * D0])
        Wo = sb("Wo", [D0 + 1, D0])
        Wp = sb("Wp", [D0, DM])
        shift = sb("shift", [P, 2])
        W1 = sb("W1", [P, LAYERS, 3, DM])
        lns = sb("lns", [P, LAYERS])
        lnb = sb("lnb", [P, LAYERS])
        invw = sb("invw", [P, D0])
        invb = sb("invb", [P, D0])
        avg = sb("avg", [P, P])
        eps = sb("eps", [P, 1])
        idxs = sb("idxs", [P, SLOTS, TG], i32)
        kv = sb("kv", [P, SLOTS, TG, 2 * DM])
        R = sb("R", [P, SLOTS, TG, P])
        kv_flat, R_flat = (a[:, :, :, :].rearrange("p a b c -> p (a b c)") for a in (kv, R))
        stage1 = [a.rearrange("p (b c) -> p b c", b=CB) for a in (
            kv_flat[:, 0:CB * 3 * DM], kv_flat[:, CB * 3 * DM:2 * CB * 3 * DM], R_flat[:, 0:CB * 3 * DM])]
        acc0 = kv[:, :, :, :].rearrange("p a b c -> p (a b c)")[:, 0:NWIN]
        scratch = sb("scratch", [P, SLOTS * TG * DM + 2 * TG * P + 2 * TG * DM])
        qw = scratch[:, 0:SLOTS * TG * DM].rearrange("p (s j c) -> p s j c", s=SLOTS, j=TG)
        o = SLOTS * TG * DM
        RT = scratch[:, o:o + 2 * TG * P].rearrange("p (s c) -> p s c", s=2)
        prods = scratch[:, o + 2 * TG * P:]
        prod = prods.rearrange("p (s j c) -> p s j c", s=2, j=TG)
        odd0 = scratch[:, 0:NWIN]
        chain = scratch[0:H0, 0:5 * T].rearrange("p (n t) -> p n t", n=5)
        red = sb("red", [P, 2, TG * H0])
        wts = sb("wts", [P, 2, TG * H1])
        vw = sb("vw", [P, 2, TG, DM])
        LT = kv[:, :, :, :].rearrange("p a b c -> p (a b c)")[:, 0:T * H0]
        EB = T * H0 // P
        EH = EB // 4
        fwd = prods[:, 0:EH * P]
        bwd = vw[:, :, :, :].rearrange("p a b c -> p (a b c)")[:, 0:EH * P]
        gate = R[:, :, :, :].rearrange("p a b c -> p (a b c)")[:, 0:EH * P]
        gate2 = R[:, :, :, :].rearrange("p a b c -> p (a b c)")[:, EH * P:2 * EH * P]
        ends_f = sb("ends_f", [P, 3, EB])
        carries = sb("carries", [P, 2, EB])

        s_x = sem("s_x")
        s_w = sem("s_w")
        s_zero = sem("s_zero")
        s_var = sem("s_var")
        s_std = sem("s_std")
        s_hn = sem("s_hn")
        s_tp = sem("s_tp")
        s_ts = sem("s_ts")
        s_pj = sem("s_pj")
        s_pjs = sem("s_pjs")
        s_tab = [sem(f"s_tab{n}") for n in range(3)]
        s_ix = sem("s_ix")
        s_kv = [sem(f"s_kv{n}") for n in range(SLOTS)]
        s_qw = [sem(f"s_qw{n}") for n in range(SLOTS)]
        s_R = sem("s_R")
        s_dist = sem("s_dist")
        s_rt = sem("s_rt")
        s_rts = sem("s_rts")
        s_qe = sem("s_qe")
        s_prod = sem("s_prod")
        s_red = sem("s_red")
        s_lg = sem("s_lg")
        s_vc = sem("s_vc")
        s_wt = sem("s_wt")
        s_vw = sem("s_vw")
        s_wb = sem("s_wb")
        s_sum = sem("s_sum")
        s_acc = sem("s_acc")
        s_ls = sem("s_ls")
        s_lt = sem("s_lt")
        s_lts = sem("s_lts")
        s_ed = sem("s_ed")
        s_edd = sem("s_edd")
        s_edl = sem("s_edl")
        s_ca = sem("s_ca")
        s_cad = sem("s_cad")
        s_cal = sem("s_cal")
        s_mx = sem("s_mx")
        s_mt = sem("s_mt")
        s_sh = sem("s_sh")
        s_ex = sem("s_ex")
        s_both = sem("s_both")
        s_den = sem("s_den")
        s_agg = sem("s_agg")
        s_o = sem("s_o")
        s_emb = sem("s_emb")
        s_c1 = sem("s_c1")
        s_m1 = sem("s_m1")
        s_xb = sem("s_xb")
        s_c1x = sem("s_c1x")
        s_mean = sem("s_mean")
        s_varp = sem("s_varp")
        s_sq = sem("s_sq")
        s_root = sem("s_root")
        s_nm = sem("s_nm")
        s_fin = sem("s_fin")
        s_out = sem("s_out")

        def fours(eng, stages):
            def step(i, s):
                for lag, fn in stages:
                    ii, ss = i + (s - lag) // SLOTS, (s - lag) % SLOTS
                    if isinstance(i, int) and not 0 <= ii * SLOTS + ss < NG:
                        continue
                    fn(ii, ss, ii * SLOTS + ss)
            lead = min(0, min(lag for lag, _ in stages))
            for n in range(lead, 0):
                step(n // SLOTS, n % SLOTS)
            for s in range(SLOTS):
                step(0, s)
            with eng.Fori(1, TI - 1) as i:
                for s in range(SLOTS):
                    step(i, s)
            for n in range((TI - 1) * SLOTS, NG + max(lag for lag, _ in stages)):
                step(n // SLOTS, n % SLOTS)

        def load_weights(sp):
            def w(dst_ap, src_ap):
                sp.dma_start(dst_ap, src_ap).then_inc(s_w, 16)
                wcount[0] += 16
            rowv = lambda a: a.rearrange("(o n) -> o n", o=1)
            col = lambda a: a.rearrange("(n o) -> n o", o=1)
            for n, (m, v) in enumerate(((wq, bq), (wk, bk), (wv, bv))):
                w(W0[0:D0, n * D0:(n + 1) * D0], m)
                w(W0[D0:D0 + 1, n * D0:(n + 1) * D0], rowv(v))
            w(Wo[0:D0, :], wo)
            w(Wo[D0:D0 + 1, :], rowv(bo))
            w(Wp[:, :], wp)
            w(shift[:, 0:1], col(wpb))
            w(shift[:, 1:2], wpos.rearrange("o n -> n o"))
            for l in range(LAYERS):
                for n, m in enumerate((qT, kT, vT)):
                    w(W1[:, l, n, :], m[l])
                w(lns[:, l:l + 1], col(ln_scale[l]))
                w(lnb[:, l:l + 1], col(ln_bias[l]))
            w(invw[:, :], inv_w)
            w(invb[:, :], inv_b.partition_broadcast(P))
        wcount = [0]

        def zeros_gpsimd(gp):
            nc.gpsimd.memset(xs[:, NB - 1:NB, :], 0.0).then_inc(s_zero, 1)
            nc.gpsimd.memset(avg[:, :], 1.0 / DM)
            nc.gpsimd.memset(eps[:, :], 1e-6).then_inc(s_zero, 1)

        def load_x(sp):
            sp.wait_ge(s_zero, 1)
            full = (NB - 1) * P
            sp.dma_start(xs[:, 0:NB - 1, :], x[0:full].rearrange("(b p) c -> p b c", p=P)).then_inc(s_x, 16)
            sp.dma_start(xs[0:N - full, NB - 1, :], x[full:N]).then_inc(s_x, 16)

        def hT_borders():
            nc.vector.memset(hT[0:D0, NPAD:NWIN], 0.0)
            vstep(nc.vector.memset(hT[D0:D0 + 1, :], 1.0))

        def norm_vector(dve, n):
            if n == 0:
                hT_borders()
            vstep(nc.vector.tensor_reduce(mean[:, :], xs[:, :, :], AX.X, ALU.add))
            vstep(nc.vector.tensor_scalar(mean[:, :], mean[:, :], 1.0 / D0, None, ALU.mult))
            vstep(nc.vector.tensor_tensor(hs[:, :, :], xs[:, :, :],
                                          mean[:, :].unsqueeze(2).to_broadcast([P, NB, D0]), ALU.subtract))
            vstep(nc.vector.tensor_tensor(sq[:, :, :], hs[:, :, :], hs[:, :, :], ALU.mult))
            vstep(nc.vector.tensor_reduce(var[:, :], sq[:, :, :], AX.X, ALU.add))
            nc.vector.tensor_scalar(var[:, :], var[:, :], 1.0 / D0, 1e-5, ALU.mult, ALU.add).then_inc(s_var, 1)
            dve.wait_ge(s_std, n + 1)
            vstep(nc.vector.reciprocal(var[:, :], var[:, :]))
            vstep(nc.vector.tensor_tensor(hs[:, :, :], hs[:, :, :],
                                          var[:, :].unsqueeze(2).to_broadcast([P, NB, D0]), ALU.mult))
            nc.vector.tensor_scalar(hs[:, :, :], hs[:, :, :], 0.0, None, ALU.max).then_inc(s_hn, 1)

        TR = -(-NB // 4)

        def norm_scalar(act, n):
            act.wait_ge(s_var, n + 1)
            nc.scalar.activation(var[:, :], var[:, :], ACT.Sqrt).then_inc(s_std, 1)
            for g in range(TR):
                blocks = min(4, NB - g * 4)
                act.wait_ge(s_tp, n * TR + g + 1)
                nc.scalar.copy(hT[0:D0, g * 512:g * 512 + blocks * P],
                               banks[g][0:D0, 0:blocks * P]).then_inc(s_ts, 1)

        def norm_tensor(pe, n):
            pe.wait_ge(s_hn, n + 1)
            for g in range(TR):
                for b in range(g * 4, min(g * 4 + 4, NB)):
                    done = nc.tensor.transpose(banks[g][0:D0, (b % 4) * P:(b % 4 + 1) * P], hs[:, b, :],
                                               ident[:, :])
                done.then_inc(s_tp, 1)
            pe.wait_ge(s_ts, (n + 1) * TR)

        NT = NB + 1
        TABLES = [32 * len(range(r, C, 3)) for r in range(3)]

        def wait_tables(eng, n):
            for r in range(3):
                eng.wait_ge(s_tab[r], TABLES[r] * (n + 1))

        def chunk_blocks(c, most=NT):
            return range(c * CB, min(c * CB + CB, most))

        def project_tensor(pe, n, c, lhs, rhs, cols):
            for b in chunk_blocks(c):
                m = n * NT + b
                since(pe, s_pjs, m - 3)
                nc.tensor.matmul(banks[b % 4][:, 0:cols], lhs[:, b * P:(b + 1) * P], rhs, start=True,
                                 stop=True).then_inc(s_pj, 1)

        def project_scalar(act, n, c, stage, cols):
            if c >= 3:
                act.wait_ge(s_tab[c % 3], TABLES[c % 3] * n + 32 * (c // 3))
            for b in chunk_blocks(c):
                act.wait_ge(s_pj, n * NT + b + 1)
                nc.scalar.copy(stage[c % 3][:, b % CB, :], banks[b % 4][:, 0:cols]).then_inc(s_pjs, 1)

        def tables_sync(sp, n, stage, width, q_d, kv_d):
            for c in range(C):
                rows_, kv_rows = chunk_blocks(c), chunk_blocks(c, NB)
                lo, nq, nk = c * CB * P, len(rows_), len(kv_rows)
                sp.wait_ge(s_pjs, n * NT + rows_[-1] + 1)
                sp.dma_start(q_d[lo:lo + nq * P].rearrange("(b p) c -> p b c", p=P),
                             stage[c % 3][:, 0:nq, 0:width]).then_inc(s_tab[c % 3], 16)
                sp.dma_start(kv_d[lo:lo + nk * P].rearrange("(b p) c -> p b c", p=P),
                             stage[c % 3][:, 0:nk, width:3 * width]).then_inc(s_tab[c % 3], 16)

        def windows_sync(sp, n, k, q_d, width):
            wait_tables(sp, n)
            sp.wait_ge(s_basel[k], 32)

            def load(i, s, g):
                since(sp, s_qe, g + (n * NG - SLOTS + 1))
                _, bases = nc.values_load_multi_w_load_instructions(
                    base_i[k][0:1, ds(g * TG, TG)], min_val=0, max_val=N - 1, engines=[mybir.EngineType.SP])
                for j in range(TG):
                    sp.dma_start(qw[:, s, j, 0:width], q_d[ds(bases[j], P), :]).then_inc(s_qw[s], 16)

            fours(sp, [(0, load)])

        def gather_gpsimd(gp, n, kv_d, width):
            wait_tables(gp, n)

            def gather(i, s, g):
                gp.wait_ge(s_ix, g + (n * NG + 1))
                since(gp, s_prod, g + (n * NG - SLOTS + 1))
                since(gp, s_vw if n else s_vc, g + (n * NG - SLOTS + 1))
                gp.sem_inc(s_turn, 1)
                for j in range(TG):
                    gp.indirect_dma_start(
                        out=kv[:, s, j, 0:2 * width], out_offset=None, in_=kv_d,
                        in_offset=bass.IndirectOffsetOnAxis(ap=idxs[:, s, j:j + 1], axis=0)
                    ).then_inc(s_kv[s], 16)

            fours(gp, [(0, gather)])

        def rows(n, i):
            return i * (16 * TG) + (n * TI + 1) * 16 * TG

        def stage_indices(act, n, k):
            def fn(i, s, g):
                since(act, s_kv[s], rows(n, i) - 16 * TG)
                nc.scalar.copy(idxs[:, s, :], idx[k][:, ds(g * TG, TG)]).then_inc(s_ix, 1)
            return fn

        def copy_transposed(act, n):
            def fn(i, s, g):
                act.wait_ge(s_rt, g + (n * NG + 1))
                since(act, s_qe, g + (n * NG - 1))
                nc.scalar.copy(RT[:, s % 2, :], banks[s % 2][:, :]).then_inc(s_rts, 1)
            return fn

        def keep_values(act):
            def fn(i, s, g):
                act.wait_ge(s_kv[s], rows(0, i))
                nc.scalar.copy(values[:, ds(g * TG, TG), :], kv[:, s, :, 0:2 * D0][:, :, D0:2 * D0]
                               ).then_inc(s_vc, 1)
            return fn

        def one_hot(dve, n, k, ring):
            def fn(i, s, g):
                ring(i, s, g)
                nc.vector.tensor_tensor(R[:, s, :, :], iota[:, :].unsqueeze(1).to_broadcast([P, TG, P]),
                                        seg[k][:, ds(g * TG, TG)].unsqueeze(2).to_broadcast([P, TG, P]),
                                        ALU.is_equal).then_inc(s_R, 1)
            return fn

        def one_hot_scalar(act, nR, k, ring):
            def distance(i, s, g):
                ring(i, s, g)
                for j in range(TG):
                    done = nc.scalar.activation(R[:, s, j, :], iota[:, :], ACT.Abs, scale=-1.0,
                                                bias=seg[k][:, ds(g * TG + j, 1)])
                done.then_inc(s_dist, 1)

            def at_zero(i, s, g):
                act.wait_ge(s_dist, g + ((nR - 1) * NG + 1))
                nc.scalar.activation(R[:, s, :, :], R[:, s, :, :], ACT.Relu, scale=-1.0,
                                     bias=ones[:, 0:1]).then_inc(s_R, 1)
            return distance, at_zero

        def transposes(pe, n, nR):
            def fn(i, s, g):
                pe.wait_ge(s_R, g + (nR * NG + 1))
                since(pe, s_rts, g + (n * NG - 1))
                for j in range(TG):
                    done = nc.tensor.transpose(banks[s % 2][:, j * P:(j + 1) * P], R[:, s, j, :], ident[:, :])
                done.then_inc(s_rt, 1)
            return fn

        def expand(pe, n, width):
            def fn(i, s, g):
                pe.wait_ge(s_rts, g + (n * NG + 1))
                pe.wait_ge(s_qw[s], rows(n, i))
                since(pe, s_prod, g + (n * NG - 1))
                for j in range(TG):
                    done = nc.tensor.matmul(banks[2 + s % 2][:, j * width:(j + 1) * width],
                                            RT[:, s % 2, j * P:(j + 1) * P], qw[:, s, j, 0:width],
                                            start=True, stop=True)
                done.then_inc(s_qe, 1)
            return fn

        def logits(dve, n, width, heads):
            def times(i, s, g):
                dve.wait_ge(s_kv[s], rows(n, i))
                dve.wait_ge(s_qe, g + (n * NG + 1))
                since(dve, s_red, g + (n * NG - 1))
                nc.vector.tensor_tensor(prod[:, s % 2, :, 0:width], kv[:, s, :, 0:width],
                                        banks[2 + s % 2][:, 0:TG * width].rearrange("p (j c) -> p j c", j=TG),
                                        ALU.mult).then_inc(s_prod, 1)

            def total(i, s, g):
                dve.wait_ge(s_prod, g + (n * NG + 1))
                since(dve, s_lg, g + (n * NG - 1))
                nc.vector.tensor_reduce(red[:, s % 2, 0:TG * heads].rearrange("p (j h) -> p j h", j=TG),
                                        prod[:, s % 2, :, 0:width].rearrange("p j (h d) -> p j h d", h=heads),
                                        AX.X, ALU.add).then_inc(s_red, 1)
            return times, total

        def a_vector(dve):
            times, total = logits(dve, 0, D0, H0)

            def bias(i, s, g):
                dve.wait_ge(s_red, g + 1)
                at = S[0][:, ds(g * TG, TG), 2:2 + H0]
                nc.vector.scalar_tensor_tensor(
                    at, red[:, s % 2, :].rearrange("p (j h) -> p j h", j=TG), (D0 // H0) ** -0.5, at,
                    ALU.mult, ALU.add).then_inc(s_lg, 1)

            def ring(i, s, g):
                since(dve, s_rt, g - SLOTS + 1)

            fours(dve, [(0, one_hot(dve, 0, 0, ring)), (1, times), (1, total), (1, bias)])

        def max_tensor(pe):
            pe.wait_ge(s_lg, NG)
            for g in range(EB // 4):
                pe.wait_ge(s_ls, g + 1)
                since(pe, s_lts, g - 3)
                for b in range(4):
                    done = nc.tensor.transpose(banks[4 + g % 4][:, b * P:(b + 1) * P],
                                               RT[:, g % 2, b * P:(b + 1) * P], ident[:, :])
                done.then_inc(s_lt, 1)
            pe.wait_ge(s_mx, 4)
            for g in range(EB // 4):
                since(pe, s_sh, g - 3)
                for b in range(4):
                    c = (g * 4 + b) * P
                    done = nc.tensor.transpose(banks[4 + g % 4][:, b * P:(b + 1) * P], LT[:, c:c + P],
                                               ident[:, :])
                done.then_inc(s_mt, 1)

        def max_scalar(act):
            act.wait_ge(s_lg, NG)
            act.wait_ge(s_qe, NG)
            for g in range(EB // 4):
                t = g * 4 * (P // H0)
                since(act, s_lt, g - 1)
                nc.scalar.copy(RT[:, g % 2, :].rearrange("p (t h) -> p t h", h=H0),
                               S[0][:, t:t + 4 * (P // H0), 2:2 + H0]).then_inc(s_ls, 1)
                act.wait_ge(s_lt, g + 1)
                nc.scalar.copy(LT[:, g * 512:(g + 1) * 512], banks[4 + g % 4][:, :]).then_inc(s_lts, 1)
            act.wait_ge(s_sh, EB // 4)
            at = S[0][:, :, 2:2 + H0]
            nc.scalar.activation(at, at, ACT.Exp).then_inc(s_ex, 1)

        def scans(c):
            x = LT[:, c * EH * P:(c + 1) * EH * P]
            pos = lambda ap: ap.rearrange("p (b e) -> p b e", e=P)
            vstep(nc.vector.tensor_scalar(gate, x, FLOOR, 2 * BIG, ALU.is_gt, ALU.mult))
            vstep(nc.vector.tensor_scalar(gate, gate, -BIG, None, ALU.add))
            vstep(nc.vector.tensor_copy(gate2, gate))
            nc.vector.memset(pos(gate)[:, :, 0:1], -BIG)
            vstep(nc.vector.memset(pos(gate2)[:, :, P - 1:P], -BIG))
            nc.vector.tensor_tensor_scan(fwd, gate, x, -BIG, ALU.min, ALU.max)
            vstep(nc.vector.tensor_tensor_scan(bwd[:, ::-1], gate2[:, ::-1], x[:, ::-1], -BIG,
                                               ALU.min, ALU.max))
            return x, pos

        def max_vector(dve):
            dve.wait_ge(s_lts, EB // 4)
            for c in range(4):
                x, pos = scans(c)
                blocks = slice(c * EH, (c + 1) * EH)
                nc.vector.tensor_copy(ends_f[:, 0, blocks], pos(fwd)[:, :, P - 1])
                nc.vector.tensor_copy(ends_f[:, 1, blocks], pos(bwd)[:, :, 0])
                vstep(nc.vector.tensor_reduce(ends_f[:, 2, blocks], pos(x), AX.X, ALU.min))
            vstep(nc.vector.tensor_scalar(ends_f[:, 2, :], ends_f[:, 2, :], FLOOR, 2 * BIG, ALU.is_gt,
                                          ALU.mult))
            nc.vector.tensor_scalar(ends_f[:, 2, :], ends_f[:, 2, :], -BIG, None, ALU.add).then_inc(s_ed, 1)
            dve.wait_ge(s_edl, 48)
            nc.vector.memset(chain[:, 3, 0:1], -BIG)
            nc.vector.memset(chain[:, 4, T - 1:T], -BIG)
            vstep(nc.vector.tensor_tensor_scan(chain[:, 3, 1:T], chain[:, 2, 0:T - 1], chain[:, 0, 0:T - 1],
                                               -BIG, ALU.min, ALU.max))
            nc.vector.tensor_tensor_scan(chain[:, 4, T - 2::-1], chain[:, 2, T - 1:0:-1],
                                         chain[:, 1, T - 1:0:-1], -BIG, ALU.min, ALU.max).then_inc(s_ca, 1)
            dve.wait_ge(s_cal, 32)
            for c in range(4):
                x = LT[:, c * EH * P:(c + 1) * EH * P].rearrange("p (b e) -> p b e", e=P)
                blocks = slice(c * EH, (c + 1) * EH)
                for n, e in enumerate((0, P - 1)):
                    g1 = red[:, n, 0:EH]
                    vstep(nc.vector.tensor_scalar(g1, x[:, :, e], FLOOR, 2 * BIG, ALU.is_gt, ALU.mult))
                    vstep(nc.vector.scalar_tensor_tensor(g1, g1, -BIG, carries[:, n, blocks], ALU.add,
                                                         ALU.min))
                    vstep(nc.vector.tensor_tensor(x[:, :, e], x[:, :, e], g1, ALU.max))
                xq, pos = scans(c)
                nc.vector.scalar_tensor_tensor(xq, fwd, FLOOR, bwd, ALU.max, ALU.max).then_inc(s_mx, 1)
                dve.wait_ge(s_mx, c + 1)
            for g in range(EB // 4):
                t = g * 4 * (P // H0)
                at = S[0][:, t:t + 4 * (P // H0), 2:2 + H0]
                dve.wait_ge(s_mt, g + 1)
                nc.vector.tensor_tensor(at, at, banks[4 + g % 4][:, :].rearrange("p (t h) -> p t h", h=H0),
                                        ALU.subtract).then_inc(s_sh, 1)

        def max_sync(sp):
            sp.wait_ge(s_ed, 1)
            for n in range(3):
                sp.dma_start(edge_d[n].rearrange("(b p) -> p b", p=P), ends_f[:, n, :],
                             allow_slow_non_contiguous=True).then_inc(s_edd, 16)
            sp.wait_ge(s_edd, 48)
            for n in range(3):
                sp.dma_start(chain[:, n, :], edge_d[n].rearrange("(t h) -> h t", h=H0),
                             allow_slow_non_contiguous=True).then_inc(s_edl, 16)
            sp.wait_ge(s_ca, 1)
            for n in range(2):
                sp.dma_start(carry_d[n].rearrange("(t h) -> h t", h=H0), chain[:, 3 + n, :],
                             allow_slow_non_contiguous=True).then_inc(s_cad, 16)
            sp.wait_ge(s_cad, 32)
            for n in range(2):
                sp.dma_start(carries[:, n, :], carry_d[n].rearrange("(b p) -> p b", p=P),
                             allow_slow_non_contiguous=True).then_inc(s_cal, 16)

        def add_sums(dve, m, k, acc, bank, apart):
            bases = [None] * TG

            def load(*tiles):
                def fn(i, s, g):
                    _, bases[tiles[0]:tiles[-1] + 1] = nc.values_load_multi_w_load_instructions(
                        base_i[k][0:1, ds(g * TG + tiles[0], len(tiles))], min_val=0, max_val=N - 1,
                        engines=[mybir.EngineType.DVE])
                return fn

            def fn(i, s, g):
                dve.wait_ge(s_sum, g + (m * NG + 1))
                for j in range(TG):
                    to, add = acc(bases[j], j), bank(s, j)
                    since(dve, s_acc, g * TG + (m * T + j + 1 - apart))
                    nc.vector.tensor_tensor(to, to, add, ALU.add).then_inc(s_acc, 1)
            return load, fn

        def b_vector(dve):
            dve.wait_ge(s_ex, 1)
            nc.vector.memset(odd0, 0.0)
            vstep(nc.vector.memset(acc0[:, :], 0.0))

            def weigh(i, s, g):
                since(dve, s_sum, g - 1)
                w = S[0][:, ds(g * TG, TG), 2:2 + H0].unsqueeze(3)
                nc.vector.tensor_tensor(
                    vw[:, s % 2, :, 0:D0].rearrange("p j (h d) -> p j h d", h=H0),
                    values[:, ds(g * TG, TG), :].rearrange("p j (h d) -> p j h d", h=H0),
                    w.to_broadcast([P, TG, H0, D0 // H0]), ALU.mult).then_inc(s_vw, 1)

            load, sums = add_sums(dve, 0, 0, lambda base, j: (acc0, odd0)[j % 2][:, ds(base, P)],
                                  lambda s, j: banks[4 + s % 2][:, j * P:(j + 1) * P], 2)
            fours(dve, [(0, weigh), (1, load(0, 1, 2, 3)), (1, sums)])
            dve.wait_ge(s_acc, T)
            nc.vector.tensor_tensor(acc0[:, :], acc0[:, :], odd0, ALU.add).then_inc(s_both, 1)

        def b_scalar(act):
            def beside(i, s, g):
                since(act, s_sum, g - 1)
                w = S[0][:, ds(g * TG, TG), 2:2 + H0].unsqueeze(3)
                nc.scalar.copy(vw[:, s % 2, :, D0:2 * D0].rearrange("p j (h d) -> p j h d", h=H0),
                               w.to_broadcast([P, TG, H0, D0 // H0])).then_inc(s_wb, 1)

            def ring(i, s, g):
                since(act, s_sum, g - SLOTS + 1)

            act.wait_ge(s_ex, 1)
            distance, at_zero = one_hot_scalar(act, 1, 0, ring)
            fours(act, [(-2, distance), (-1, at_zero), (0, beside)])

        def b_tensor(pe):
            def fn(i, s, g):
                pe.wait_ge(s_R, g + (NG + 1))
                pe.wait_ge(s_vw, g + 1)
                pe.wait_ge(s_wb, g + 1)
                since(pe, s_acc, (g - 1) * TG)
                for j in range(TG):
                    done = nc.tensor.matmul(banks[4 + s % 2][:, j * P:(j + 1) * P], vw[:, s % 2, j, :],
                                            R[:, s, j, :], start=True, stop=True)
                done.then_inc(s_sum, 1)

            fours(pe, [(0, fn)])

        def out0_sync(sp):
            sp.wait_ge(s_both, 1)
            sp.dma_start(den0[:, :], acc0[D0:2 * D0, :]).then_inc(s_den, 16)

        def out0_vector(dve):
            hT_borders()
            dve.wait_ge(s_den, 16)
            vstep(nc.vector.tensor_scalar(den0[:, :], den0[:, :], 1e-16, None, ALU.add))
            vstep(nc.vector.reciprocal(den0[:, :], den0[:, :]))
            nc.vector.tensor_tensor(hT[0:D0, 0:NPAD], acc0[0:D0, 0:NPAD], den0[:, 0:NPAD],
                                    ALU.mult).then_inc(s_agg, 1)
            for g in range(4):
                lo, hi = g * 7, min(g * 7 + 7, NB)
                dve.wait_ge(s_o, g + 1)
                vstep(nc.vector.tensor_tensor(
                    xs[:, lo:hi, :], xs[:, lo:hi, :],
                    banks[g][:, 0:(hi - lo) * D0].rearrange("p (b c) -> p b c", c=D0), ALU.add))

        def out_tensor(pe, lhs, rhs):
            for g in range(4):
                for b in range(g * 7, min(g * 7 + 7, NB)):
                    done = nc.tensor.matmul(banks[g][:, (b % 7) * D0:(b % 7 + 1) * D0],
                                            lhs[:, b * P:(b + 1) * P], rhs, start=True, stop=True)
                done.then_inc(s_o, 1)

        def features(pe, c, l):
            pe.wait_ge(s_emb, l * C + c + 1)
            if l < LAYERS:
                project_tensor(pe, l + 1, c, emb, W1[:, l, :, :].rearrange("p a n -> p (a n)"), 3 * DM)
                return
            since(pe, s_fin, c - 3)
            for b in chunk_blocks(c, NB):
                done = nc.tensor.matmul(banks[c % 4][:, (b % CB) * D0:(b % CB + 1) * D0],
                                        emb[:, b * P:(b + 1) * P], invw[:, :], start=True, stop=True)
            done.then_inc(s_o, 1)

        def embed_tensor(pe):
            for t in range(C + 1):
                if t < C:
                    lo, w = CHUNKS[t]
                    since(pe, s_emb, t - 3)
                    nc.tensor.matmul(banks[4 + t % 4][:, 0:w], Wp[:, :], hT[0:D0, lo:lo + w], start=True,
                                     stop=True).then_inc(s_c1, 1)
                if t > 0:
                    features(pe, t - 1, 0)

        def embed_scalar(act):
            for t in range(C + 1):
                if t < C:
                    lo, w = CHUNKS[t]
                    act.wait_ge(s_c1, t + 1)
                    nc.scalar.activation(emb[:, lo:lo + w], banks[4 + t % 4][:, 0:w], ACT.Identity,
                                         bias=shift[:, 0:1]).then_inc(s_emb, 1)
                if t > 0:
                    project_scalar(act, 1, t - 1, stage1, 3 * DM)

        def c_vector(dve, l):
            n = l + 1
            times, total = logits(dve, n, DM, H1)

            def clip(i, s, g):
                dve.wait_ge(s_red, g + (n * NG + 1))
                since(dve, s_wt, g + (l * NG - 1))
                nc.vector.tensor_scalar(red[:, s % 2, 0:TG * H1], red[:, s % 2, 0:TG * H1], -10.0, 10.0,
                                        ALU.max, ALU.min).then_inc(s_lg, 1)

            def weigh(i, s, g):
                dve.wait_ge(s_vc, g + (n * NG + 1))
                since(dve, s_sum, g + (n * NG - 1))
                nc.vector.scalar_tensor_tensor(
                    wts[:, s % 2, :].rearrange("p (j h) -> p j h", j=TG),
                    seg[1][:, ds(g * TG, TG)].unsqueeze(2).to_broadcast([P, TG, H1]), 0.0,
                    red[:, s % 2, 0:TG * H1].rearrange("p (j h) -> p j h", j=TG),
                    ALU.is_ge, ALU.mult).then_inc(s_wt, 1)
                dve.wait_ge(s_wt, g + (l * NG + 1))
                nc.vector.tensor_tensor(
                    vw[:, s % 2, :, :].rearrange("p j (h d) -> p j h d", h=H1),
                    kv[:, s, :, DM:2 * DM].rearrange("p j (h d) -> p j h d", h=H1),
                    wts[:, s % 2, :].rearrange("p (j h) -> p j h", j=TG).unsqueeze(3)
                    .to_broadcast([P, TG, H1, DM // H1]),
                    ALU.mult).then_inc(s_vw, 1)

            load, sums = add_sums(dve, n, 1, lambda base, j: (acc1, odd1)[j % 2][:, :, ds(base, P)],
                            lambda s, j: banks[4 + 2 * (s % 2) + j // 2][:, (j % 2) * 2 * P:(j % 2 + 1) * 2 * P]
                            .rearrange("p (a m) -> p a m", a=2), 2)
            dve.wait_ge(s_m1, 2 + l * C)
            fours(dve, [(2, weigh), (1, times), (3, load(0, 1)), (1, total), (3, load(2, 3)), (1, clip), (3, sums)])

        def c_scalar(act, l):
            n = l + 1

            def exp(i, s, g):
                act.wait_ge(s_lg, g + (n * NG + 1))
                nc.scalar.activation(red[:, s % 2, 0:TG * H1], red[:, s % 2, 0:TG * H1],
                                     ACT.Exp).then_inc(s_vc, 1)

            def beside(i, s, g):
                act.wait_ge(s_wt, g + (l * NG + 1))
                since(act, s_sum, g + (n * NG - 1))
                nc.scalar.copy(wx[:, s % 2, :, :].rearrange("p j (h d) -> p (j h) d", h=H1),
                               wts[:, s % 2, :].unsqueeze(2).to_broadcast([P, TG * H1, DM // H1])
                               ).then_inc(s_wb, 1)

            def ring(i, s, g):
                since(act, s_sum, g + (n * NG - SLOTS + 1))

            act.wait_ge(s_seg, 2)
            wait_tables(act, n)
            distance, at_zero = one_hot_scalar(act, n + 1, 1, ring)
            fours(act, [(2, beside), (0, copy_transposed(act, n)), (-1, distance), (-3, stage_indices(act, n, 1)), (1, exp), (-1, at_zero)])

        def c_tensor(pe, l):
            n = l + 1

            def sums(i, s, g):
                pe.wait_ge(s_vw, g + (n * NG + 1))
                pe.wait_ge(s_wb, g + (n * NG + 1))
                since(pe, s_acc, g * TG + (n * T - TG))
                for j in range(TG):
                    to = banks[4 + 2 * (s % 2) + j // 2]
                    at = (j % 2) * 2 * P
                    nc.tensor.matmul(to[:, at:at + P], vw[:, s % 2, j, :], R[:, s, j, :], start=True,
                                     stop=True)
                    done = nc.tensor.matmul(
                        to[:, at + P:at + 2 * P], wx[:, s % 2, j, :], R[:, s, j, :], start=True, stop=True)
                done.then_inc(s_sum, 1)

            fours(pe, [(1, expand(pe, n, DM)), (0, transposes(pe, n, n + 1)), (2, sums)])

        def post_vector(dve, l):
            def residual(c, lo, w):
                both, odd = acc1[:, :, lo:lo + w], odd1[:, :, lo:lo + w]
                num, den = acc1[:, 0, lo:lo + w], acc1[:, 1, lo:lo + w]
                vstep(nc.vector.tensor_tensor(both, both, odd, ALU.add))
                vstep(nc.vector.tensor_scalar(den, den, 1e-8, None, ALU.add))
                vstep(nc.vector.reciprocal(den, den))
                vstep(nc.vector.tensor_tensor(num, num, den, ALU.mult))
                nc.vector.tensor_tensor(num, num, emb[:, lo:lo + w], ALU.add).then_inc(s_c1x, 1)

            def deviations(c, lo, w):
                dve.wait_ge(s_mean, l * C + c + 1)
                vstep(nc.vector.tensor_tensor(cent[:, lo:lo + w], acc1[:, 0, lo:lo + w],
                                              banks[4 + c % 2][:, 0:w], ALU.subtract))
                nc.vector.tensor_tensor(work1[:, lo:lo + w], cent[:, lo:lo + w], cent[:, lo:lo + w],
                                        ALU.mult).then_inc(s_sq, 1)

            def norm(c, lo, w):
                dve.wait_ge(s_root, l * C + c + 1)
                vstep(nc.vector.reciprocal(work1[:, lo:lo + w], work1[:, lo:lo + w]))
                nc.vector.tensor_tensor(cent[:, lo:lo + w], cent[:, lo:lo + w], work1[:, lo:lo + w],
                                        ALU.mult).then_inc(s_nm, 1)

            def output(c, lo, w):
                if l < LAYERS - 1:
                    return
                own = chunk_blocks(c, NB)
                at = xs[:, own[0]:own[-1] + 1, :]
                dve.wait_ge(s_o, 4 + c + 1)
                nc.vector.tensor_tensor(at, at, banks[c % 4][:, 0:len(own) * D0].rearrange(
                    "p (b c) -> p b c", c=D0), ALU.add).then_inc(s_fin, 1)

            dve.wait_ge(s_acc, T * (l + 2))
            for t in range(C + 3):
                for lag, fn in enumerate((residual, deviations, norm, output)):
                    if 0 <= t - lag < C:
                        fn(t - lag, *CHUNKS[t - lag])

        def post_tensor(pe, l):
            for t in range(C + 2):
                if t < C:
                    lo, w = CHUNKS[t]
                    pe.wait_ge(s_c1x, l * C + t + 1)
                    since(pe, s_sq, l * C + t - 1)
                    nc.tensor.matmul(banks[4 + t % 2][:, 0:w], avg[:, :], acc1[:, 0, lo:lo + w],
                                     start=True, stop=True).then_inc(s_mean, 1)
                if 0 <= t - 1 < C:
                    lo, w = CHUNKS[t - 1]
                    pe.wait_ge(s_sq, l * C + t)
                    since(pe, s_root, l * C + t - 2)
                    nc.tensor.matmul(banks[6 + (t - 1) % 2][:, 0:w], avg[:, :], work1[:, lo:lo + w],
                                     start=True, stop=True).then_inc(s_varp, 1)
                if t >= 2:
                    features(pe, t - 2, l + 1)

        def post_scalar(act, l):
            for t in range(1, C + 2):
                if t - 1 < C:
                    lo, w = CHUNKS[t - 1]
                    act.wait_ge(s_varp, l * C + t)
                    nc.scalar.activation(work1[:, lo:lo + w], banks[6 + (t - 1) % 2][:, 0:w], ACT.Sqrt,
                                         bias=eps[:, 0:1]).then_inc(s_root, 1)
                if t >= 2:
                    lo, w = CHUNKS[t - 2]
                    act.wait_ge(s_nm, l * C + t - 1)
                    nc.scalar.activation(emb[:, lo:lo + w], cent[:, lo:lo + w], ACT.Identity,
                                         bias=lnb[:, l:l + 1], scale=lns[:, l:l + 1]).then_inc(s_emb, 1)
                    if l < LAYERS - 1:
                        project_scalar(act, l + 2, t - 2, stage1, 3 * DM)

        def clear_gpsimd(gp, l):
            if l == 0:
                gp.wait_ge(s_both, 1)
                nc.gpsimd.memset(acc1[:, :, :], 0.0).then_inc(s_m1, 1)
                nc.gpsimd.memset(odd1[:, :, :], 0.0).then_inc(s_m1, 1)
                return
            for c, (lo, w) in enumerate(CHUNKS):
                gp.wait_ge(s_mean, (l - 1) * C + c + 1)
                gp.wait_ge(s_sq, (l - 1) * C + c + 1)
                nc.gpsimd.memset(odd1[:, :, lo:lo + w], 0.0)
                nc.gpsimd.memset(acc1[:, :, lo:lo + w], 0.0).then_inc(s_m1, 1)

        block = ctx.enter_context(nc.Block())

        @block.sync
        def _(sp):
            loads_sync(sp)
            load_x(sp)
            load_weights(sp)
            sort_sync(sp)
            tables_sync(sp, 0, stage0, D0, q0_d, kv0_d)
            windows_sync(sp, 0, 0, q0_d, D0)
            max_sync(sp)
            out0_sync(sp)
            sorted_sync(sp, 1)
            for l in range(LAYERS):
                tables_sync(sp, l + 1, stage1, DM, q1_d[l], kv1_d[l])
                windows_sync(sp, l + 1, 1, q1_d[l], DM)
            for c in range(C):
                sp.wait_ge(s_fin, c + 1)
                own = chunk_blocks(c, NB)
                lo, hi = own[0] * P, min((own[-1] + 1) * P, N)
                if hi % P:
                    sp.dma_start(out[lo:hi], xs[0:hi - lo, own[0], :]).then_inc(s_out, 16)
                else:
                    sp.dma_start(out[lo:hi].rearrange("(b p) c -> p b c", p=P),
                                 xs[:, own[0]:own[-1] + 1, :]).then_inc(s_out, 16)
            sp.wait_ge(s_out, 16 * C)

        @block.gpsimd
        def _(gp):
            constants_gpsimd(gp)
            zeros_gpsimd(gp)
            sort_gpsimd(gp)
            gather_gpsimd(gp, 0, kv0_d, D0)
            second_gpsimd(gp)
            for l in range(LAYERS):
                clear_gpsimd(gp, l)
                gather_gpsimd(gp, l + 1, kv1_d[l], DM)

        @block.vector
        def _(dve):
            constants_vector(dve)
            sort_vector(dve)
            dve.wait_ge(s_seg, 1)
            dve.wait_ge(s_x, 32)
            norm_vector(dve, 0)
            a_vector(dve)
            max_vector(dve)
            b_vector(dve)
            out0_vector(dve)
            norm_vector(dve, 1)
            dve.wait_ge(s_w, wcount[0])
            vstep(nc.vector.tensor_tensor(shift[:, 0:1], shift[:, 0:1], shift[:, 1:2], ALU.add))
            nc.vector.tensor_tensor(xs[:, :, :], xs[:, :, :], invb[:, :].unsqueeze(1).to_broadcast([P, NB, D0]),
                                    ALU.add).then_inc(s_xb, 1)
            windows_vector(dve, 1)
            dve.wait_ge(s_seg, 2)
            for l in range(LAYERS):
                c_vector(dve, l)
                post_vector(dve, l)
        @block.scalar
        def _(act):
            sort_scalar(act)
            norm_scalar(act, 0)
            act.wait_ge(s_fill, 32)
            for c in range(C):
                project_scalar(act, 0, c, stage0, 3 * D0)
            act.wait_ge(s_seg, 1)
            wait_tables(act, 0)
            fours(act, [(-3, stage_indices(act, 0, 0)), (0, copy_transposed(act, 0)), (1, keep_values(act))])
            max_scalar(act)
            b_scalar(act)
            norm_scalar(act, 1)
            act.wait_ge(s_xb, 1)
            embed_scalar(act)
            for l in range(LAYERS):
                c_scalar(act, l)
                post_scalar(act, l)

        @block.tensor
        def _(pe):
            sort_tensor(pe)
            norm_tensor(pe, 0)
            pe.wait_ge(s_w, wcount[0])
            pe.wait_ge(s_zero, 2)
            for c in range(C):
                project_tensor(pe, 0, c, hT, W0[:, :], 3 * D0)
            pe.wait_ge(s_pjs, NT)
            fours(pe, [(0, transposes(pe, 0, 0)), (0, expand(pe, 0, D0))])
            max_tensor(pe)
            b_tensor(pe)
            pe.wait_ge(s_agg, 1)
            out_tensor(pe, hT, Wo[:, :])
            norm_tensor(pe, 1)
            embed_tensor(pe)
            for l in range(LAYERS):
                pe.wait_ge(s_pjs, (l + 2) * NT)
                c_tensor(pe, l)
                post_tensor(pe, l)


_INS = ['x', 'src', 'dst', 'edge_attr_8', 'L0_gnn_Wq', 'L0_gnn_bq', 'L0_gnn_Wk', 'L0_gnn_bk', 'L0_gnn_Wv',
        'L0_gnn_bv', 'L0_gnn_Wo', 'L0_gnn_bo', 'L1_gnn_W_P_w', 'L1_gnn_W_P_b', 'L1_gnn_W_pos',
        'L1_gnn_qT', 'L1_gnn_kT', 'L1_gnn_vT', 'L1_gnn_ln_scale', 'L1_gnn_ln_bias', 'L1_gnn_inv_w',
        'L1_gnn_inv_b']


def kernel(**inputs):
    import numpy as _np
    import concourse.bacc as _bacc
    from concourse import mybir as _mybir
    from concourse.bass_utils import run_bass_kernel_spmd as _run

    nc = _bacc.Bacc("TRN2", target_bir_lowering=False, num_devices=1)
    arrays, args = {}, []
    for name in _INS:
        a = _np.ascontiguousarray(inputs[name])
        arrays[f"in_{name}_dram"] = a
        args.append(nc.dram_tensor(f"in_{name}_dram", a.shape, _mybir.dt.from_np(a.dtype), kind="ExternalInput").ap())
    args.append(nc.dram_tensor("out_0_dram", (N, D0), _mybir.dt.from_np(_np.dtype("float32")),
                               kind="ExternalOutput").ap())
    build(nc, *args)
    r = _run(nc, [arrays], core_ids=[0])
    return r.results[0]["out_0_dram"]
```
